# Optimizing a Trainium2 kernel written in Bass

```python
import numpy as np
import jax
import jax.numpy as jnp

def _softmax(x, axis=-1):
    return jax.nn.softmax(x, axis=axis)

def _gelu(x):
    return jax.nn.gelu(x, approximate=True)

def _silu(x):
    return jax.nn.silu(x)

def _sigmoid(x):
    return jax.nn.sigmoid(x)

def _layernorm(x, axis=-1, eps=1e-05):
    m = jnp.mean(x, axis=axis, keepdims=True)
    v = jnp.var(x, axis=axis, keepdims=True)
    return (x - m) / jnp.sqrt(v + eps)

def _scatter_add(tgt, idx, src, axis=0):
    return tgt.at[idx].add(src)

def _segment_sum(src, seg, n):
    return jax.ops.segment_sum(src, seg, n)
kernel_name = 'mk_decoder_preln_d1_seqx_r4_b0660b'

def setup_inputs(seed: int=0):
    np.random.seed(seed)
    _w = jnp.asarray

    def _rec_inputs():
        import jax
        import jax.numpy as jnp
        _rk = jax.random.key(seed)
        x = 0.0003765 + 1 * jax.random.normal(jax.random.fold_in(_rk, 1), (2, 1024, 256), jnp.float32)
        _lenS = 1024 - jax.random.randint(jax.random.fold_in(_rk, 7), (2,), 0, max(1, 1024 // 4) + 1, jnp.int32)
        _lenS2 = 154 - jax.random.randint(jax.random.fold_in(_rk, 8), (2,), 0, max(1, 154 // 4) + 1, jnp.int32)
        _ctx_1024P = jax.random.normal(jax.random.fold_in(_rk, 11), (2, 16, 256), jnp.float32)
        _ctx_1024c = jax.random.dirichlet(jax.random.fold_in(_rk, 511), 0.3 * jnp.ones((16,), jnp.float32), (2, 154))
        _ctx_1024t = jnp.einsum('bsk,bkd->bsd', _ctx_1024c, _ctx_1024P)
        _ctx_1024t = _ctx_1024t * jax.lax.rsqrt(jnp.mean(jnp.square(_ctx_1024t)) + 1e-12) * 0.953939
        ctx_1024 = -0.000292821 + 1.00034 * (_ctx_1024t + 0.3 * jax.random.normal(jax.random.fold_in(_rk, 611), (2, 154, 256), jnp.float32))
        _validS = jnp.arange(1024)[None, :] < _lenS[:, None]
        _validS2 = jnp.arange(154)[None, :] < _lenS2[:, None]
        _causal = jnp.tril(jnp.ones((1024, 1024), dtype=bool))
        mask_Bx1xSxS2_ik1 = jnp.where(jnp.broadcast_to(_validS2[:, None, None, :], (2, 1, 1024, 154)), 1, 0).astype(jnp.int32)
        return (x, ctx_1024, mask_Bx1xSxS2_ik1)
    x, ctx_1024, mask_Bx1xSxS2_ik1 = _rec_inputs()

    def _L0_attn_setup():
        import jax, jax.numpy as jnp
        import numpy as np
        NUM_HEADS = 16
        EMB = 256
        DH = 64
        B, S = (4, 512)
        key = jax.random.key(seed)
        ks = jax.random.split(key, 9)
        sc = lambda fan_in: 1.0 / np.sqrt(fan_in)
        Wq = jax.random.uniform(ks[0], (NUM_HEADS, EMB, DH), minval=-sc(EMB), maxval=sc(EMB))
        Wk = jax.random.uniform(ks[1], (NUM_HEADS, EMB, DH), minval=-sc(EMB), maxval=sc(EMB))
        Wv = jax.random.uniform(ks[2], (NUM_HEADS, EMB, DH), minval=-sc(EMB), maxval=sc(EMB))
        bq = jax.random.uniform(ks[3], (NUM_HEADS, DH), minval=-sc(EMB), maxval=sc(EMB))
        bk = jax.random.uniform(ks[4], (NUM_HEADS, DH), minval=-sc(EMB), maxval=sc(EMB))
        bv = jax.random.uniform(ks[5], (NUM_HEADS, DH), minval=-sc(EMB), maxval=sc(EMB))
        Wo = jax.random.uniform(ks[6], (NUM_HEADS * DH, EMB), minval=-sc(NUM_HEADS * DH), maxval=sc(NUM_HEADS * DH))
        bo = jax.random.uniform(ks[7], (EMB,), minval=-sc(NUM_HEADS * DH), maxval=sc(NUM_HEADS * DH))
        x = jax.random.normal(ks[8], (B, S, EMB), dtype=jnp.float32)
        return {'x': x, 'Wq': Wq, 'Wk': Wk, 'Wv': Wv, 'bq': bq, 'bk': bk, 'bv': bv, 'Wo': Wo, 'bo': bo}
    _L0_attn_all = _L0_attn_setup()
    _L0_attn_in = {k: v for k, v in _L0_attn_all.items() if k in ('Wq', 'Wk', 'Wv', 'bq', 'bk', 'bv', 'Wo', 'bo')}
    del _L0_attn_all

    def _L0_xattn_setup():
        import jax, jax.numpy as jnp
        import numpy as np
        HEADS = 16
        key = jax.random.key(seed)
        k1, k2, k3, k4, k5, k6 = jax.random.split(key, 6)
        N, L, E = (2, 512, 256)
        return {'values': jax.random.normal(k1, (N, L, E), dtype=jnp.float32), 'key': jax.random.normal(k2, (N, L, E), dtype=jnp.float32), 'query': jax.random.normal(k3, (N, L, E), dtype=jnp.float32), 'mask': jax.random.randint(k4, (N, 1, L, L), 0, 2, dtype=jnp.int32), 'W_out': jax.random.normal(k5, (E, E), dtype=jnp.float32) / np.sqrt(E), 'b_out': jax.random.normal(k6, (E,), dtype=jnp.float32) * 0.01}
    _L0_xattn_all = _L0_xattn_setup()
    _L0_xattn_in = {k: v for k, v in _L0_xattn_all.items() if k in ('W_out', 'b_out')}
    del _L0_xattn_all

    def _L0_ffn_setup():
        import jax, jax.numpy as jnp
        import numpy as np
        D_MODEL = 256
        D_FF = 1024
        N_EXP = 8
        TOP_K = 2

        def _gelu(x):
            return jax.nn.gelu(x, approximate=False)
        key = jax.random.key(seed)
        ks = jax.random.split(key, 12)
        s = 0.02
        return {'x': jax.random.normal(ks[0], (4, 512, D_MODEL), dtype=jnp.float32), 'shared_w1': jax.random.normal(ks[1], (D_MODEL, D_FF), dtype=jnp.float32) * s, 'shared_b1': jnp.zeros((D_FF,), jnp.float32), 'shared_w2': jax.random.normal(ks[2], (D_FF, D_MODEL), dtype=jnp.float32) * s, 'shared_b2': jnp.zeros((D_MODEL,), jnp.float32), 'router_w': jax.random.normal(ks[3], (D_MODEL, N_EXP), dtype=jnp.float32) * s, 'router_b': jnp.zeros((N_EXP,), jnp.float32), 'exp_w1': jax.random.normal(ks[4], (N_EXP, D_MODEL, D_FF), dtype=jnp.float32) * s, 'exp_b1': jnp.zeros((N_EXP, D_FF), jnp.float32), 'exp_w2': jax.random.normal(ks[5], (N_EXP, D_FF, D_MODEL), dtype=jnp.float32) * s, 'exp_b2': jnp.zeros((N_EXP, D_MODEL), jnp.float32)}
    _L0_ffn_all = _L0_ffn_setup()
    _L0_ffn_in = {k: v for k, v in _L0_ffn_all.items() if k in ('shared_w1', 'shared_b1', 'shared_w2', 'shared_b2', 'router_w', 'router_b', 'exp_w1', 'exp_b1', 'exp_w2', 'exp_b2')}
    del _L0_ffn_all
    return {'x': x, 'ctx_1024': ctx_1024, 'mask_Bx1xSxS2_ik1': mask_Bx1xSxS2_ik1, 'L0_attn_Wq': _L0_attn_in['Wq'], 'L0_attn_Wk': _L0_attn_in['Wk'], 'L0_attn_Wv': _L0_attn_in['Wv'], 'L0_attn_bq': _L0_attn_in['bq'], 'L0_attn_bk': _L0_attn_in['bk'], 'L0_attn_bv': _L0_attn_in['bv'], 'L0_attn_Wo': _L0_attn_in['Wo'], 'L0_attn_bo': _L0_attn_in['bo'], 'L0_xattn_W_out': _L0_xattn_in['W_out'], 'L0_xattn_b_out': _L0_xattn_in['b_out'], 'L0_ffn_shared_w1': _L0_ffn_in['shared_w1'], 'L0_ffn_shared_b1': _L0_ffn_in['shared_b1'], 'L0_ffn_shared_w2': _L0_ffn_in['shared_w2'], 'L0_ffn_shared_b2': _L0_ffn_in['shared_b2'], 'L0_ffn_router_w': _L0_ffn_in['router_w'], 'L0_ffn_router_b': _L0_ffn_in['router_b'], 'L0_ffn_exp_w1': _L0_ffn_in['exp_w1'], 'L0_ffn_exp_b1': _L0_ffn_in['exp_b1'], 'L0_ffn_exp_w2': _L0_ffn_in['exp_w2'], 'L0_ffn_exp_b2': _L0_ffn_in['exp_b2']}

def reference(x, ctx_1024, mask_Bx1xSxS2_ik1, L0_attn_Wq, L0_attn_Wk, L0_attn_Wv, L0_attn_bq, L0_attn_bk, L0_attn_bv, L0_attn_Wo, L0_attn_bo, L0_xattn_W_out, L0_xattn_b_out, L0_ffn_shared_w1, L0_ffn_shared_b1, L0_ffn_shared_w2, L0_ffn_shared_b2, L0_ffn_router_w, L0_ffn_router_b, L0_ffn_exp_w1, L0_ffn_exp_b1, L0_ffn_exp_w2, L0_ffn_exp_b2):
    import jax
    import jax.numpy as jnp

    def _L0_attn_ref(x, Wq, Wk, Wv, bq, bk, bv, Wo, bo):
        import jax, jax.numpy as jnp
        import numpy as np
        NUM_HEADS = 16
        EMB = 256
        DH = 64
        B, S = (4, 512)
        seq_len = x.shape[1]
        q = jnp.einsum('bse,hed->bhsd', x, Wq) + bq[None, :, None, :]
        k = jnp.einsum('bse,hed->bhsd', x, Wk) + bk[None, :, None, :]
        v = jnp.einsum('bse,hed->bhsd', x, Wv) + bv[None, :, None, :]
        scores = jnp.einsum('bhsd,bhtd->bhst', q, k) / jnp.sqrt(jnp.float32(DH))
        causal = jnp.tril(jnp.ones((seq_len, seq_len), dtype=bool))
        scores = jnp.where(causal[None, None, :, :], scores, -jnp.inf)
        attn = jax.nn.softmax(scores, axis=-1)
        out = jnp.einsum('bhst,bhtd->bhsd', attn, v)
        out = out.transpose(0, 2, 1, 3).reshape(x.shape[0], seq_len, NUM_HEADS * DH)
        return out @ Wo + bo

    def _L0_xattn_ref(values, key, query, mask, W_out, b_out):
        import jax, jax.numpy as jnp
        import numpy as np
        HEADS = 16
        N, Lq, E = query.shape
        Lk = key.shape[1]
        H = HEADS
        D = E // H
        q = query.reshape(N, Lq, H, D)
        k = key.reshape(N, Lk, H, D)
        v = values.reshape(N, Lk, H, D)
        energy = jnp.einsum('nqhd,nkhd->nhqk', q, k)
        energy = jnp.where(mask == 0, jnp.float32(-1e+20), energy)
        attn = jax.nn.softmax(energy / np.float32(np.sqrt(D)), axis=3)
        out = jnp.einsum('nhqk,nkhd->nqhd', attn, v).reshape(N, Lq, H * D)
        return out @ W_out.T + b_out

    def _L0_ffn_ref(x, shared_w1, shared_b1, shared_w2, shared_b2, router_w, router_b, exp_w1, exp_b1, exp_w2, exp_b2):
        import jax, jax.numpy as jnp
        import numpy as np
        D_MODEL = 256
        D_FF = 1024
        N_EXP = 8
        TOP_K = 2

        def _gelu(x):
            return jax.nn.gelu(x, approximate=False)
        leading = x.shape[:-1]
        d = x.shape[-1]
        xf = x.reshape(-1, d)
        T = xf.shape[0]
        h_shared = _gelu(xf @ shared_w1 + shared_b1) @ shared_w2 + shared_b2
        logits = xf @ router_w + router_b
        routing = jax.nn.softmax(logits, axis=-1)
        sel_w, sel_idx = jax.lax.top_k(routing, TOP_K)
        sel_w = sel_w / (jnp.sum(sel_w, axis=-1, keepdims=True) + 1e-09)
        combine = jnp.zeros((T, N_EXP), routing.dtype)
        combine = combine.at[jnp.arange(T)[:, None], sel_idx].add(sel_w)
        residual = jnp.zeros_like(xf)
        for e in range(N_EXP):
            h = _gelu(xf @ exp_w1[e] + exp_b1[e])
            y = h @ exp_w2[e] + exp_b2[e]
            residual = residual + combine[:, e:e + 1] * y
        out = h_shared + residual
        return out.reshape(*leading, d)
    x = x + _L0_attn_ref(_layernorm(x, axis=-1), L0_attn_Wq, L0_attn_Wk, L0_attn_Wv, L0_attn_bq, L0_attn_bk, L0_attn_bv, L0_attn_Wo, L0_attn_bo)
    x = x + _L0_xattn_ref(ctx_1024, ctx_1024, _layernorm(x, axis=-1), mask_Bx1xSxS2_ik1, L0_xattn_W_out, L0_xattn_b_out)
    x = x + _L0_ffn_ref(_layernorm(x, axis=-1), L0_ffn_shared_w1, L0_ffn_shared_b1, L0_ffn_shared_w2, L0_ffn_shared_b2, L0_ffn_router_w, L0_ffn_router_b, L0_ffn_exp_w1, L0_ffn_exp_b1, L0_ffn_exp_w2, L0_ffn_exp_b2)
    return x

_drawn_inputs = setup_inputs


def setup_inputs(seed=0):
    import zlib

    import numpy as np

    out = dict(_drawn_inputs(seed))
    spreads = {'L0_ffn_shared_b1': (0.0, 0.302),
     'L0_ffn_shared_b2': (0.0, 0.1),
     'L0_ffn_router_b': (0.0, 0.1),
     'L0_ffn_exp_b1': (0.0, 0.382),
     'L0_ffn_exp_b2': (0.0, 0.1)}
    factors = {'L0_attn_Wq': 4.607,
     'L0_attn_Wk': 4.768,
     'L0_attn_bq': 8.0,
     'L0_attn_bk': 8.0,
     'L0_attn_bo': 2.95,
     'L0_xattn_b_out': 5.447}
    for name, (base, spread) in spreads.items():
        noise = np.random.default_rng([zlib.crc32(name.encode()), seed]).standard_normal(out[name].shape)
        drawn = base * np.exp(spread * noise) if base else spread * noise
        out[name] = jnp.asarray(drawn.astype(out[name].dtype))
    for name, factor in factors.items():
        out[name] = (out[name] * factor).astype(out[name].dtype)
    return out
```

```python
from contextlib import ExitStack

import numpy as np
import concourse.bass as bass
from concourse import mybir

F32 = mybir.dt.float32
BF16 = mybir.dt.bfloat16
I32 = mybir.dt.int32
U32 = mybir.dt.uint32
ALU = mybir.AluOpType
ACT = mybir.ActivationFunctionType
AX = mybir.AxisListType
ds = bass.ds

P = 128
EPS = 1e-5
MASKED = -1e30
FREE = 1
CROSS_MASKED = -1e20


class Chain:

    def __init__(self, eng, sem):
        self.eng, self.sem, self.base, self.k, self.turn, self.per = eng, sem, 0, 0, 0, 0

    def loop(self, turn, per):
        self.base += self.k
        self.turn, self.per, self.k = turn, per, 0

    def end(self, turns):
        assert self.k == self.per, (self.k, self.per)
        self.base += turns * self.per
        self.turn, self.per, self.k = 0, 0, 0

    def __call__(self, ins):
        self.k += 1
        ins.then_inc(self.sem, 1)
        self.eng.wait_ge(self.sem, self.turn * self.per + (self.base + self.k))


def decoder_layer(nc, x, ctx, mask, wq, wk, wv, bq, bk, bv, wo, bo, w_out, b_out,
                  sw1, sb1, sw2, sb2, rw, rb, ew1, eb1, ew2, eb2, out):
    NB, S, D = x.shape
    H, _, DH = wq.shape
    K2 = ctx.shape[1]
    F = sw1.shape[1]
    NE = rw.shape[1]
    T = NB * S
    NT = T // P
    TB = S // P
    C = D // P
    NP = H // 2
    HD = H * DH
    J = HD // P
    FJ = F // P
    CD = D // H
    HC = P // CD
    KR = K2 - P
    RS = 32
    V1 = CD + 1
    BLK = 256
    TT = BLK // P
    NSH = T // BLK
    MAX_BLOCKS = 2 * T // BLK + NE
    assert DH * 2 == P and TB == 8 and C == 2 and 0 < KR <= RS and MAX_BLOCKS % 2 == 0 and HC == 8

    with ExitStack() as stack:
        def sb(name, shape, dt=F32):
            return stack.enter_context(nc.sbuf_tensor(name, shape, dt))

        def sem(name):
            return stack.enter_context(nc.semaphore(name))

        x_sb = sb("x_sb", [P, NT, D])
        xT = sb("xT", [P, C, T])
        o_all = sb("o_all", [P, NT, HD])
        wo_sb = sb("wo_sb", [P, J, D])
        ctx_diag = sb("ctx_diag", [P, NB, C, HC, K2])
        v_main = sb("v_main", [P, NB, H, V1])
        v_rest = sb("v_rest", [P, NB, H, V1])
        w_outT = sb("w_outT", [P, C, D])
        rw_sb = sb("rw_sb", [P, C, NE])
        ident = sb("ident", [P, P])
        identb = sb("identb", [P, P], BF16)
        causal = sb("causal", [P, P], BF16)
        bias_qkv = sb("bias_qkv", [P, 3, NP])
        bo_b = sb("bo_b", [P, D])
        bout_b = sb("bout_b", [P, D])
        sb2_b = sb("sb2_b", [P, D])
        rb_b = sb("rb_b", [P, NE])
        b1T = sb("b1T", [P, (NE + 1) * FJ])
        mean_var = sb("mean_var", [P, NT, 2])
        stats = sb("stats", [P, NT, 6])
        rstd = sb("rstd", [P, NT])
        power = sb("power", [P, NT])
        logits = sb("logits", [P, NT, NE])
        weight = sb("weight", [P, 2, NT])
        dest = sb("dest", [P, 2, NT], U32)
        block_expert = sb("block_expert", [P, MAX_BLOCKS], I32)
        zero_rows = sb("zero_rows", [P, D])
        head_of = sb("head_of", [P, HC])
        arena = sb("arena", [P, 14592])

        place = [0]

        def region(*shape, dt=F32):
            words = int(np.prod(shape))
            a = arena[:, place[0]:place[0] + words]
            place[0] += words
            assert place[0] <= arena.shape[1], place[0]
            if dt is not F32:
                a = a.bitcast(dt)
            names = "abcd"[:len(shape)]
            if len(shape) > 1:
                a = a.rearrange(f"p ({' '.join(names)}) -> p {' '.join(names)}",
                                **{n: s for n, s in zip(names, shape)})
            return a

        xn = [region(D) for _ in range(2)]
        w_pair = region(3, C, P)
        q_pad = [region(S) for _ in range(2)]
        kT = region(S)
        vT = region(S)
        v_pair = region(TB, P)
        prob = [region(S) for _ in range(2)]
        probT = [region(TB, P) for _ in range(2)]
        neg_max = region(2)
        row_sum = region(2 * TB)
        row_inv = region(2 * TB)
        ctx_in = region(NB, 2, D)
        bias_in = region(P)
        b1_in = region(P)
        wout_in = region(C, D)
        place[0] = 0
        UH = 4
        NQ = H // UH
        o_tile = [region(HD) for _ in range(2)]
        oT = [region(J, P) for _ in range(2)]
        xn2 = [region(D) for _ in range(2)]
        xn2T = [region(C, P) for _ in range(2)]
        mask_in = [region(K2, dt=I32) for _ in range(2)]
        mask_add = [region(K2 // 2, dt=BF16) for _ in range(2)]
        energy = [region(UH, K2) for _ in range(2)]
        pm = [region(UH, P) for _ in range(2)]
        pr = [region(UH, RS) for _ in range(2)]
        pmT = [region(UH, P) for _ in range(2)]
        prT = [region(P) for _ in range(2)]
        cmax = [region(UH) for _ in range(2)]
        cinv = [region(H) for _ in range(2)]
        o2 = [region(D) for _ in range(2)]
        o2T = [region(C, P) for _ in range(2)]
        ln_sum = [region(1) for _ in range(2)]
        ln_sq = [region(D) for _ in range(2)]
        ln_var = [region(1) for _ in range(2)]
        ln_r = [region(1) for _ in range(2)]
        REST = 320
        place[0] = 0
        w1 = [region(C, F) for _ in range(2)]
        w2 = [region(FJ, D) for _ in range(2)]
        hT = region(FJ, BLK)
        xb = [region(TT, D) for _ in range(2)]
        xbT = [region(C, BLK) for _ in range(2)]
        b1 = [region(FJ) for _ in range(2)]
        b2 = [region(D) for _ in range(2)]
        yb = [region(TT, D) for _ in range(2)]
        y_got = [w[0].rearrange("p a b -> p (a b)").rearrange("p (n d) -> p n d", d=D) for w in (w1, w2)]

        route = sb("route", [P, 12, NT, NE])
        hot1, hot2, eq, cand, masked, shifted, expd, both, pos, picked, jm8, pos2 = [
            route[:, i] for i in range(12)]
        tile_base = sb("tile_base", [P, NT + 1, NE])
        small = sb("small", [P, 11, NT])
        first_max, first_at, second_max, second_at, gap, gap_exp, total, inv_total, w_sum, w_inv, destf = [
            small[:, i, :] for i in range(11)]
        ne_small = sb("ne_small", [P, 3, NE])
        n_blocks, blocks_incl, expert_base = [ne_small[:, i, :] for i in range(3)]
        block_starts = sb("block_starts", [P, NE, T // BLK])
        block_cmp = sb("block_cmp", [P, NE, T // BLK])
        block_no = sb("block_no", [P, MAX_BLOCKS, NE])
        block_ge = sb("block_ge", [P, MAX_BLOCKS, NE])
        block_f = sb("block_f", [P, MAX_BLOCKS])
        lower = sb("lower", [P, P])
        ones = sb("ones", [P, P])

        xs = nc.dram_tensor("x_sorted", [MAX_BLOCKS * BLK, D], F32, kind="Internal").ap()
        ys = nc.dram_tensor("y_sorted", [MAX_BLOCKS * BLK, D], F32, kind="Internal").ap()

        sc = stack.enter_context(nc.psum_tensor("sc", [P, 4 * 512], F32))
        tp = [stack.enter_context(nc.psum_tensor(f"tp{i}", [P, 512], F32)) for i in range(2)]
        acc = [stack.enter_context(nc.psum_tensor(f"acc{i}", [P, 512], F32)) for i in range(2)]

        def pair(name):
            return [sem(name + "_even"), sem(name + "_odd")]

        pool_step, vector_step = sem("pool_step"), sem("vector_step")
        x_in, small_in, w_in, rows_in, rest_in, zeros_ready, xs_zero = [sem(n) for n in (
            "x_in", "small_in", "w_in", "rows_in", "rest_in", "zeros_ready", "xs_zero")]
        consts_ready, prep_turned, prep_copied = sem("consts_ready"), sem("prep_turned"), sem("prep_copied")
        stats_done, rstd_done = sem("stats_done"), sem("rstd_done")
        xn_ready, xn_turned, xT_ready = pair("xn_ready"), pair("xn_turned"), pair("xT_ready")
        w_pair_in, proj_done, q_taken, k_taken, v_taken = [sem(n) for n in (
            "w_pair_in", "proj_done", "q_taken", "k_taken", "v_taken")]
        turned, turned_taken = pair("turned"), pair("turned_taken")
        scores_done, max_done, exp_done, pv_done, o_taken = [sem(n) for n in (
            "scores_done", "max_done", "exp_done", "pv_done", "o_taken")]
        o_staged, mask_staged, mask_ready = pair("o_staged"), pair("mask_staged"), pair("mask_ready")
        o_turned, o_turned_dve, o_turned_act, y_done = [pair(n) for n in (
            "o_turned", "o_turned_dve", "o_turned_act", "y_done")]
        var_done, rstd2_done = pair("var_done"), pair("rstd2_done")
        xn2_ready, xn2_turned, xn2_taken = [pair(n) for n in ("xn2_ready", "xn2_turned", "xn2_taken")]
        energy_done, shifted_done, cexp_done, p_turned, pm_taken, pr_taken, cpv_done = [pair(n) for n in (
            "energy_done", "shifted_done", "cexp_done", "p_turned", "pm_taken", "pr_taken", "cpv_done")]
        o2_ready, o2_turned, o2_taken, y2_done, x3_stored, logits_done, logits_taken = [pair(n) for n in (
            "o2_ready", "o2_turned", "o2_taken", "y2_done", "x3_stored", "logits_done", "logits_taken")]
        gap_ready, route_exp_done, both_ready, counted, experts_ready, dest_ready, scattered = [sem(n) for n in (
            "gap_ready", "route_exp_done", "both_ready", "counted", "experts_ready", "dest_ready", "scattered")]
        sw_in, blk_in, xb_turned, xb_taken = sem("sw_in"), pair("blk_in"), sem("xb_turned"), sem("xb_taken")
        h_done, gelu_done, ffn_done, ffn_taken = [sem(n) for n in ("h_done", "gelu_done", "ffn_done", "ffn_taken")]
        yb_taken, y_stored, gathered, final_done, out_stored = (
            pair("yb_taken"), pair("y_stored"), pair("gathered"), sem("final_done"), sem("out_stored"))

        xf = x.rearrange("b (t p) d -> p (b t) d", p=P)
        of = out.rearrange("b (t p) d -> p (b t) d", p=P)
        STEPS = 2 * TB
        TURNS = NB * NP
        chunks = [[(s % 2, 0, s // 2 + 1)] if s // 2 < 4 else [(0, 0, 4), (1, 4, s // 2 - 3)] for s in range(STEPS)]
        fills = [[1 + sum(cb == k for r in range(s + 1) for cb, _, _ in chunks[r]) for k in range(2)]
                 for s in range(STEPS)]
        FILLS = fills[-1][0]
        assert fills[-1] == [FILLS, FILLS]
        block = stack.enter_context(nc.Block())

        @block.sync
        def _(sp):
            sp.dma_start(x_sb[:, 0:NT // 2, :], xf[:, 0:NT // 2, :]).then_inc(x_in, 16)
            sp.dma_start(x_sb[:, NT // 2:NT, :], xf[:, NT // 2:NT, :]).then_inc(x_in, 16)
            for b in range(NB):
                sp.dma_start(ctx_in[:, b, 0, :], ctx[b, 0:P, :]).then_inc(small_in, 16)
                sp.dma_start(ctx_in[0:KR, b, 1, :], ctx[b, P:K2, :]).then_inc(small_in, 16)
            for k, w in enumerate((bq, bk, bv)):
                sp.dma_start(bias_in[k * NP:(k + 1) * NP, :], w.rearrange("(p h) d -> p (h d)", h=2)).then_inc(small_in, 16)
            sp.dma_start(b1_in[0:NE * FJ, :], eb1.rearrange("e (j p) -> (e j) p", p=P)).then_inc(small_in, 16)
            sp.dma_start(b1_in[NE * FJ:(NE + 1) * FJ, :], sb1.rearrange("(j p) -> j p", p=P)).then_inc(small_in, 16)
            sp.dma_start(wout_in, w_out.rearrange("(c p) d -> p c d", p=P)).then_inc(small_in, 16)
            with sp.Fori(0, NB) as b:
                with sp.Fori(0, NP) as p:
                    sp.wait_ge(proj_done, (b * NP + p) * 3 + FREE)
                    for k, w in enumerate((wq, wk, wv)):
                        for c in range(C):
                            sp.dma_start(w_pair[:, k, c, :].rearrange("e (h d) -> e h d", h=2),
                                         w[ds(2 * p, 2), c * P:(c + 1) * P, :].rearrange("h e d -> e h d")
                                         ).then_inc(w_pair_in, 16)
            sp.wait_ge(o_taken, TURNS * STEPS + FREE)
            with sp.Fori(0, NB) as b:
                with sp.Fori(0, TB // 2) as j:
                    jj = b * (TB // 2) + j
                    for u in range(2):
                        sp.wait_ge(o_turned[u], jj + FREE)
                        sp.dma_start(o_tile[u], o_all[:, ds(jj * 2 + u, 1), :].rearrange("p a n -> p (a n)")
                                     ).then_inc(o_staged[u], 16)
                        sp.wait_ge(mask_ready[u], jj + FREE)
                        sp.dma_start(mask_in[u], mask[ds(b, 1), 0, ds((j * 2 + u) * P, P), :]
                                     .rearrange("a p k -> (a p) k")).then_inc(mask_staged[u], 16)
            for u in range(2):
                sp.wait_ge(logits_taken[u], NT // 2 + FREE)
                sp.wait_ge(x3_stored[u], NT // 2 + FREE)
            sp.dma_start(w1[1], sw1.rearrange("(c p) f -> p c f", p=P)).then_inc(sw_in, 16)
            sp.dma_start(w2[1], sw2.rearrange("(c p) f -> p c f", p=P)).then_inc(sw_in, 16)
            sp.wait_ge(experts_ready, 1)
            with sp.Fori(0, MAX_BLOCKS // 2) as j:
                for u in range(2):
                    n = j * 2 + u
                    if u == 1:
                        sp.wait_ge(ffn_taken, NSH + FREE)
                    sp.wait_ge(yb_taken[u], j + FREE)
                    e = sp.value_load(block_expert[0:1, ds(n, 1)], min_val=0, max_val=NE - 1)
                    sp.dma_start(w1[u], ew1[ds(e, 1)].rearrange("a (c p) f -> p (a c) f", p=P)).then_inc(blk_in[u], 16)
                    sp.dma_start(w2[u], ew2[ds(e, 1)].rearrange("a (c p) f -> p (a c) f", p=P)).then_inc(blk_in[u], 16)
                    sp.dma_start(b1[u], b1T[:, ds(e * FJ, FJ)]).then_inc(blk_in[u], 16)
                    sp.dma_start(b2[u], eb2[ds(e, 1), :].rearrange("a d -> (a d)").partition_broadcast(P)
                                 ).then_inc(blk_in[u], 16)
                    sp.wait_ge(scattered, 16 * 2 * NT)
                    sp.dma_start(xb[u], xs[ds(n * BLK, BLK), :].rearrange("(t p) d -> p t d", p=P)
                                 ).then_inc(blk_in[u], 16)
            with sp.Fori(0, NT) as t:
                sp.wait_ge(final_done, t + 1)
                sp.dma_start(of[:, ds(t, 1), :], x_sb[:, ds(t, 1), :]).then_inc(out_stored, 16)
            sp.wait_ge(out_stored, 16 * NT)

        @block.gpsimd
        def _(pool):
            step = Chain(pool, pool_step)
            for signal in x3_stored:
                pool.sem_inc(signal, FREE)
            step(pool.memset(ident[:], 0.0))
            step(pool.affine_select(out=ident[:], in_=ident[:], compare_op=ALU.not_equal, fill=1.0, base=0,
                                    pattern=[[-1, P]], channel_multiplier=1))
            step(pool.tensor_copy(identb[:], ident[:]))
            step(pool.memset(causal[:], 0.0))
            step(pool.affine_select(out=causal[:], in_=causal[:], compare_op=ALU.is_ge, fill=MASKED, base=0,
                                    pattern=[[-1, P]], channel_multiplier=1))
            step(pool.memset(ones[:], 1.0))
            step(pool.affine_select(out=lower[:], in_=ones[:], compare_op=ALU.is_gt, fill=0.0, base=0,
                                    pattern=[[1, P]], channel_multiplier=-1))
            step(pool.affine_select(out=head_of[:], in_=ones[:, 0:HC], compare_op=ALU.is_ge, fill=0.0, base=0,
                                    pattern=[[-CD, HC]], channel_multiplier=1))
            step(pool.affine_select(out=head_of[:], in_=head_of[:], compare_op=ALU.is_ge, fill=0.0, base=CD - 1,
                                    pattern=[[CD, HC]], channel_multiplier=-1))
            step(pool.memset(power[:], -0.5))
            step(pool.memset(q_pad[0][DH:P, :], 0.0))
            step(pool.memset(q_pad[1][0:DH, :], 0.0))
            step(pool.memset(v_rest[:], 0.0))
            step(pool.memset(v_main[:], 1.0))
            step(pool.memset(tile_base[:, 0, :], 0.0))
            for r in range(UH):
                step(pool.memset(v_rest[r * RS:r * RS + KR, :, r::UH, CD:V1], 1.0))
            step(pool.iota(jm8, [[0, NT], [1, NE]], base=-NE, channel_multiplier=0,
                           allow_small_or_imprecise_dtypes=True))
            step(pool.iota(block_starts[:], [[0, NE], [BLK, T // BLK]], base=0, channel_multiplier=0,
                           allow_small_or_imprecise_dtypes=True))
            step(pool.iota(block_no[:], [[1, MAX_BLOCKS], [0, NE]], base=0, channel_multiplier=0,
                           allow_small_or_imprecise_dtypes=True))
            pool.memset(zero_rows[:], 0.0).then_inc(consts_ready, 1)
            pool.wait_ge(consts_ready, 1)
            for r in range(UH):
                for b in range(NB):
                    pool.dma_start(v_rest[r * RS:r * RS + KR, b, r::UH, 0:CD],
                                   ctx[b, P:K2, :].rearrange("k (h d) -> k h d", d=CD)[:, r::UH, :]).then_inc(rest_in, 16)
            pool.dma_start(wo_sb[:], wo.rearrange("(j p) d -> p j d", p=P)).then_inc(w_in, 16)
            pool.dma_start(rw_sb[:], rw.rearrange("(c p) f -> p c f", p=P)).then_inc(w_in, 16)
            for dst, src in ((bo_b, bo), (bout_b, b_out), (sb2_b, sb2), (rb_b, rb)):
                pool.dma_start(dst[:], src.partition_broadcast(P)).then_inc(rows_in, 16)
            pool.wait_ge(stats_done, 1)
            step(pool.tensor_scalar(rstd[:], mean_var[:, :, 1], EPS, None, ALU.add))
            pool.tensor_tensor(rstd[:], rstd[:], power[:], ALU.pow).then_inc(rstd_done, 1)
            for n in range(MAX_BLOCKS * TT):
                pool.dma_start(xs[n * P:(n + 1) * P, :], zero_rows[:]).then_inc(xs_zero, 16)
            pool.wait_ge(o_taken, TURNS * STEPS + FREE)
            for u in range(2):
                step(pool.memset(pr[u], 0.0))
            pool.sem_inc(zeros_ready, 1)
            with pool.Fori(0, NT // 2) as j:
                for ln in range(2):
                    for u in range(2):
                        pool.wait_ge(var_done[u], j * 2 + ln + 1)
                        pool.tensor_tensor(ln_r[u], ln_var[u], power[:, 0:1], ALU.pow).then_inc(rstd2_done[u], 1)
                for u in range(2):
                    pool.wait_ge(xn2_ready[u], j * 2 + 2)
                    pool.tensor_copy(o_all[:, ds(j * 2 + u, 1), 0:D].rearrange("p a d -> p (a d)"), xn2[u]
                                     ).then_inc(x3_stored[u], 1)
            pool.wait_ge(dest_ready, 2)
            for u in range(2):
                pool.wait_ge(x3_stored[u], NT // 2 + FREE)
            pool.wait_ge(xs_zero, 16 * MAX_BLOCKS * TT)
            for t in range(NT):
                for k in range(2):
                    pool.indirect_dma_start(xs, bass.IndirectOffsetOnAxis(ap=dest[:, k, t:t + 1], axis=0),
                                            o_all[:, t, 0:D], None).then_inc(scattered, 16)
            for u in range(2):
                pool.wait_ge(y_stored[u], 16 * (MAX_BLOCKS // 2) + 16 * FREE)
            for t in range(NT):
                if t >= 2:
                    pool.wait_ge(final_done, t - 1)
                for k in range(2):
                    pool.indirect_dma_start(y_got[k][:, t % 2, :], None, ys,
                                            bass.IndirectOffsetOnAxis(ap=dest[:, k, t:t + 1], axis=0)
                                            ).then_inc(gathered[t % 2], 16)

        @block.vector
        def _(v):
            step = Chain(v, vector_step)
            for signal in (*mask_ready, *logits_taken, *yb_taken, ffn_taken, o_taken):
                v.sem_inc(signal, FREE)
            v.wait_ge(x_in, 32)
            for t in range(NT):
                st = v.bn_stats(stats[:, t, :], x_sb[:, t, :])
            step(st)
            for t in range(NT):
                ag = v.bn_aggr(mean_var[:, t, :], stats[:, t, :])
            ag.then_inc(stats_done, 1)
            v.wait_ge(prep_turned, 1)
            v.wait_ge(consts_ready, 1)
            for b in range(NB):
                for c in range(C):
                    for h in range(HC):
                        v.tensor_scalar(ctx_diag[:, b, c, h, :], sc[:, b * 512 + c * K2:b * 512 + (c + 1) * K2],
                                        head_of[:, h:h + 1], None, ALU.mult)
                v.tensor_copy(v_main[:, b, :, 0:CD], ctx_in[:, b, 0, :].rearrange("p (h d) -> p h d", d=CD))
            v.tensor_copy(w_outT[:].rearrange("p c d -> p (c d)"), sc[:, 1024:1536])
            v.tensor_copy(bias_qkv[:].rearrange("p a b -> p (a b)"), sc[:, 1536:1536 + 3 * NP])
            v.tensor_copy(b1T[:], sc[:, 1536 + P:1536 + P + (NE + 1) * FJ]).then_inc(prep_copied, 1)
            v.wait_ge(rstd_done, 1)
            with v.Fori(0, NT // 2) as j:
                for u in range(2):
                    t = j * 2 + u
                    v.wait_ge(xn_turned[u], j + FREE)
                    v.tensor_scalar(xn[u], x_sb[:, ds(t, 1), :].rearrange("p a d -> p (a d)"),
                                    mean_var[:, ds(t, 1), 0], rstd[:, ds(t, 1)],
                                    ALU.subtract, ALU.mult).then_inc(xn_ready[u], 1)

            def scaled_q(it):
                v.wait_ge(proj_done, it * 3 + 1 + FREE)
                for h in range(2):
                    rows = slice(h * DH, (h + 1) * DH)
                    q = v.tensor_scalar(q_pad[h][rows, :], sc[rows, 0:S], bias_qkv[rows, 0, ds(p, 1)],
                                        DH ** -0.5, ALU.add, ALU.mult)
                q.then_inc(q_taken, 1)

            def row_max(it, s):
                n = (s // 2 + 1) * P
                v.wait_ge(scores_done, it * STEPS + s + 1)
                v.tensor_reduce(neg_max[:, s % 2:s % 2 + 1], sc[:, (s % 2) * 1024:(s % 2) * 1024 + n], AX.X, ALU.max,
                                negate=True).then_inc(max_done, 1)

            with v.Fori(0, NB) as b:
                with v.Fori(0, NP) as p:
                    it = b * NP + p
                    step.loop(it, STEPS)
                    scaled_q(it)
                    v.wait_ge(turned[0], it * FILLS + 1)
                    v.tensor_copy(v_pair[:, 0:4, :].rearrange("p a b -> p (a b)"), tp[0][:]).then_inc(turned_taken[0], 1)
                    row_max(it, 0)
                    row_max(it, 1)
                    for s in range(STEPS):
                        for k, t0, m in chunks[s]:
                            if k == 0:
                                v.wait_ge(turned[0], it * FILLS + fills[s][0])
                                v.tensor_copy(probT[s % 2][:, t0:t0 + m, :].rearrange("p a b -> p (a b)"),
                                              tp[0][:, 0:m * P]).then_inc(turned_taken[0], 1)
                        if s + 2 < STEPS:
                            row_max(it, s + 2)
                        v.wait_ge(exp_done, it * STEPS + s + 1)
                        step(v.reciprocal(row_inv[:, s:s + 1], row_sum[:, s:s + 1]))
                        v.wait_ge(pv_done, it * STEPS + s + 1)
                        v.tensor_scalar(o_all[:, ds(b * TB + s // 2, 1), ds(p * P + (s % 2) * DH, DH)]
                                        .rearrange("p a d -> p (a d)"),
                                        acc[s % 2][:, 0:DH], row_inv[:, s:s + 1], None, ALU.mult).then_inc(o_taken, 1)
            step.end(TURNS)

            def x_tile(t):
                return x_sb[:, ds(t, 1), :].rearrange("p a d -> p (a d)")

            def residual(t, u, add, row):
                step(v.tensor_tensor(x_tile(t), add, x_tile(t), ALU.add))
                step(v.scalar_tensor_tensor(x_tile(t), x_tile(t), 1.0, row, ALU.mult, ALU.add, accum_out=ln_sum[u]))
                step(v.tensor_scalar(ln_sum[u], ln_sum[u], -1.0 / D, None, ALU.mult))
                step(v.tensor_scalar(xn2[u], x_tile(t), ln_sum[u], None, ALU.add))
                step(v.tensor_tensor_reduce(ln_sq[u], xn2[u], xn2[u], 1.0, 0.0, ALU.mult, ALU.add, ln_var[u]))
                v.tensor_scalar(ln_var[u], ln_var[u], 1.0 / D, EPS, ALU.mult, ALU.add).then_inc(var_done[u], 1)

            def normalize(u, ln, jj):
                v.wait_ge(rstd2_done[u], jj * 2 + ln)
                v.tensor_scalar(xn2[u], xn2[u], ln_r[u], None, ALU.mult).then_inc(xn2_ready[u], 1)

            v.wait_ge(rows_in, 64)
            with v.Fori(0, NT // 2) as jj:
                step.loop(jj, 2 * (5 + NQ + 1 + 5))
                for u in range(2):
                    v.wait_ge(mask_staged[u], jj * 16 + 16)
                    v.wait_ge(energy_done[u], jj * NQ + FREE)
                    v.tensor_scalar(mask_add[u], mask_in[u], 0.0, CROSS_MASKED, ALU.is_equal, ALU.mult
                                    ).then_inc(mask_ready[u], 1)
                for u in range(2):
                    v.wait_ge(o_turned[u], jj + 1 + FREE)
                    v.tensor_copy(oT[u][:, 0:4, :].rearrange("p a b -> p (a b)"), sc[:, u * 1024:u * 1024 + 512]
                                  ).then_inc(o_turned_dve[u], 1)
                for u in range(2):
                    v.wait_ge(y_done[u], jj + 1)
                    v.wait_ge(x3_stored[u], jj + FREE)
                    residual(jj * 2 + u, u, acc[u][:, 0:D], bo_b[:])
                for u in range(2):
                    normalize(u, 1, jj)

                def shift(k):
                    u, q = k % 2, k // 2
                    v.wait_ge(energy_done[u], jj * NQ + q + 1 + FREE)
                    e = sc[:, u * 1024:(u + 1) * 1024].rearrange("p (a n) -> p a n", a=2)[:, :, 0:2 * K2] \
                        .rearrange("p a (h k) -> p a h k", h=2)
                    step(v.tensor_reduce(cmax[u].rearrange("p (a h) -> p a h", a=2), e, AX.X, ALU.max))
                    for a in range(2):
                        i = v.tensor_tensor(energy[u][:, 2 * a:2 * a + 2, :], e[:, a],
                                            cmax[u][:, 2 * a:2 * a + 2].unsqueeze(2).to_broadcast([P, 2, K2]),
                                            ALU.subtract)
                    i.then_inc(shifted_done[u], 1)
                shift(0)
                shift(1)
                for k in range(2 * NQ):
                    u, q = k % 2, k // 2
                    v.wait_ge(p_turned[u], jj * NQ + q + 1)
                    v.tensor_copy(prT[u], acc[u][:, REST:REST + P]).then_inc(pr_taken[u], 1)
                    if k + 2 < 2 * NQ:
                        shift(k + 2)
                for u in range(2):
                    v.wait_ge(cpv_done[u], (jj + 1) * NQ)
                    sums = acc[u][:, 0:H * V1].rearrange("p (h d) -> p h d", d=V1)
                    step(v.reciprocal(cinv[u], sums[:, :, CD]))
                    v.tensor_tensor(o2[u].rearrange("p (h d) -> p h d", d=CD), sums[:, :, 0:CD],
                                    cinv[u].unsqueeze(2).to_broadcast([P, H, CD]), ALU.mult).then_inc(o2_ready[u], 1)
                for u in range(2):
                    v.wait_ge(y2_done[u], jj + 1)
                    residual(jj * 2 + u, u, acc[u][:, 0:D], bout_b[:])
                for u in range(2):
                    normalize(u, 2, jj)
                for u in range(2):
                    v.wait_ge(logits_done[u], jj + 1)
                    v.tensor_tensor(logits[:, ds(jj * 2 + u, 1), :].rearrange("p a d -> p (a d)"),
                                    acc[u][:, 0:NE], rb_b[:], ALU.add).then_inc(logits_taken[u], 1)
            step.end(NT // 2)

            for u in range(2):
                v.wait_ge(logits_taken[u], NT // 2 + FREE)

            def over_experts(a):
                return a.unsqueeze(2).to_broadcast([P, NT, NE])

            def top(src, best, at, hot):
                step(v.tensor_reduce(best, src, AX.X, ALU.max))
                step(v.tensor_tensor(eq, src, over_experts(best), ALU.is_equal))
                step(v.tensor_tensor(cand, eq, jm8, ALU.mult))
                step(v.tensor_reduce(at, cand, AX.X, ALU.min))
                step(v.tensor_tensor(hot, jm8, over_experts(at), ALU.is_equal))
            top(logits[:], first_max, first_at, hot1)
            step(v.scalar_tensor_tensor(masked, hot1, -3e38, logits[:], ALU.mult, ALU.add))
            top(masked, second_max, second_at, hot2)
            v.tensor_tensor(both, hot1, hot2, ALU.add).then_inc(both_ready, 1)
            v.tensor_tensor(gap, second_max, first_max, ALU.subtract)
            v.tensor_tensor(shifted, logits[:], over_experts(first_max), ALU.subtract).then_inc(gap_ready, 1)
            v.wait_ge(counted, 1)
            for t in range(NT):
                step(v.tensor_tensor(tile_base[:, t + 1, :], tile_base[:, t, :], acc[1][:, t * NE:(t + 1) * NE], ALU.add))
            step(v.tensor_tensor(block_cmp[:], tile_base[:, NT, :].unsqueeze(2).to_broadcast([P, NE, T // BLK]),
                                 block_starts[:], ALU.is_gt))
            step(v.tensor_reduce(n_blocks, block_cmp[:], AX.X, ALU.add))
            step(v.tensor_copy(blocks_incl, n_blocks))
            for e in range(1, NE):
                step(v.tensor_tensor(blocks_incl[:, e:e + 1], blocks_incl[:, e - 1:e], n_blocks[:, e:e + 1], ALU.add))
            step(v.tensor_tensor(block_ge[:], blocks_incl.unsqueeze(1).to_broadcast([P, MAX_BLOCKS, NE]),
                                 block_no[:], ALU.is_le))
            step(v.tensor_reduce(block_f[:], block_ge[:], AX.X, ALU.add))
            v.tensor_scalar(block_expert[:], block_f[:], float(NE - 1), None, ALU.min).then_inc(experts_ready, 1)
            step(v.tensor_tensor(expert_base, blocks_incl, n_blocks, ALU.subtract))
            step(v.tensor_scalar(expert_base, expert_base, float(BLK), None, ALU.mult))
            step(v.tensor_tensor(pos, acc[0][:, 0:NT * NE].rearrange("p (t e) -> p t e", e=NE), tile_base[:, 0:NT, :], ALU.add))
            step(v.tensor_tensor(pos2, pos, expert_base.unsqueeze(1).to_broadcast([P, NT, NE]), ALU.add))
            for k, hot in enumerate((hot1, hot2)):
                step(v.tensor_tensor(picked, hot, pos2, ALU.mult))
                step(v.tensor_reduce(destf, picked, AX.X, ALU.add))
                step(v.tensor_copy(dest[:, k, :], destf))
            v.sem_inc(dest_ready, 2)
            v.wait_ge(route_exp_done, 1)
            step(v.tensor_reduce(total, expd, AX.X, ALU.add))
            step(v.reciprocal(inv_total, total))
            step(v.tensor_tensor(gap_exp, gap_exp, inv_total, ALU.mult))
            step(v.tensor_tensor(w_sum, inv_total, gap_exp, ALU.add))
            step(v.tensor_scalar(w_sum, w_sum, 1e-9, None, ALU.add))
            step(v.reciprocal(w_inv, w_sum))
            step(v.tensor_tensor(weight[:, 0, :], inv_total, w_inv, ALU.mult))
            step(v.tensor_tensor(weight[:, 1, :], gap_exp, w_inv, ALU.mult))

            with v.Fori(0, NSH) as n:
                step.loop(n, 2 * TT)
                v.wait_ge(ffn_done, n + 1)
                for tt in range(TT):
                    step(v.tensor_tensor(x_tile(n * TT + tt), acc[tt][:, 0:D], x_tile(n * TT + tt), ALU.add))
                for tt in range(TT):
                    step(v.tensor_tensor(x_tile(n * TT + tt), x_tile(n * TT + tt), sb2_b[:], ALU.add))
                v.sem_inc(ffn_taken, 1)
            step.end(NSH)
            with v.Fori(0, MAX_BLOCKS // 2) as j:
                for u in range(2):
                    n = j * 2 + u
                    v.wait_ge(xb_turned, n + 1)
                    v.tensor_copy(xbT[u].rearrange("p a b -> p (a b)"), tp[0][:]).then_inc(xb_taken, 1)
                    v.wait_ge(ffn_done, n + NSH + 1)
                    v.wait_ge(y_stored[u], j * 16 + 16 * FREE)
                    for tt in range(TT):
                        y = v.tensor_tensor(yb[u][:, tt, :], acc[tt][:, 0:D], b2[u], ALU.add)
                    y.then_inc(yb_taken[u], 1)
            for t in range(NT):
                v.wait_ge(gathered[t % 2], (t // 2 + 1) * 32)
                step(v.scalar_tensor_tensor(x_sb[:, t, :], y_got[0][:, t % 2, :], weight[:, 0, t:t + 1],
                                            x_sb[:, t, :], ALU.mult, ALU.add))
                v.scalar_tensor_tensor(x_sb[:, t, :], y_got[1][:, t % 2, :], weight[:, 1, t:t + 1],
                                       x_sb[:, t, :], ALU.mult, ALU.add).then_inc(final_done, 1)

        @block.scalar
        def _(act):
            for signal in xT_ready:
                act.sem_inc(signal, FREE)
            for signal in y_stored:
                act.sem_inc(signal, 16 * FREE)
            with act.Fori(0, NT // 2) as j:
                for u in range(2):
                    act.wait_ge(xn_turned[u], j + 1 + FREE)
                    act.activation(xT[:, :, ds((j * 2 + u) * P, P)], tp[u][:, 0:D].rearrange("p (c t) -> p c t", c=C),
                                   ACT.Copy).then_inc(xT_ready[u], 1)
            act.wait_ge(prep_copied, 1)

            def softmax(it, s):
                n = (s // 2 + 1) * P
                act.wait_ge(max_done, it * STEPS + s + 1)
                act.activation(prob[s % 2][:, 0:n], sc[:, (s % 2) * 1024:(s % 2) * 1024 + n], ACT.Exp,
                               bias=neg_max[:, s % 2:s % 2 + 1], accum_out=row_sum[:, s:s + 1]).then_inc(exp_done, 1)

            with act.Fori(0, NB) as b:
                with act.Fori(0, NP) as p:
                    it = b * NP + p
                    act.wait_ge(proj_done, it * 3 + 2 + FREE)
                    act.activation(kT, sc[:, 1024:2048], ACT.Identity, bias=bias_qkv[:, 1, ds(p, 1)]).then_inc(k_taken, 1)
                    act.wait_ge(proj_done, it * 3 + 3 + FREE)
                    act.activation(vT, sc[:, 0:1024], ACT.Identity, bias=bias_qkv[:, 2, ds(p, 1)]).then_inc(v_taken, 1)
                    act.wait_ge(turned[1], it * FILLS + 1)
                    act.activation(v_pair[:, 4:8, :].rearrange("p a b -> p (a b)"), tp[1][:], ACT.Copy
                                   ).then_inc(turned_taken[1], 1)
                    softmax(it, 0)
                    softmax(it, 1)
                    for s in range(STEPS):
                        for k, t0, m in chunks[s]:
                            if k == 1:
                                act.wait_ge(turned[1], it * FILLS + fills[s][1])
                                act.activation(probT[s % 2][:, t0:t0 + m, :].rearrange("p a b -> p (a b)"),
                                               tp[1][:, 0:m * P], ACT.Copy).then_inc(turned_taken[1], 1)
                        if s + 2 < STEPS:
                            softmax(it, s + 2)
            act.wait_ge(zeros_ready, 1)
            with act.Fori(0, NT // 2) as jj:
                for u in range(2):
                    act.wait_ge(o_turned[u], jj + 1 + FREE)
                    act.activation(oT[u][:, 4:8, :].rearrange("p a b -> p (a b)"), sc[:, u * 1024 + 512:(u + 1) * 1024],
                                   ACT.Copy).then_inc(o_turned_act[u], 1)

                def take_xn2(ln):
                    for u in range(2):
                        act.wait_ge(xn2_turned[u], jj * 2 + ln)
                        turned_rows = tp[u][:, 0:D].rearrange("p (c t) -> p c t", c=C)
                        i = act.activation(xn2T[u], turned_rows, ACT.Copy)
                        if ln == 2:
                            i = act.activation(xT[:, :, ds((jj * 2 + u) * P, P)], turned_rows, ACT.Copy)
                        i.then_inc(xn2_taken[u], 1)
                take_xn2(1)

                def cross_exp(k):
                    u, q = k % 2, k // 2
                    act.wait_ge(shifted_done[u], jj * NQ + q + 1)
                    act.activation(pm[u], energy[u][:, :, 0:P], ACT.Exp, scale=CD ** -0.5)
                    act.activation(pr[u][:, :, 0:KR], energy[u][:, :, P:K2], ACT.Exp, scale=CD ** -0.5
                                   ).then_inc(cexp_done[u], 1)
                cross_exp(0)
                cross_exp(1)
                for k in range(2 * NQ):
                    u, q = k % 2, k // 2
                    act.wait_ge(p_turned[u], jj * NQ + q + 1)
                    act.activation(pmT[u].rearrange("p a b -> p (a b)"), tp[u][:], ACT.Copy).then_inc(pm_taken[u], 1)
                    if k + 2 < 2 * NQ:
                        cross_exp(k + 2)
                for u in range(2):
                    act.wait_ge(o2_turned[u], jj + 1)
                    act.activation(o2T[u], tp[u][:, 0:D].rearrange("p (c t) -> p c t", c=C), ACT.Copy
                                   ).then_inc(o2_taken[u], 1)
                take_xn2(2)
            act.wait_ge(gap_ready, 1)
            act.activation(gap_exp, gap, ACT.Exp)
            act.activation(expd, shifted, ACT.Exp).then_inc(route_exp_done, 1)
            def gelu(m, bias):
                for k in range(FJ // 2):
                    act.wait_ge(h_done, m * (FJ // 2) + k + 1)
                    for i in range(2):
                        y = act.activation(hT[:, 2 * k + i, :], sc[:, k * 512 + i * BLK:k * 512 + (i + 1) * BLK], ACT.Gelu,
                                           bias=bias[:, 2 * k + i:2 * k + i + 1])
                    y.then_inc(gelu_done, 1)
            with act.Fori(0, NSH) as n:
                gelu(n, b1T[:, NE * FJ:(NE + 1) * FJ])
            with act.Fori(0, MAX_BLOCKS // 2) as j:
                for u in range(2):
                    act.wait_ge(blk_in[u], (j + 1) * 80)
                    gelu(j * 2 + u + NSH, b1[u])
                    act.wait_ge(yb_taken[u], j + 1 + FREE)
                    act.dma_start(ys[ds((j * 2 + u) * BLK, BLK), :].rearrange("(t p) d -> p t d", p=P), yb[u]
                                  ).then_inc(y_stored[u], 16)

        @block.tensor
        def _(pe):
            for signal in (proj_done, *xn_turned, *o_turned, *energy_done):
                pe.sem_inc(signal, FREE)
            pe.wait_ge(consts_ready, 1)
            pe.wait_ge(small_in, 16 * (2 * NB + 6))
            for b in range(NB):
                for c in range(C):
                    at = b * 512 + c * K2
                    pe.transpose(sc[:, at:at + P], ctx_in[:, b, 0, c * P:(c + 1) * P], ident[:])
                    pe.transpose(sc[:, at + P:at + K2], ctx_in[0:KR, b, 1, c * P:(c + 1) * P], ident[0:KR, 0:KR])
            for ci in range(C):
                for co in range(C):
                    pe.transpose(sc[:, 1024 + ci * D + co * P:1024 + ci * D + (co + 1) * P],
                                 wout_in[:, co, ci * P:(ci + 1) * P], ident[:])
            pe.transpose(sc[:, 1536:1536 + 3 * NP], bias_in[0:3 * NP, :], ident[0:3 * NP, 0:3 * NP])
            nb1 = (NE + 1) * FJ
            pe.transpose(sc[:, 1536 + P:1536 + P + nb1], b1_in[0:nb1, :], ident[0:nb1, 0:nb1]).then_inc(prep_turned, 1)
            with pe.Fori(0, NT // 2) as j:
                for u in range(2):
                    pe.wait_ge(xn_ready[u], j + 1)
                    pe.wait_ge(xT_ready[u], j + FREE)
                    for c in range(C):
                        tr = pe.transpose(tp[u][:, c * P:(c + 1) * P], xn[u][:, c * P:(c + 1) * P], ident[:])
                    tr.then_inc(xn_turned[u], 1)
            for u in range(2):
                pe.wait_ge(xT_ready[u], NT // 2 + FREE)
            pe.wait_ge(prep_copied, 1)

            def project(b, k, at):
                for n in range(S // 512):
                    for c in range(C):
                        mm = pe.matmul(sc[:, at + n * 512:at + (n + 1) * 512], w_pair[:, k, c, :],
                                       xT[:, c, ds(b * S + n * 512, 512)], start=(c == 0), stop=(c == C - 1))
                mm.then_inc(proj_done, 1)

            def scores(s):
                i, h = s // 2, s % 2
                n = (i + 1) * P
                at = h * 1024
                for n0 in range(0, n, 512):
                    w = min(512, n - n0)
                    diag = n0 + w == n
                    mm = pe.matmul(sc[:, at + n0:at + n0 + w], q_pad[h][:, i * P:(i + 1) * P], kT[:, n0:n0 + w],
                                   start=True, stop=not diag)
                pe.matmul(sc[:, at + n - P:at + n], identb[:], causal[:], start=False, stop=True
                          ).then_inc(scores_done, 1)

            with pe.Fori(0, NB) as b:
                with pe.Fori(0, NP) as p:
                    it = b * NP + p
                    pe.wait_ge(w_pair_in, (it + 1) * (16 * 3 * C))
                    project(b, 0, 0)
                    project(b, 1, 1024)
                    pe.wait_ge(q_taken, it + 1)
                    project(b, 2, 0)
                    pe.wait_ge(v_taken, it + 1)
                    for k in range(2):
                        for m in range(4):
                            tr = pe.transpose(tp[k][:, m * P:(m + 1) * P], vT[:, (k * 4 + m) * P:(k * 4 + m + 1) * P],
                                              ident[:])
                        tr.then_inc(turned[k], 1)
                    pe.wait_ge(k_taken, it + 1)
                    scores(0)
                    scores(1)
                    for s in range(STEPS):
                        i, h = s // 2, s % 2
                        pe.wait_ge(exp_done, it * STEPS + s + 1)
                        for k, t0, m in chunks[s]:
                            pe.wait_ge(turned_taken[k], it * FILLS + fills[s][k] - 1)
                            for r in range(m):
                                tr = pe.transpose(tp[k][:, r * P:(r + 1) * P], prob[h][:, (t0 + r) * P:(t0 + r + 1) * P],
                                                  ident[:])
                            tr.then_inc(turned[k], 1)
                        if s + 2 < STEPS:
                            scores(s + 2)
                        pe.wait_ge(o_taken, it * STEPS + max(s - 1, 0) + FREE)
                        for k, t0, m in chunks[s]:
                            pe.wait_ge(turned_taken[k], it * FILLS + fills[s][k])
                            if s == 0:
                                pe.wait_ge(turned_taken[1], it * FILLS + 1)
                            for r in range(t0, t0 + m):
                                mm = pe.matmul(acc[h][:, 0:DH], probT[h][:, r, :], v_pair[:, r, h * DH:(h + 1) * DH],
                                               start=(r == 0), stop=(r == i))
                        mm.then_inc(pv_done, 1)
            pe.wait_ge(o_taken, TURNS * STEPS + FREE)
            pe.wait_ge(w_in, 32)
            pe.wait_ge(rest_in, 16 * UH * NB)
            with pe.Fori(0, NB) as b:
                with pe.Fori(0, TB // 2) as j:
                    jj = b * (TB // 2) + j
                    for u in range(2):
                        pe.wait_ge(o_staged[u], jj * 16 + 16)
                        for r in range(J):
                            tr = pe.transpose(sc[:, u * 1024 + r * P:u * 1024 + (r + 1) * P],
                                              o_tile[u][:, r * P:(r + 1) * P], ident[:])
                        tr.then_inc(o_turned[u], 1)
                    for u in range(2):
                        pe.wait_ge(o_turned_dve[u], jj + 1)
                        pe.wait_ge(o_turned_act[u], jj + 1)
                        pe.wait_ge(logits_taken[u], jj + FREE)
                        for r in range(J):
                            mm = pe.matmul(acc[u][:, 0:D], oT[u][:, r, :], wo_sb[:, r, :], start=(r == 0), stop=(r == J - 1))
                        mm.then_inc(y_done[u], 1)

                    def turn_xn2(ln):
                        for u in range(2):
                            pe.wait_ge(xn2_ready[u], jj * 2 + ln)
                            for c in range(C):
                                tr = pe.transpose(tp[u][:, c * P:(c + 1) * P], xn2[u][:, c * P:(c + 1) * P], ident[:])
                            tr.then_inc(xn2_turned[u], 1)
                    turn_xn2(1)

                    def energies(k):
                        u, q = k % 2, k // 2
                        c, h0 = q * UH // HC, q * UH % HC
                        if q == 0:
                            pe.wait_ge(xn2_taken[u], jj * 2 + 1)
                            pe.wait_ge(mask_ready[u], jj + 1 + FREE)
                        for a in range(2):
                            bank = sc[:, u * 1024 + a * 512:u * 1024 + a * 512 + 2 * K2]
                            pe.matmul(bank, xn2T[u][:, c, :],
                                      ctx_diag[:, ds(b, 1), c, h0 + 2 * a:h0 + 2 * a + 2, :].rearrange("p a h k -> p (a h k)"),
                                      start=True, stop=False)
                            mm = pe.matmul(bank.rearrange("p (h k) -> p h k", h=2), identb[:],
                                           mask_add[u].unsqueeze(1).to_broadcast([P, 2, K2]), start=False, stop=True)
                        mm.then_inc(energy_done[u], 1)
                    energies(0)
                    energies(1)
                    for k in range(2 * NQ):
                        u, q = k % 2, k // 2
                        pe.wait_ge(cexp_done[u], jj * NQ + q + 1)
                        for r in range(UH):
                            pe.transpose(tp[u][:, r * P:(r + 1) * P], pm[u][:, r, :], ident[:])
                        pe.transpose(acc[u][:, REST:REST + P], pr[u].rearrange("p h k -> p (h k)"), ident[:]
                                     ).then_inc(p_turned[u], 1)
                        if k + 2 < 2 * NQ:
                            energies(k + 2)
                        pe.wait_ge(pr_taken[u], jj * NQ + q + 1)
                        pe.wait_ge(pm_taken[u], jj * NQ + q + 1)
                        at = q * UH * V1
                        pe.matmul(acc[u][:, at:at + UH * V1], prT[u],
                                  v_rest[:, ds(b, 1), q * UH:(q + 1) * UH, :].rearrange("p a h k -> p (a h k)"),
                                  start=True, stop=False)
                        for r in range(UH):
                            mm = pe.matmul(acc[u][:, at + r * V1:at + (r + 1) * V1], pmT[u][:, r, :],
                                           v_main[:, ds(b, 1), q * UH + r, :].rearrange("p a k -> p (a k)"),
                                           start=False, stop=(r == UH - 1))
                        mm.then_inc(cpv_done[u], 1)
                    for u in range(2):
                        pe.wait_ge(o2_ready[u], jj + 1)
                        for c in range(C):
                            tr = pe.transpose(tp[u][:, c * P:(c + 1) * P], o2[u][:, c * P:(c + 1) * P], ident[:])
                        tr.then_inc(o2_turned[u], 1)
                    for u in range(2):
                        pe.wait_ge(o2_taken[u], jj + 1)
                        for c in range(C):
                            mm = pe.matmul(acc[u][:, 0:D], o2T[u][:, c, :], w_outT[:, c, :], start=(c == 0), stop=(c == C - 1))
                        mm.then_inc(y2_done[u], 1)
                    turn_xn2(2)
                    for u in range(2):
                        pe.wait_ge(xn2_taken[u], jj * 2 + 2)
                        for c in range(C):
                            mm = pe.matmul(acc[u][:, 0:NE], xn2T[u][:, c, :], rw_sb[:, c, :], start=(c == 0), stop=(c == C - 1))
                        mm.then_inc(logits_done[u], 1)
            pe.wait_ge(both_ready, 1)
            bf = both.rearrange("p t e -> p (t e)")
            pe.matmul(acc[0][:, 0:NT * NE], lower[:], bf, start=True, stop=True)
            pe.matmul(acc[1][:, 0:NT * NE], ones[:], bf, start=True, stop=True).then_inc(counted, 1)

            def ffn_in(w1u, xT_of):
                for k in range(FJ):
                    for c in range(C):
                        mm = pe.matmul(sc[:, k * BLK:(k + 1) * BLK], w1u[:, c, k * P:(k + 1) * P], xT_of(c),
                                       start=(c == 0), stop=(c == C - 1))
                    if k % 2:
                        mm.then_inc(h_done, 1)

            def ffn_out(m, w2u):
                for k in range(FJ):
                    if k % 2 == 0:
                        pe.wait_ge(gelu_done, m * (FJ // 2) + k // 2 + 1)
                    for tt in range(TT):
                        mm = pe.matmul(acc[tt][:, 0:D], hT[:, k, tt * P:(tt + 1) * P], w2u[:, k, :],
                                       start=(k == 0), stop=(k == FJ - 1))
                mm.then_inc(ffn_done, 1)

            pe.wait_ge(sw_in, 32)
            pe.wait_ge(dest_ready, 2)
            with pe.Fori(0, NSH) as n:
                ffn_in(w1[1], lambda c: xT[:, c, ds(n * BLK, BLK)])
                pe.wait_ge(ffn_taken, n + FREE)
                ffn_out(n, w2[1])
            pe.wait_ge(ffn_taken, NSH + FREE)
            with pe.Fori(0, MAX_BLOCKS // 2) as j:
                for u in range(2):
                    n = j * 2 + u
                    pe.wait_ge(blk_in[u], (j + 1) * 80)
                    for c in range(C):
                        for tt in range(TT):
                            tr = pe.transpose(tp[0][:, c * BLK + tt * P:c * BLK + (tt + 1) * P],
                                              xb[u][:, tt, c * P:(c + 1) * P], ident[:])
                    tr.then_inc(xb_turned, 1)
                    pe.wait_ge(xb_taken, n + 1)
                    ffn_in(w1[u], lambda c: xbT[u][:, c, :])
                    if u == 0:
                        pe.wait_ge(yb_taken[1], j + FREE)
                    else:
                        pe.wait_ge(yb_taken[0], j + 1 + FREE)
                    ffn_out(n + NSH, w2[u])


_INS = ['x', 'ctx_1024', 'mask_Bx1xSxS2_ik1', 'L0_attn_Wq', 'L0_attn_Wk', 'L0_attn_Wv', 'L0_attn_bq', 'L0_attn_bk',
        'L0_attn_bv', 'L0_attn_Wo', 'L0_attn_bo', 'L0_xattn_W_out', 'L0_xattn_b_out', 'L0_ffn_shared_w1',
        'L0_ffn_shared_b1', 'L0_ffn_shared_w2', 'L0_ffn_shared_b2', 'L0_ffn_router_w', 'L0_ffn_router_b',
        'L0_ffn_exp_w1', 'L0_ffn_exp_b1', 'L0_ffn_exp_w2', 'L0_ffn_exp_b2']


def kernel(**inputs):
    import numpy as _np
    import concourse.bacc as _bacc
    from concourse import mybir as _mybir
    from concourse.bass_utils import run_bass_kernel_spmd as _run

    nc = _bacc.Bacc("TRN2", target_bir_lowering=False, num_devices=1)
    arrays, args = {}, []
    for name in _INS:
        a = _np.ascontiguousarray(inputs[name])
        arrays[f"in_{name}_dram"] = a
        args.append(nc.dram_tensor(f"in_{name}_dram", a.shape, _mybir.dt.from_np(a.dtype), kind="ExternalInput").ap())
    shape = inputs['x'].shape
    args.append(nc.dram_tensor("out_dram", shape, _mybir.dt.from_np(_np.dtype('float32')), kind="ExternalOutput").ap())
    decoder_layer(nc, *args)
    r = _run(nc, [arrays], core_ids=[0])
    return r.results[0]["out_dram"]
```

```python
from contextlib import ExitStack, contextmanager

import numpy as np
import concourse.bass as bass
from concourse import mybir

F32 = mybir.dt.float32
F32R = mybir.dt.float32r
BF16 = mybir.dt.bfloat16
I32 = mybir.dt.int32
U32 = mybir.dt.uint32
ALU = mybir.AluOpType
ACT = mybir.ActivationFunctionType
AX = mybir.AxisListType
ds = bass.ds

P = 128
EPS = 1e-5
MASKED = -1e30
FREE = 1
FREE_2 = 2
CROSS_MASKED = -1e20


class Chain:

    def __init__(self, eng, sem):
        self.eng, self.sem, self.base, self.k, self.turn, self.per = eng, sem, 0, 0, 0, 0

    def loop(self, turn, per):
        self.base += self.k
        self.turn, self.per, self.k = turn, per, 0

    def end(self, turns):
        assert self.k == self.per, (self.k, self.per)
        self.base += turns * self.per
        self.turn, self.per, self.k = 0, 0, 0

    def __call__(self, ins):
        self.k += 1
        ins.then_inc(self.sem, 1)
        self.eng.wait_ge(self.sem, self.turn * self.per + (self.base + self.k))


def decoder_layer(nc, x, ctx, mask, wq, wk, wv, bq, bk, bv, wo, bo, w_out, b_out,
                  sw1, sb1, sw2, sb2, rw, rb, ew1, eb1, ew2, eb2, out):
    NB, S, D = x.shape
    H, _, DH = wq.shape
    K2 = ctx.shape[1]
    F = sw1.shape[1]
    NE = rw.shape[1]
    T = NB * S
    NT = T // P
    TB = S // P
    C = D // P
    NP = H // 2
    HD = H * DH
    J = HD // P
    FJ = F // P
    CD = D // H
    HC = P // CD
    KR = K2 - P
    RS = 32
    V1 = CD + 1
    BLK = 256
    TT = BLK // P
    NSH = T // BLK
    MAX_BLOCKS = 2 * T // BLK + NE - 1
    assert DH * 2 == P and TB == 8 and C == 2 and 0 < KR <= RS and HC == 8

    with ExitStack() as stack:
        def sb(name, shape, dt=F32):
            return stack.enter_context(nc.sbuf_tensor(name, shape, dt))

        def sem(name):
            return stack.enter_context(nc.semaphore(name))

        x_sb = sb("x_sb", [P, NT, D])
        xT_hi = sb("xT_hi", [P, C, T], F32R)
        xT_lo = sb("xT_lo", [P, C, T], F32R)
        wo_sb = sb("wo_sb", [P, J, D])
        ctx_diag = sb("ctx_diag", [P, NB, C, HC, K2])
        v_main = sb("v_main", [P, NB, H, V1])
        v_rest = sb("v_rest", [P, NB, H, V1])
        w_outT = sb("w_outT", [P, C, D])
        rw_sb = sb("rw_sb", [P, C, NE])
        ident = sb("ident", [P, P])
        identb = sb("identb", [P, P], BF16)
        causal = sb("causal", [P, P], BF16)
        bias_qkv = sb("bias_qkv", [P, 3, NP])
        bias_now = sb("bias_now", [P, 3])
        bo_b = sb("bo_b", [P, D])
        bout_b = sb("bout_b", [P, D])
        sb2_b = sb("sb2_b", [P, D])
        rb_b = sb("rb_b", [P, NE])
        b1T = sb("b1T", [P, (NE + 1) * FJ])
        mean_var = sb("mean_var", [P, NT, 2])
        stats = sb("stats", [P, NT, 6])
        rstd = sb("rstd", [P, NT])
        power = sb("power", [P, NT])
        logits = sb("logits", [P, NT, NE])
        weight = sb("weight", [P, 2, NT])
        dest = sb("dest", [P, 2, NT], U32)
        block_expert = sb("block_expert", [P, MAX_BLOCKS], I32)
        zero_rows = sb("zero_rows", [P, D])
        head_of = sb("head_of", [P, HC])
        arena = sb("arena", [P, 12288])
        arena_r = sb("arena_r", [P, 13824], F32R)

        place = [0]

        def region(*shape, dt=F32):
            words = int(np.prod(shape))
            a = arena[:, place[0]:place[0] + words]
            place[0] += words
            assert place[0] <= arena.shape[1], place[0]
            if dt is not F32:
                a = a.bitcast(dt)
            names = "abcd"[:len(shape)]
            if len(shape) > 1:
                a = a.rearrange(f"p ({' '.join(names)}) -> p {' '.join(names)}",
                                **{n: s for n, s in zip(names, shape)})
            return a

        place_r = [0]

        def region_r(*shape):
            words = int(np.prod(shape))
            a = arena_r[:, place_r[0]:place_r[0] + words]
            place_r[0] += words
            assert place_r[0] <= arena_r.shape[1], place_r[0]
            names = "abcd"[:len(shape)]
            if len(shape) > 1:
                a = a.rearrange(f"p ({' '.join(names)}) -> p {' '.join(names)}",
                                **{n: s for n, s in zip(names, shape)})
            return a

        xn = [region(D) for _ in range(2)]
        w_pair = region(3, C, P)
        fresh = [region(S // 2) for _ in range(2)]
        o_turn = [region(TB, P) for _ in range(2)]
        v_pair = [region(TB, P) for _ in range(2)]
        ctx_in = region(NB, 2, D)
        bias_in = region(P)
        b1_in = region(P)
        wout_in = region(C, D)
        place[0] -= NB * 2 * D + 2 * P + C * D
        prob = [region(S) for _ in range(2)]
        probT = [region(TB, P) for _ in range(2)]
        neg_max = region(2)
        row_sum = region(2 * TB)
        row_inv = region(2 * TB)
        w_pair_hi, w_pair_lo = region_r(3, C, P), region_r(3, C, P)
        q_parts = [[region_r(S) for _ in range(2)] for _ in range(2)]
        k_hi = [[region_r(S) for _ in range(2)] for _ in range(2)]
        k_lo = [[region_r(S) for _ in range(2)] for _ in range(2)]
        half_rows = [slice(0, DH), slice(DH, P)]
        place[0] = 0
        UH = 4
        NQ = H // UH
        o_tile = [region(HD) for _ in range(2)]
        oT = region(J, P)
        xn2, ln2_sum, ln2_sq, ln2_var, ln2_r = region(D), region(1), region(D), region(1), region(1)
        xn2T = [region(C, P) for _ in range(2)]
        mask_in = [region(K2, dt=I32) for _ in range(2)]
        mask_add = [region(K2 // 2, dt=BF16) for _ in range(2)]
        energy = [region(UH, K2) for _ in range(2)]
        pm = [region(UH, P) for _ in range(2)]
        pr = [region(UH, RS) for _ in range(2)]
        pmT = [region(UH, P) for _ in range(2)]
        prT = [region(P) for _ in range(2)]
        cmax = [region(UH) for _ in range(2)]
        cinv, o2, o2T = region(H), region(D), region(C, P)
        xn3 = [region(D) for _ in range(2)]
        ln3_sum, ln3_sq, ln3_var, ln3_r, xn3T = region(1), region(D), region(1), region(1), region(C, P)
        REST = 320
        place[0] = 0
        w1_raw = region(C, F)
        w2_raw = region(FJ, D)
        h_raw = [region(2, BLK) for _ in range(2)]
        xb = region(TT, D)
        yb = region(TT, D)
        b2_all = region(NE, D)
        x3_rows = region(NT, D)
        place[0] -= NT * D
        y_got = [region(2, D) for _ in range(2)]
        place_r[0] = 0
        w1_hi, w1_lo = region_r(C, F), region_r(C, F)
        w2_hi, w2_lo = region_r(FJ, D), region_r(FJ, D)
        h_hi, h_lo = region_r(FJ, BLK), region_r(FJ, BLK)
        xb_hi, xb_lo = region_r(C, BLK), region_r(C, BLK)

        route = sb("route", [P, 12, NT, NE])
        hot1, hot2, eq, cand, masked, shifted, expd, both, pos, picked, jm8, pos2 = [
            route[:, i] for i in range(12)]
        tile_base = sb("tile_base", [P, NT + 1, NE])
        small = sb("small", [P, 11, NT])
        first_max, first_at, second_max, second_at, gap, gap_exp, total, inv_total, w_sum, w_inv, destf = [
            small[:, i, :] for i in range(11)]
        ne_small = sb("ne_small", [P, 3, NE])
        n_blocks, blocks_incl, expert_base = [ne_small[:, i, :] for i in range(3)]
        block_starts = sb("block_starts", [P, NE, T // BLK])
        block_cmp = sb("block_cmp", [P, NE, T // BLK])
        block_no = sb("block_no", [P, MAX_BLOCKS, NE])
        block_ge = sb("block_ge", [P, MAX_BLOCKS, NE])
        block_f = sb("block_f", [P, MAX_BLOCKS])
        lower = sb("lower", [P, P])
        ones = sb("ones", [P, P])

        xs = nc.dram_tensor("x_sorted", [MAX_BLOCKS * BLK, D], F32, kind="Internal").ap()
        o_dram = nc.dram_tensor("attention_out", [T, HD], F32, kind="Internal").ap()
        x3_dram = nc.dram_tensor("x3", [T, D], F32, kind="Internal").ap()
        ys = nc.dram_tensor("y_sorted", [MAX_BLOCKS * BLK, D], F32, kind="Internal").ap()

        sc = stack.enter_context(nc.psum_tensor("sc", [P, 4 * 512], F32))
        tp = [stack.enter_context(nc.psum_tensor(f"tp{i}", [P, 512], F32)) for i in range(2)]
        acc = [stack.enter_context(nc.psum_tensor(f"acc{i}", [P, 512], F32)) for i in range(2)]

        def pair(name):
            return [sem(name + "_even"), sem(name + "_odd")]

        pool_step, vector_step = sem("pool_step"), sem("vector_step")
        x_in = [sem(f"x_in_{q}") for q in range(4)]
        small_in, w_in, rows_in, rest_in, zeros_ready, xs_zero = [sem(n) for n in (
            "small_in", "w_in", "rows_in", "rest_in", "zeros_ready", "xs_zero")]
        consts_ready, prep_turned, prep_copied = sem("consts_ready"), sem("prep_turned"), sem("prep_copied")
        diag_copied = sem("diag_copied")
        stats_done, rstd_done = sem("stats_done"), sem("rstd_done")
        xn_ready, xn_turned, xT_hi_ready, xT_ready = [sem(n) for n in ("xn_ready", "xn_turned", "xT_hi_ready", "xT_ready")]
        w_hi_ready, w_lo_ready = sem("w_hi_ready"), sem("w_lo_ready")
        o_stored, x3_loaded = sem("o_stored"), sem("x3_loaded")
        w_pair_in, proj_done, fresh_ready, hi_ready, lo_ready, v_turned, v_taken = [sem(n) for n in (
            "w_pair_in", "proj_done", "fresh_ready", "hi_ready", "lo_ready", "v_turned", "v_taken")]
        turned, turned_taken = pair("turned"), pair("turned_taken")
        scores_done, max_done, exp_done, pv_done, o_taken = [sem(n) for n in (
            "scores_done", "max_done", "exp_done", "pv_done", "o_taken")]
        o_staged, mask_staged, x3_stored = pair("o_staged"), pair("mask_staged"), pair("x3_stored")
        mask_ready, first_turned, second_turned, first_taken, second_taken, y_done, y_taken, var2_done, rstd2_done = [
            sem(n) for n in ("mask_ready", "first_turned", "second_turned", "first_taken", "second_taken", "y_done",
                             "y_taken", "var2_done", "rstd2_done")]
        xn2_ready, xn2_turned, xn2_taken = [sem(n) for n in ("xn2_ready", "xn2_turned", "xn2_taken")]
        energy_done, shifted_done, cexp_done, pm_turned, pr_turned, pm_taken, pr_taken, cpv_done = [sem(n) for n in (
            "energy_done", "shifted_done", "cexp_done", "pm_turned", "pr_turned", "pm_taken", "pr_taken", "cpv_done")]
        o2_ready, o2_turned, o2_taken, y2_done, y2_taken, var3_done, rstd3_done = [sem(n) for n in (
            "o2_ready", "o2_turned", "o2_taken", "y2_done", "y2_taken", "var3_done", "rstd3_done")]
        xn3_ready, xn3_turned, xn3_taken, xn3_low, x3_free, logits_done, logits_taken = [sem(n) for n in (
            "xn3_ready", "xn3_turned", "xn3_taken", "xn3_low", "x3_free", "logits_done", "logits_taken")]
        gap_ready, route_exp_done, both_ready, counted, experts_ready, dest_ready, scattered = [sem(n) for n in (
            "gap_ready", "route_exp_done", "both_ready", "counted", "experts_ready", "dest_ready", "scattered")]
        o_free = sem("o_free")
        b2_in, w1_in, w2_in, xb_in = [sem(n) for n in ("b2_in", "w1_in", "w2_in", "xb_in")]
        w1_hi_ready, w1_ready, w2_hi_ready, w2_ready = [sem(n) for n in (
            "w1_hi_ready", "w1_ready", "w2_hi_ready", "w2_ready")]
        xb_turned, xb_hi_ready, xb_ready = [sem(n) for n in ("xb_turned", "xb_hi_ready", "xb_ready")]
        h_done, gelu_done, h_ready, ffn_done, ffn_taken = [sem(n) for n in (
            "h_done", "gelu_done", "h_ready", "ffn_done", "ffn_taken")]
        yb_taken, y_stored, gathered, final_done, out_stored = (
            sem("yb_taken"), sem("y_stored"), pair("gathered"), sem("final_done"), sem("out_stored"))

        xf = x.rearrange("b (t p) d -> p (b t) d", p=P)
        of = out.rearrange("b (t p) d -> p (b t) d", p=P)
        STEPS = 2 * TB
        TURNS = NB * NP
        chunks = [[(s % 2, 0, s // 2 + 1)] if s // 2 < 4 else [(0, 0, 4), (1, 4, s // 2 - 3)] for s in range(STEPS)]
        fills = [[sum(cb == k for r in range(s + 1) for cb, _, _ in chunks[r]) for k in range(2)]
                 for s in range(STEPS)]
        FILLS = fills[-1][0]
        assert fills[-1] == [FILLS, FILLS] and NB == 2
        SLOTS = [("q", 0, 0), ("q", 1, 1), ("k", 0, 2), ("k", 1, 3), ("v", 0, 4), ("turn", 0, 0), ("v", 1, 5), ("turn", 1, 1)]
        UNITS, QK, HALVES = 6, 4, 2
        SLOT_OF = {0: 0, 2: 1, 5: 2, 7: 3, 9: 4, 10: 5, 11: 6, 12: 7}
        SPLIT_AT = 13
        HS = S // 2

        def prelude(tile, slot):
            for t in range(NT):
                tile(t)
                if t >= TB:
                    slot(t - TB)

        stage1_banks = [tp[0], tp[1], acc[0]]

        def attention(turn, loop):
            with loop(0, NP - 1) as p:
                turn(p, 0, True, True)
                turn(p, 1, True, True)
            turn(NP - 1, 0, True, False)
            turn(NP - 1, 1, False, False)


        class Tile:

            def __init__(self, j, n):
                self.j, self.n, self.odd = j, n, n % 2
                self.t, self.half = (n, n // 2) if j is None else (j * 2 + n, j + n // 2)
                self.real = j is not None or 0 <= n < NT

            def __add__(self, k):
                return Tile(self.j, self.n + k)

        def tiles(cycle, loop):
            def peeled(first, end):
                for n in range(first, end):
                    cycle(Tile(None, n), n // TB, (n + 1) // TB)

            def looped(first, end, b):
                with loop(0, (end - first) // 2) as j:
                    for n in (first, first + 1):
                        cycle(Tile(j, n), b, b)
            peeled(-2, 2)
            looped(2, TB - 2, 0)
            peeled(TB - 2, TB)
            looped(TB, NT - 2, 1)
            peeled(NT - 2, NT + 2)

        def after(eng, signal, count):
            if not isinstance(count, int) or count > 0:
                eng.wait_ge(signal, count)

        block = stack.enter_context(nc.Block())

        @block.sync
        def _(sp):
            for q in range(4):
                at = slice(q * NT // 4, (q + 1) * NT // 4)
                sp.dma_start(x_sb[:, at, :], xf[:, at, :]).then_inc(x_in[q], 16)
            for b in range(NB):
                sp.dma_start(ctx_in[:, b, 0, :], ctx[b, 0:P, :]).then_inc(small_in, 16)
                sp.dma_start(ctx_in[0:KR, b, 1, :], ctx[b, P:K2, :]).then_inc(small_in, 16)
            for k, w in enumerate((bq, bk, bv)):
                sp.dma_start(bias_in[k * NP:(k + 1) * NP, :], w.rearrange("(p h) d -> p (h d)", h=2)).then_inc(small_in, 16)
            sp.dma_start(b1_in[0:NE * FJ, :], eb1.rearrange("e (j p) -> (e j) p", p=P)).then_inc(small_in, 16)
            sp.dma_start(b1_in[NE * FJ:(NE + 1) * FJ, :], sb1.rearrange("(j p) -> j p", p=P)).then_inc(small_in, 16)
            sp.dma_start(wout_in, w_out.rearrange("(c p) d -> p c d", p=P)).then_inc(small_in, 16)
            def load_pair(p):
                for k, w in enumerate((wq, wk, wv)):
                    for c in range(C):
                        sp.dma_start(w_pair[:, k, c, :].rearrange("e (h d) -> e h d", h=2),
                                     w[ds(2 * p, 2), c * P:(c + 1) * P, :].rearrange("h e d -> e h d")
                                     ).then_inc(w_pair_in, 16)
            load_pair(0)
            sp.wait_ge(consts_ready, 1)
            for r in range(UH):
                for b in range(NB):
                    sp.dma_start(v_rest[r * RS:r * RS + KR, b, r::UH, 0:CD],
                                 ctx[b, P:K2, :].rearrange("k (h d) -> k h d", d=CD)[:, r::UH, :]).then_inc(rest_in, 16)
            sp.dma_start(wo_sb[:], wo.rearrange("(j p) d -> p j d", p=P)).then_inc(w_in, 16)
            sp.dma_start(rw_sb[:], rw.rearrange("(c p) f -> p c f", p=P)).then_inc(w_in, 16)
            for dst, src in ((bo_b, bo), (bout_b, b_out), (sb2_b, sb2), (rb_b, rb)):
                sp.dma_start(dst[:], src.partition_broadcast(P)).then_inc(rows_in, 16)
            for n in range(MAX_BLOCKS * TT):
                sp.dma_start(xs[n * P:(n + 1) * P, :], zero_rows[:]).then_inc(xs_zero, 16)
            with sp.Fori(0, NP - 1) as p:
                sp.wait_ge(w_lo_ready, p + 1)
                load_pair(p + 1)
            sp.wait_ge(o_taken, TURNS * STEPS + FREE)
            sp.wait_ge(o_stored, TURNS * TB * 16)
            with sp.Fori(0, NB) as b:
                with sp.Fori(0, TB // 2) as j:
                    jj = b * (TB // 2) + j
                    for u in range(2):
                        t = jj * 2 + u
                        sp.wait_ge(first_turned, t - 1 + FREE_2)
                        sp.dma_start(o_tile[u], o_dram[ds(t * P, P), :]).then_inc(o_staged[u], 16)
                        sp.wait_ge(mask_ready, t - 1 + FREE_2)
                        sp.dma_start(mask_in[u], mask[ds(b, 1), 0, ds((j * 2 + u) * P, P), :]
                                     .rearrange("a p k -> (a p) k")).then_inc(mask_staged[u], 16)
            sp.wait_ge(logits_taken, NT)
            for u in range(2):
                sp.wait_ge(x3_stored[u], 16 * (NT // 2))
            sp.dma_start(w1_raw, sw1.rearrange("(c p) f -> p c f", p=P)).then_inc(w1_in, 16)
            sp.dma_start(w2_raw, sw2.rearrange("(c p) f -> p c f", p=P)).then_inc(w2_in, 16)
            sp.dma_start(x3_rows, x3_dram.rearrange("(t p) d -> p t d", p=P)).then_inc(x3_loaded, 16)
            sp.dma_start(b2_all, eb2.rearrange("e d -> (e d)").partition_broadcast(P)
                         .rearrange("p (e d) -> p e d", d=D)).then_inc(b2_in, 16)
            sp.wait_ge(experts_ready, 1)
            with sp.Fori(0, MAX_BLOCKS) as n:
                e = sp.value_load(block_expert[0:1, ds(n, 1)], min_val=0, max_val=NE - 1)
                sp.wait_ge(w1_ready, n * 2 + 2)
                sp.dma_start(w1_raw, ew1[ds(e, 1)].rearrange("a (c p) f -> p (a c) f", p=P)).then_inc(w1_in, 16)
                sp.wait_ge(scattered, 16 * 2 * NT)
                sp.wait_ge(xb_turned, n + FREE)
                sp.dma_start(xb, xs[ds(n * BLK, BLK), :].rearrange("(t p) d -> p t d", p=P)).then_inc(xb_in, 16)
                sp.wait_ge(w2_ready, n * 4 + 4)
                sp.dma_start(w2_raw, ew2[ds(e, 1)].rearrange("a (c p) f -> p (a c) f", p=P)).then_inc(w2_in, 16)
            with sp.Fori(0, NT) as t:
                sp.wait_ge(final_done, t + 1)
                sp.dma_start(of[:, ds(t, 1), :], x_sb[:, ds(t, 1), :]).then_inc(out_stored, 16)
            sp.wait_ge(out_stored, 16 * NT)

        @block.gpsimd
        def _(pool):
            step = Chain(pool, pool_step)
            pool.sem_inc(x3_free, FREE)
            pool.sem_inc(o_free, FREE_2)
            step(pool.memset(ident[:], 0.0))
            step(pool.affine_select(out=ident[:], in_=ident[:], compare_op=ALU.not_equal, fill=1.0, base=0,
                                    pattern=[[-1, P]], channel_multiplier=1))
            step(pool.tensor_copy(identb[:], ident[:]))
            step(pool.memset(causal[:], 0.0))
            step(pool.affine_select(out=causal[:], in_=causal[:], compare_op=ALU.is_ge, fill=MASKED, base=0,
                                    pattern=[[-1, P]], channel_multiplier=1))
            step(pool.memset(ones[:], 1.0))
            step(pool.affine_select(out=lower[:], in_=ones[:], compare_op=ALU.is_gt, fill=0.0, base=0,
                                    pattern=[[1, P]], channel_multiplier=-1))
            step(pool.affine_select(out=head_of[:], in_=ones[:, 0:HC], compare_op=ALU.is_ge, fill=0.0, base=0,
                                    pattern=[[-CD, HC]], channel_multiplier=1))
            step(pool.affine_select(out=head_of[:], in_=head_of[:], compare_op=ALU.is_ge, fill=0.0, base=CD - 1,
                                    pattern=[[CD, HC]], channel_multiplier=-1))
            step(pool.memset(power[:], -0.5))
            step(pool.memset(v_rest[:], 0.0))
            step(pool.memset(v_main[:], 1.0))
            step(pool.memset(tile_base[:, 0, :], 0.0))
            for r in range(UH):
                step(pool.memset(v_rest[r * RS:r * RS + KR, :, r::UH, CD:V1], 1.0))
            step(pool.iota(jm8, [[0, NT], [1, NE]], base=-NE, channel_multiplier=0,
                           allow_small_or_imprecise_dtypes=True))
            step(pool.iota(block_starts[:], [[0, NE], [BLK, T // BLK]], base=0, channel_multiplier=0,
                           allow_small_or_imprecise_dtypes=True))
            step(pool.iota(block_no[:], [[1, MAX_BLOCKS], [0, NE]], base=0, channel_multiplier=0,
                           allow_small_or_imprecise_dtypes=True))
            pool.memset(zero_rows[:], 0.0).then_inc(consts_ready, 1)
            pool.wait_ge(consts_ready, 1)
            pool.wait_ge(stats_done, 1)
            step(pool.tensor_scalar(rstd[:], mean_var[:, :, 1], EPS, None, ALU.add))
            pool.tensor_tensor(rstd[:], rstd[:], power[:], ALU.pow).then_inc(rstd_done, 1)
            def weights_low(p):
                pool.wait_ge(w_hi_ready, p + 1)
                pool.tensor_tensor(w_pair_lo, w_pair, w_pair_hi.bitcast(F32), ALU.subtract).then_inc(w_lo_ready, 1)

            def low_parts(t, b, slot):
                what, half, k = SLOTS[slot]
                at = slice(half * HS, (half + 1) * HS)
                if what in "qk":
                    if not isinstance(t, int) or t * QK + k > 0:
                        pool.wait_ge(lo_ready, t * QK + k)
                    pool.wait_ge(hi_ready, t * QK + k + 1)
                if what == "q":
                    for h in range(2):
                        own, other = half_rows[h], half_rows[1 - h]
                        i = pool.tensor_tensor(q_parts[b][h][other, at], fresh[k % 2][own, :],
                                               q_parts[b][h][own, at].bitcast(F32), ALU.subtract)
                    i.then_inc(lo_ready, 1)
                if what == "k":
                    for h in range(2):
                        own = half_rows[h]
                        for rows in half_rows:
                            i = pool.tensor_tensor(k_lo[b][h][rows, at], fresh[k % 2][own, :],
                                                   k_hi[b][h][own, at].bitcast(F32), ALU.subtract)
                    i.then_inc(lo_ready, 1)

            def turn(p, b, next_turn, next_pair):
                it = p * NB + b
                for s in range(STEPS):
                    if next_turn and s == 0:
                        pool.wait_ge(w_lo_ready, p + b + 1)
                    if next_turn and s in SLOT_OF:
                        low_parts(it + 1, 1 - b, SLOT_OF[s])
                    if s == SPLIT_AT and next_pair and b == 0:
                        pool.wait_ge(lo_ready, (it + 2) * QK)
                        weights_low(p + 1)
                    if s % 2:
                        pool.wait_ge(o_taken, it * STEPS + s + 1 + FREE)
                        pool.dma_start(o_dram[b * S + s // 2 * P:b * S + (s // 2 + 1) * P, ds(p * P, P)],
                                       o_turn[b][:, s // 2, :]).then_inc(o_stored, 16)
                pool.wait_ge(o_stored, (it + 1) * (TB * 16))
                pool.sem_inc(o_free, 1)
            weights_low(0)
            pool.wait_ge(w_lo_ready, 1)
            for slot in range(len(SLOTS)):
                low_parts(0, 0, slot)
            attention(turn, pool.Fori)
            pool.wait_ge(lo_ready, TURNS * QK)
            pool.wait_ge(o_taken, TURNS * STEPS + FREE)
            for u in range(2):
                step(pool.memset(pr[u], 0.0))
            pool.sem_inc(zeros_ready, 1)
            def cycle(tile, b, b_next):
                last, ahead = tile + -1, tile + 2
                if last.real:
                    pool.wait_ge(var3_done, last.t + 1)
                    pool.tensor_tensor(ln3_r, ln3_var, power[:, 0:1], ALU.pow).then_inc(rstd3_done, 1)
                    pool.wait_ge(xn3_ready, last.t + 1)
                    pool.dma_start(x3_dram[ds(last.t * P, P), :], xn3[last.odd]).then_inc(x3_stored[last.odd], 16)
                if ahead.real:
                    pool.wait_ge(var2_done, ahead.t + 1)
                    pool.tensor_tensor(ln2_r, ln2_var, power[:, 0:1], ALU.pow).then_inc(rstd2_done, 1)
                if last.real:
                    pool.wait_ge(x3_stored[last.odd], last.half * 16 + 16)
                    pool.sem_inc(x3_free, 1)
            tiles(cycle, pool.Fori)
            def w2_low(idx):
                for q in range(4):
                    pool.wait_ge(w2_hi_ready, idx * 4 + q + 1)
                    at = slice(q * FJ // 4, (q + 1) * FJ // 4)
                    pool.tensor_tensor(w2_lo[:, at, :], w2_raw[:, at, :], w2_hi[:, at, :].bitcast(F32), ALU.subtract
                                       ).then_inc(w2_ready, 1)
            w2_low(0)
            pool.wait_ge(dest_ready, 2)
            pool.wait_ge(x3_loaded, 16)
            pool.wait_ge(xs_zero, 16 * MAX_BLOCKS * TT)
            for t in range(NT):
                for k in range(2):
                    pool.indirect_dma_start(xs, bass.IndirectOffsetOnAxis(ap=dest[:, k, t:t + 1], axis=0),
                                            x3_rows[:, t, :], None).then_inc(scattered, 16)
            with pool.Fori(0, MAX_BLOCKS) as n:
                w2_low(n + 1)
            pool.wait_ge(y_stored, 16 * MAX_BLOCKS + 16 * FREE)
            for t in range(NT):
                if t >= 2:
                    pool.wait_ge(final_done, t - 1)
                for k in range(2):
                    pool.indirect_dma_start(y_got[k][:, t % 2, :], None, ys,
                                            bass.IndirectOffsetOnAxis(ap=dest[:, k, t:t + 1], axis=0)
                                            ).then_inc(gathered[t % 2], 16)

        @block.vector
        def _(v):
            step = Chain(v, vector_step)
            for signal in (ffn_taken, o_taken, turned_taken[0]):
                v.sem_inc(signal, FREE)
            for signal in (h_ready, mask_ready):
                v.sem_inc(signal, FREE_2)
            for t in range(NT):
                if t % (NT // 4) == 0:
                    v.wait_ge(x_in[t // (NT // 4)], 16)
                st = v.bn_stats(stats[:, t, :], x_sb[:, t, :])
            step(st)
            for t in range(NT):
                ag = v.bn_aggr(mean_var[:, t, :], stats[:, t, :])
            ag.then_inc(stats_done, 1)
            v.wait_ge(prep_turned, 1)
            v.wait_ge(consts_ready, 1)
            v.tensor_scalar(bias_qkv[:, 0, :], sc[:, 1536:1536 + NP], DH ** -0.5, None, ALU.mult)
            step(v.tensor_copy(bias_qkv[:, 1:3, :].rearrange("p a b -> p (a b)"), sc[:, 1536 + NP:1536 + 3 * NP]))
            v.tensor_copy(bias_now[:], bias_qkv[:, :, 0])
            v.tensor_copy(b1T[:], sc[:, 1536 + P:1536 + P + (NE + 1) * FJ]).then_inc(prep_copied, 1)
            for c in range(C):
                for h in range(HC):
                    i = v.tensor_scalar(ctx_diag[:, 1, c, h, :], sc[:, 512 + c * K2:512 + (c + 1) * K2],
                                        head_of[:, h:h + 1], None, ALU.mult)
            i.then_inc(diag_copied, 1)

            def low_part(t, bank):
                at = ds(t * P, P)
                return v.tensor_tensor(xT_lo[:, :, at], bank[:, 0:D].rearrange("p (c t) -> p c t", c=C),
                                       xT_hi[:, :, at].bitcast(F32), ALU.subtract)

            def normalize(t):
                if t < NT:
                    if t >= 2:
                        v.wait_ge(xn_turned, t - 1)
                    v.tensor_scalar(xn[t % 2], x_sb[:, t, :], mean_var[:, t, 0:1], rstd[:, t:t + 1],
                                    ALU.subtract, ALU.mult).then_inc(xn_ready, 1)

            def stage1_tile(t):
                normalize(t + 2)
                v.wait_ge(xT_hi_ready, t + 1)
                low_part(t, stage1_banks[t % 3]).then_inc(xT_ready, 1)

            def high_parts(t, b, slot):
                what, half, k = SLOTS[slot]
                at = slice(half * HS, (half + 1) * HS)
                if what in "qk":
                    v.wait_ge(fresh_ready, t * UNITS + k + 1)
                if what == "q":
                    for h in range(2):
                        i = v.tensor_copy(q_parts[b][h][half_rows[h], at], fresh[k % 2][half_rows[h], :])
                    i.then_inc(hi_ready, 1)
                if what == "k":
                    for h in range(2):
                        for rows in half_rows:
                            i = v.tensor_copy(k_hi[b][h][rows, at], fresh[k % 2][half_rows[h], :])
                    i.then_inc(hi_ready, 1)
                if what == "turn":
                    v.wait_ge(v_turned, t * HALVES + k + 1)
                    v.tensor_copy(v_pair[b][:, half * 4:half * 4 + 4, :].rearrange("p a b -> p (a b)"), acc[1][:]
                                  ).then_inc(v_taken, 1)

            def row_max(it, s):
                n = (s // 2 + 1) * P
                v.wait_ge(scores_done, it * STEPS + s + 1)
                v.tensor_reduce(neg_max[:, s % 2:s % 2 + 1], sc[:, (s % 2) * 1024:(s % 2) * 1024 + n], AX.X, ALU.max,
                                negate=True).then_inc(max_done, 1)

            def turn(p, b, next_turn, next_pair):
                it = p * NB + b
                if next_turn:
                    v.tensor_copy(bias_now[:].unsqueeze(2), bias_qkv[:, :, ds(p + b, 1)])
                for s in range(STEPS):
                    for k, t0, m in chunks[s]:
                        if k == 0:
                            v.wait_ge(turned[0], it * FILLS + fills[s][0])
                            v.tensor_copy(probT[s % 2][:, t0:t0 + m, :].rearrange("p a b -> p (a b)"),
                                          tp[0][:, 0:m * P]).then_inc(turned_taken[0], 1)
                    if s + 2 < STEPS:
                        row_max(it, s + 2)
                    elif next_turn:
                        row_max(it + 1, s + 2 - STEPS)
                    if next_turn and s - 1 in SLOT_OF:
                        high_parts(it + 1, 1 - b, SLOT_OF[s - 1])
                    v.wait_ge(exp_done, it * STEPS + s + 1)
                    step(v.reciprocal(row_inv[:, s:s + 1], row_sum[:, s:s + 1]))
                    v.wait_ge(pv_done, it * STEPS + s + 1)
                    if s == 0:
                        v.wait_ge(o_free, it + FREE_2 - 1)
                    v.tensor_scalar(o_turn[b][:, s // 2, (s % 2) * DH:(s % 2 + 1) * DH],
                                    acc[0][:, 0:DH], row_inv[:, s:s + 1], None, ALU.mult).then_inc(o_taken, 1)

            v.wait_ge(rstd_done, 1)
            normalize(0)
            normalize(1)
            prelude(stage1_tile, lambda slot: high_parts(0, 0, slot))
            for b in range(NB):
                v.tensor_copy(v_main[:, b, :, 0:CD], ctx_in[:, b, 0, :].rearrange("p (h d) -> p h d", d=CD))
            v.sem_inc(diag_copied, 1)
            row_max(0, 0)
            row_max(0, 1)

            @contextmanager
            def counted_loop(first, end):
                with v.Fori(first, end) as p:
                    step.loop(p, NB * STEPS)
                    yield p
                step.end(end - first)
            attention(turn, counted_loop)

            def x_tile(t):
                return x_sb[:, ds(t, 1), :].rearrange("p a d -> p (a d)")

            def residual(t, add, row, taken, rows, total, square, var):
                v.tensor_tensor(x_tile(t), add, x_tile(t), ALU.add).then_inc(taken, 1)
                v.wait_ge(taken, t + 1)
                step(v.scalar_tensor_tensor(x_tile(t), x_tile(t), 1.0, row, ALU.mult, ALU.add, accum_out=total))
                step(v.tensor_scalar(total, total, -1.0 / D, None, ALU.mult))
                step(v.tensor_scalar(rows, x_tile(t), total, None, ALU.add))
                step(v.tensor_tensor_reduce(square, rows, rows, 1.0, 0.0, ALU.mult, ALU.add, var))
                return v.tensor_scalar(var, var, 1.0 / D, EPS, ALU.mult, ALU.add)

            def shift(tile, q):
                u = q % 2
                v.wait_ge(energy_done, tile.t * NQ + q + 1)
                e = sc[:, u * 1024:(u + 1) * 1024].rearrange("p (a n) -> p a n", a=2)[:, :, 0:2 * K2] \
                    .rearrange("p a (h k) -> p a h k", h=2)
                step(v.tensor_reduce(cmax[u].rearrange("p (a h) -> p a h", a=2), e, AX.X, ALU.max))
                for a in range(2):
                    i = v.tensor_tensor(energy[u][:, 2 * a:2 * a + 2, :], e[:, a],
                                        cmax[u][:, 2 * a:2 * a + 2].unsqueeze(2).to_broadcast([P, 2, K2]),
                                        ALU.subtract)
                i.then_inc(shifted_done, 1)

            def cycle(tile, b, b_next):
                before, last, near, ahead = tile + -2, tile + -1, tile + 1, tile + 2
                for q in range(NQ):
                    if q == 0 and last.real:
                        v.wait_ge(cpv_done, tile.t * NQ)
                        sums = acc[0][:, 0:H * V1].rearrange("p (h d) -> p h d", d=V1)
                        step(v.reciprocal(cinv, sums[:, :, CD]))
                        v.tensor_tensor(o2.rearrange("p (h d) -> p h d", d=CD), sums[:, :, 0:CD],
                                        cinv.unsqueeze(2).to_broadcast([P, H, CD]), ALU.mult).then_inc(o2_ready, 1)
                    if tile.real:
                        v.wait_ge(pr_turned, tile.t * NQ + q + 1)
                        v.tensor_copy(prT[q % 2], acc[0][:, REST:REST + P]).then_inc(pr_taken, 1)
                    of_unit = tile if q < 2 else near
                    if of_unit.real:
                        shift(of_unit, (q + 2) % NQ)
                    if q == 0:
                        if near.real:
                            v.wait_ge(mask_staged[near.odd], near.half * 16 + 16)
                            after(v, energy_done, tile.t * NQ)
                            v.tensor_scalar(mask_add[near.odd], mask_in[near.odd], 0.0, CROSS_MASKED,
                                            ALU.is_equal, ALU.mult).then_inc(mask_ready, 1)
                            v.wait_ge(rstd2_done, near.t + 1)
                            v.tensor_scalar(xn2, xn2, ln2_r, None, ALU.mult).then_inc(xn2_ready, 1)
                        if before.real:
                            v.wait_ge(logits_done, before.t + 1)
                            v.tensor_tensor(logits[:, ds(before.t, 1), :].rearrange("p a d -> p (a d)"),
                                            acc[1][:, 0:NE], rb_b[:], ALU.add).then_inc(logits_taken, 1)
                    elif q == 1 and last.real:
                        v.wait_ge(y2_done, last.t + 1)
                        after(v, x3_free, last.t - 1 + FREE)
                        residual(last.t, acc[1][:, 0:D], bout_b[:], y2_taken, xn3[last.odd], ln3_sum, ln3_sq, ln3_var
                                 ).then_inc(var3_done, 1)
                    elif q == 2:
                        if ahead.real:
                            v.wait_ge(first_turned, ahead.t + 1 + FREE_2)
                            v.tensor_copy(oT[:, 0:4, :].rearrange("p a b -> p (a b)"), acc[1][:]).then_inc(first_taken, 1)
                        if last.real:
                            v.wait_ge(rstd3_done, last.t + 1)
                            v.tensor_scalar(xn3[last.odd], xn3[last.odd], ln3_r, None, ALU.mult).then_inc(xn3_ready, 1)
                    elif q == 3:
                        if last.real:
                            v.wait_ge(xn3_taken, last.t + 1)
                            low_part(last.t, tp[1]).then_inc(xn3_low, 1)
                        if ahead.real:
                            v.wait_ge(y_done, ahead.t + 1)
                            after(v, xn2_turned, ahead.t)
                            residual(ahead.t, acc[1][:, 0:D], bo_b[:], y_taken, xn2, ln2_sum, ln2_sq, ln2_var
                                     ).then_inc(var2_done, 1)

            @contextmanager
            def counted_tiles(first, end):
                with v.Fori(first, end) as j:
                    step.loop(j, 2 * (1 + NQ + 4 + 4))
                    yield j
                step.end(end - first)
            v.wait_ge(rows_in, 64)
            tiles(cycle, counted_tiles)

            v.wait_ge(logits_taken, NT)

            def over_experts(a):
                return a.unsqueeze(2).to_broadcast([P, NT, NE])

            def top(src, best, at, hot):
                step(v.tensor_reduce(best, src, AX.X, ALU.max))
                step(v.tensor_tensor(eq, src, over_experts(best), ALU.is_equal))
                step(v.tensor_tensor(cand, eq, jm8, ALU.mult))
                step(v.tensor_reduce(at, cand, AX.X, ALU.min))
                step(v.tensor_tensor(hot, jm8, over_experts(at), ALU.is_equal))
            top(logits[:], first_max, first_at, hot1)
            step(v.scalar_tensor_tensor(masked, hot1, -3e38, logits[:], ALU.mult, ALU.add))
            top(masked, second_max, second_at, hot2)
            v.tensor_tensor(both, hot1, hot2, ALU.add).then_inc(both_ready, 1)
            v.tensor_tensor(gap, second_max, first_max, ALU.subtract)
            v.tensor_tensor(shifted, logits[:], over_experts(first_max), ALU.subtract).then_inc(gap_ready, 1)
            v.wait_ge(counted, 1)
            for t in range(NT):
                step(v.tensor_tensor(tile_base[:, t + 1, :], tile_base[:, t, :], acc[1][:, t * NE:(t + 1) * NE], ALU.add))
            step(v.tensor_tensor(block_cmp[:], tile_base[:, NT, :].unsqueeze(2).to_broadcast([P, NE, T // BLK]),
                                 block_starts[:], ALU.is_gt))
            step(v.tensor_reduce(n_blocks, block_cmp[:], AX.X, ALU.add))
            step(v.tensor_copy(blocks_incl, n_blocks))
            for e in range(1, NE):
                step(v.tensor_tensor(blocks_incl[:, e:e + 1], blocks_incl[:, e - 1:e], n_blocks[:, e:e + 1], ALU.add))
            step(v.tensor_tensor(block_ge[:], blocks_incl.unsqueeze(1).to_broadcast([P, MAX_BLOCKS, NE]),
                                 block_no[:], ALU.is_le))
            step(v.tensor_reduce(block_f[:], block_ge[:], AX.X, ALU.add))
            v.tensor_scalar(block_expert[:], block_f[:], float(NE - 1), None, ALU.min).then_inc(experts_ready, 1)
            step(v.tensor_tensor(expert_base, blocks_incl, n_blocks, ALU.subtract))
            step(v.tensor_scalar(expert_base, expert_base, float(BLK), None, ALU.mult))
            step(v.tensor_tensor(pos, acc[0][:, 0:NT * NE].rearrange("p (t e) -> p t e", e=NE), tile_base[:, 0:NT, :], ALU.add))
            step(v.tensor_tensor(pos2, pos, expert_base.unsqueeze(1).to_broadcast([P, NT, NE]), ALU.add))
            for k, hot in enumerate((hot1, hot2)):
                step(v.tensor_tensor(picked, hot, pos2, ALU.mult))
                step(v.tensor_reduce(destf, picked, AX.X, ALU.add))
                step(v.tensor_copy(dest[:, k, :], destf))
            v.sem_inc(dest_ready, 2)
            v.wait_ge(route_exp_done, 1)
            step(v.tensor_reduce(total, expd, AX.X, ALU.add))
            step(v.reciprocal(inv_total, total))
            step(v.tensor_tensor(gap_exp, gap_exp, inv_total, ALU.mult))
            step(v.tensor_tensor(w_sum, inv_total, gap_exp, ALU.add))
            step(v.tensor_scalar(w_sum, w_sum, 1e-9, None, ALU.add))
            step(v.reciprocal(w_inv, w_sum))
            step(v.tensor_tensor(weight[:, 0, :], inv_total, w_inv, ALU.mult))
            step(v.tensor_tensor(weight[:, 1, :], gap_exp, w_inv, ALU.mult))

            def hidden_parts(m):
                for k in range(FJ // 2):
                    at = slice(2 * k, 2 * k + 2)
                    v.wait_ge(gelu_done, m * (FJ // 2) + k + 1)
                    if k == 0:
                        v.wait_ge(ffn_done, m + FREE)
                    step(v.tensor_copy(h_hi[:, at, :], h_raw[k % 2]))
                    v.tensor_tensor(h_lo[:, at, :], h_raw[k % 2], h_hi[:, at, :].bitcast(F32), ALU.subtract
                                    ).then_inc(h_ready, 1)

            def w1_low(idx):
                for q in range(2):
                    v.wait_ge(w1_hi_ready, idx * 2 + q + 1)
                    at = slice(q * F // 2, (q + 1) * F // 2)
                    v.tensor_tensor(w1_lo[:, :, at], w1_raw[:, :, at], w1_hi[:, :, at].bitcast(F32), ALU.subtract
                                    ).then_inc(w1_ready, 1)

            def next_block(n):
                v.wait_ge(xb_hi_ready, n + 1)
                v.tensor_tensor(xb_lo.rearrange("p a b -> p (a b)"), tp[0][:], xb_hi.rearrange("p a b -> p (a b)").bitcast(F32),
                                ALU.subtract).then_inc(xb_ready, 1)
                w1_low(n + 1)

            def shared_block(m, last):
                hidden_parts(m)
                if last:
                    next_block(0)
                v.wait_ge(ffn_done, m + 1 + FREE)
                for tt in range(TT):
                    step(v.tensor_tensor(x_tile(m * TT + tt), acc[tt][:, 0:D], x_tile(m * TT + tt), ALU.add))
                for tt in range(TT):
                    step(v.tensor_tensor(x_tile(m * TT + tt), x_tile(m * TT + tt), sb2_b[:], ALU.add))
                v.sem_inc(ffn_taken, 1)

            def expert_block(n, last):
                hidden_parts(n + NSH)
                if not last:
                    next_block(n + 1)
                e = v.value_load(block_expert[0:1, ds(n, 1)], min_val=0, max_val=NE - 1)
                v.wait_ge(ffn_done, n + (NSH + 1 + FREE))
                v.wait_ge(y_stored, n * 16 + 16 * FREE)
                for tt in range(TT):
                    y = v.tensor_tensor(yb[:, tt, :], acc[tt][:, 0:D], b2_all[:, ds(e, 1), :].rearrange("p a d -> p (a d)"),
                                        ALU.add)
                y.then_inc(yb_taken, 1)
                v.sem_inc(ffn_taken, 1)

            w1_low(0)
            with v.Fori(0, NSH - 1) as m:
                step.loop(m, FJ // 2 + 2 * TT)
                shared_block(m, False)
            step.end(NSH - 1)
            shared_block(NSH - 1, True)
            v.wait_ge(b2_in, 16)
            with v.Fori(0, MAX_BLOCKS - 1) as n:
                step.loop(n, FJ // 2)
                expert_block(n, False)
            step.end(MAX_BLOCKS - 1)
            expert_block(MAX_BLOCKS - 1, True)
            for t in range(NT):
                v.wait_ge(gathered[t % 2], (t // 2 + 1) * 32)
                step(v.scalar_tensor_tensor(x_sb[:, t, :], y_got[0][:, t % 2, :], weight[:, 0, t:t + 1],
                                            x_sb[:, t, :], ALU.mult, ALU.add))
                v.scalar_tensor_tensor(x_sb[:, t, :], y_got[1][:, t % 2, :], weight[:, 1, t:t + 1],
                                       x_sb[:, t, :], ALU.mult, ALU.add).then_inc(final_done, 1)

        @block.scalar
        def _(act):
            act.sem_inc(y_stored, 16 * FREE)
            act.sem_inc(turned_taken[1], FREE)
            act.wait_ge(prep_turned, 1)
            act.wait_ge(consts_ready, 1)
            act.activation(w_outT[:].rearrange("p c d -> p (c d)"), sc[:, 1024:1536], ACT.Copy)
            for c in range(C):
                for h in range(HC):
                    i = act.activation(ctx_diag[:, 0, c, h, :], sc[:, c * K2:(c + 1) * K2], ACT.Copy, scale=head_of[:, h:h + 1])
            i.then_inc(diag_copied, 1)

            def stage1_tile(t):
                act.wait_ge(xn_turned, t + 1)
                act.activation(xT_hi[:, :, t * P:(t + 1) * P], stage1_banks[t % 3][:, 0:D].rearrange("p (c t) -> p c t", c=C),
                               ACT.Copy).then_inc(xT_hi_ready, 1)

            def weights_high(p):
                act.wait_ge(w_pair_in, p * (16 * 3 * C) + 16 * 3 * C)
                act.activation(w_pair_hi, w_pair, ACT.Copy).then_inc(w_hi_ready, 1)

            def take_projection(t, b, slot):
                what, half, k = SLOTS[slot]
                if what == "turn":
                    return
                if k >= 2:
                    act.wait_ge(lo_ready, t * QK + k - 1)
                elif not isinstance(t, int) or t > 0:
                    act.wait_ge(v_turned, t * HALVES + k - 1)
                act.wait_ge(proj_done, t * UNITS + k + 1)
                kind = "qkv".index(what)
                act.activation(fresh[k % 2], acc[1][:], ACT.Identity, bias=bias_now[:, kind:kind + 1],
                               scale=DH ** -0.5 if what == "q" else 1.0).then_inc(fresh_ready, 1)

            def softmax(it, s):
                n = (s // 2 + 1) * P
                act.wait_ge(max_done, it * STEPS + s + 1)
                act.activation(prob[s % 2][:, 0:n], sc[:, (s % 2) * 1024:(s % 2) * 1024 + n], ACT.Exp,
                               bias=neg_max[:, s % 2:s % 2 + 1], accum_out=row_sum[:, s:s + 1]).then_inc(exp_done, 1)

            def turn(p, b, next_turn, next_pair):
                it = p * NB + b
                for s in range(STEPS):
                    for k, t0, m in chunks[s]:
                        if k == 1:
                            act.wait_ge(turned[1], it * FILLS + fills[s][1])
                            act.activation(probT[s % 2][:, t0:t0 + m, :].rearrange("p a b -> p (a b)"),
                                           tp[1][:, 0:m * P], ACT.Copy).then_inc(turned_taken[1], 1)
                    if s + 2 < STEPS:
                        softmax(it, s + 2)
                    elif next_turn:
                        softmax(it + 1, s + 2 - STEPS)
                    if next_turn and s in SLOT_OF:
                        take_projection(it + 1, 1 - b, SLOT_OF[s])
                    if s == SPLIT_AT and next_pair and b == 0:
                        act.wait_ge(proj_done, (it + 2) * UNITS)
                        weights_high(p + 1)

            weights_high(0)
            act.wait_ge(prep_copied, 1)
            prelude(stage1_tile, lambda slot: take_projection(0, 0, slot))
            softmax(0, 0)
            softmax(0, 1)
            attention(turn, act.Fori)
            act.wait_ge(zeros_ready, 1)
            def cross_exp(tile, q):
                u = q % 2
                act.wait_ge(shifted_done, tile.t * NQ + q + 1)
                act.activation(pm[u], energy[u][:, :, 0:P], ACT.Exp, scale=CD ** -0.5)
                act.activation(pr[u][:, :, 0:KR], energy[u][:, :, P:K2], ACT.Exp, scale=CD ** -0.5).then_inc(cexp_done, 1)

            def cycle(tile, b, b_next):
                last, near, ahead = tile + -1, tile + 1, tile + 2
                rows_turned = tp[1][:, 0:D].rearrange("p (c t) -> p c t", c=C)
                for q in range(NQ):
                    if tile.real:
                        act.wait_ge(pm_turned, tile.t * NQ + q + 1)
                        act.activation(pmT[q % 2].rearrange("p a b -> p (a b)"), tp[0][:], ACT.Copy).then_inc(pm_taken, 1)
                    if q == 0 and last.real:
                        act.wait_ge(o2_turned, last.t + 1)
                        act.activation(o2T, rows_turned, ACT.Copy).then_inc(o2_taken, 1)
                    elif q == 1 and near.real:
                        act.wait_ge(xn2_turned, near.t + 1)
                        act.activation(xn2T[near.odd], rows_turned, ACT.Copy).then_inc(xn2_taken, 1)
                    elif q == 2 and ahead.real:
                        act.wait_ge(second_turned, ahead.t + 1)
                        act.activation(oT[:, 4:8, :].rearrange("p a b -> p (a b)"), tp[1][:], ACT.Copy
                                       ).then_inc(second_taken, 1)
                    elif q == 3 and last.real:
                        act.wait_ge(xn3_turned, last.t + 1)
                        act.activation(xn3T, rows_turned, ACT.Copy)
                        act.activation(xT_hi[:, :, ds(last.t * P, P)], rows_turned, ACT.Copy).then_inc(xn3_taken, 1)
                    of_unit = tile if q < 2 else near
                    if of_unit.real:
                        cross_exp(of_unit, (q + 2) % NQ)
            tiles(cycle, act.Fori)
            act.wait_ge(gap_ready, 1)
            act.activation(gap_exp, gap, ACT.Exp)
            act.activation(expd, shifted, ACT.Exp).then_inc(route_exp_done, 1)
            def w1_high(idx):
                act.wait_ge(w1_in, idx * 16 + 16)
                for q in range(2):
                    at = slice(q * F // 2, (q + 1) * F // 2)
                    act.activation(w1_hi[:, :, at], w1_raw[:, :, at], ACT.Copy).then_inc(w1_hi_ready, 1)

            def w2_high(q):
                at = slice(q * FJ // 4, (q + 1) * FJ // 4)
                act.activation(w2_hi[:, at, :], w2_raw[:, at, :], ACT.Copy).then_inc(w2_hi_ready, 1)

            def hidden(m, first_bias, w2_idx):
                for k in range(FJ // 2):
                    act.wait_ge(h_done, m * (FJ // 2) + k + 1)
                    act.wait_ge(h_ready, m * (FJ // 2) + k + FREE_2 - 1)
                    for i in range(2):
                        y = act.activation(h_raw[k % 2][:, i, :], sc[:, k * 512 + i * BLK:k * 512 + (i + 1) * BLK], ACT.Gelu,
                                           bias=b1T[:, ds(first_bias + 2 * k + i, 1)])
                    y.then_inc(gelu_done, 1)
                    if w2_idx is not None:
                        if k == 0:
                            act.wait_ge(w2_in, w2_idx * 16 + 16)
                        w2_high(k)

            def next_block(n):
                act.wait_ge(xb_turned, n + 1 + FREE)
                act.activation(xb_hi.rearrange("p a b -> p (a b)"), tp[0][:], ACT.Copy).then_inc(xb_hi_ready, 1)
                w1_high(n + 1)

            def expert_block(n, last):
                e = act.value_load(block_expert[0:1, ds(n, 1)], min_val=0, max_val=NE - 1)
                hidden(n + NSH, e * FJ, n + 1)
                if not last:
                    next_block(n + 1)
                act.wait_ge(yb_taken, n + 1)
                act.dma_start(ys[ds(n * BLK, BLK), :].rearrange("(t p) d -> p t d", p=P), yb).then_inc(y_stored, 16)

            w1_high(0)
            act.wait_ge(w2_in, 16)
            for q in range(4):
                w2_high(q)
            with act.Fori(0, NSH - 1) as m:
                hidden(m, NE * FJ, None)
            hidden(NSH - 1, NE * FJ, None)
            next_block(0)
            act.wait_ge(experts_ready, 1)
            with act.Fori(0, MAX_BLOCKS - 1) as n:
                expert_block(n, False)
            expert_block(MAX_BLOCKS - 1, True)

        @block.tensor
        def _(pe):
            for signal in (xb_turned, ffn_done):
                pe.sem_inc(signal, FREE)
            pe.sem_inc(first_turned, FREE_2)
            pe.wait_ge(consts_ready, 1)
            pe.wait_ge(small_in, 16 * (2 * NB + 6))
            for b in range(NB):
                for c in range(C):
                    at = b * 512 + c * K2
                    pe.transpose(sc[:, at:at + P], ctx_in[:, b, 0, c * P:(c + 1) * P], ident[:])
                    pe.transpose(sc[:, at + P:at + K2], ctx_in[0:KR, b, 1, c * P:(c + 1) * P], ident[0:KR, 0:KR])
            for ci in range(C):
                for co in range(C):
                    pe.transpose(sc[:, 1024 + ci * D + co * P:1024 + ci * D + (co + 1) * P],
                                 wout_in[:, co, ci * P:(ci + 1) * P], ident[:])
            pe.transpose(sc[:, 1536:1536 + 3 * NP], bias_in[0:3 * NP, :], ident[0:3 * NP, 0:3 * NP])
            nb1 = (NE + 1) * FJ
            pe.transpose(sc[:, 1536 + P:1536 + P + nb1], b1_in[0:nb1, :], ident[0:nb1, 0:nb1]).then_inc(prep_turned, 1)
            def stage1_tile(t):
                pe.wait_ge(xn_ready, t + 1)
                if t >= 3:
                    pe.wait_ge(xT_ready, t - 2)
                for c in range(C):
                    tr = pe.transpose(stage1_banks[t % 3][:, c * P:(c + 1) * P], xn[t % 2][:, c * P:(c + 1) * P], ident[:])
                tr.then_inc(xn_turned, 1)

            def project(t, b, slot):
                what, half, k = SLOTS[slot]
                if what == "turn":
                    pe.wait_ge(fresh_ready, t * UNITS + 5 + k)
                    for m in range(4):
                        tr = pe.transpose(acc[1][:, m * P:(m + 1) * P], fresh[k][:, m * P:(m + 1) * P], ident[:])
                    tr.then_inc(v_turned, 1)
                    return
                if what == "v" and half == 1:
                    pe.wait_ge(v_taken, t * HALVES + 1)
                elif k > 0:
                    pe.wait_ge(fresh_ready, t * UNITS + k)
                elif not isinstance(t, int) or t > 0:
                    pe.wait_ge(v_taken, t * HALVES)
                kind = "qkv".index(what)
                tokens = slice(b * S + half * HS, b * S + (half + 1) * HS)
                terms = [(w, x, c) for w, x in ((w_pair_hi, xT_hi), (w_pair_lo, xT_hi), (w_pair_hi, xT_lo))
                         for c in range(C)]
                for i, (w, x, c) in enumerate(terms):
                    mm = pe.matmul(acc[1][:], w[:, kind, c, :], x[:, c, tokens],
                                   start=(i == 0), stop=(i == len(terms) - 1))
                mm.then_inc(proj_done, 1)

            def scores(it, b, s):
                i, h = s // 2, s % 2
                n = (i + 1) * P
                at = h * 1024
                if s == 0:
                    pe.wait_ge(lo_ready, it * QK + QK)
                for n0 in range(0, n, 512):
                    w = min(512, n - n0)
                    last = n0 + w == n
                    for r, k in enumerate((k_hi, k_lo)):
                        pe.matmul(sc[:, at + n0:at + n0 + w], q_parts[b][h][:, i * P:(i + 1) * P], k[b][h][:, n0:n0 + w],
                                  start=(r == 0), stop=(r == 1 and not last))
                pe.matmul(sc[:, at + n - P:at + n], identb[:], causal[:], start=False, stop=True
                          ).then_inc(scores_done, 1)

            def turn(p, b, next_turn, next_pair):
                it = p * NB + b
                for s in range(STEPS):
                    i, h = s // 2, s % 2
                    pe.wait_ge(exp_done, it * STEPS + s + 1)
                    for k, t0, m in chunks[s]:
                        pe.wait_ge(turned_taken[k], it * FILLS + fills[s][k] - 1 + FREE)
                        for r in range(m):
                            tr = pe.transpose(tp[k][:, r * P:(r + 1) * P], prob[h][:, (t0 + r) * P:(t0 + r + 1) * P],
                                              ident[:])
                        tr.then_inc(turned[k], 1)
                    if s + 2 < STEPS:
                        scores(it, b, s + 2)
                    elif next_turn:
                        scores(it + 1, 1 - b, s + 2 - STEPS)
                    if next_turn and s in SLOT_OF:
                        if s == 0:
                            pe.wait_ge(w_lo_ready, p + b + 1)
                        project(it + 1, 1 - b, SLOT_OF[s])
                    if s == 0:
                        pe.wait_ge(v_taken, it * HALVES + HALVES)
                    pe.wait_ge(o_taken, it * STEPS + s + FREE)
                    for k, t0, m in chunks[s]:
                        pe.wait_ge(turned_taken[k], it * FILLS + fills[s][k] + FREE)
                        for r in range(t0, t0 + m):
                            mm = pe.matmul(acc[0][:, 0:DH], probT[h][:, r, :], v_pair[b][:, r, h * DH:(h + 1) * DH],
                                           start=(r == 0), stop=(r == i))
                    mm.then_inc(pv_done, 1)

            def first_projection(slot):
                if slot == 0:
                    pe.wait_ge(w_lo_ready, 1)
                    pe.wait_ge(xT_ready, TB)
                project(0, 0, slot)
            prelude(stage1_tile, first_projection)
            pe.wait_ge(xT_ready, NT)
            pe.wait_ge(diag_copied, 2)
            scores(0, 0, 0)
            scores(0, 0, 1)
            attention(turn, pe.Fori)
            pe.wait_ge(o_taken, TURNS * STEPS + FREE)
            pe.wait_ge(diag_copied, 3)
            pe.wait_ge(w_in, 32)
            pe.wait_ge(rest_in, 16 * UH * NB)
            def energies(tile, b, q):
                u = q % 2
                c, h0 = q * UH // HC, q * UH % HC
                if q == 0:
                    pe.wait_ge(xn2_taken, tile.t + 1)
                    pe.wait_ge(mask_ready, tile.t + 1 + FREE_2)
                for a in range(2):
                    bank = sc[:, u * 1024 + a * 512:u * 1024 + a * 512 + 2 * K2]
                    pe.matmul(bank, xn2T[tile.odd][:, c, :],
                              ctx_diag[:, b, c, h0 + 2 * a:h0 + 2 * a + 2, :].rearrange("p h k -> p (h k)"),
                              start=True, stop=False)
                    mm = pe.matmul(bank.rearrange("p (h k) -> p h k", h=2), identb[:],
                                   mask_add[tile.odd].unsqueeze(1).to_broadcast([P, 2, K2]), start=False, stop=True)
                mm.then_inc(energy_done, 1)

            def turn_rows(rows):
                for c in range(C):
                    tr = pe.transpose(tp[1][:, c * P:(c + 1) * P], rows[:, c * P:(c + 1) * P], ident[:])
                return tr

            def besides(tile, q):
                before, last, near, ahead = tile + -2, tile + -1, tile + 1, tile + 2
                if q == 0:
                    if last.real:
                        pe.wait_ge(o2_ready, last.t + 1)
                        after(pe, xn3_low, last.t)
                        turn_rows(o2).then_inc(o2_turned, 1)
                    if before.real:
                        pe.wait_ge(xn3_taken, before.t + 1)
                        if near.real:
                            pe.wait_ge(y_taken, near.t + 1)
                        for c in range(C):
                            mm = pe.matmul(acc[1][:, 0:NE], xn3T[:, c, :], rw_sb[:, c, :], start=(c == 0), stop=(c == C - 1))
                        mm.then_inc(logits_done, 1)
                elif q == 1:
                    if last.real:
                        pe.wait_ge(o2_taken, last.t + 1)
                    if near.real:
                        pe.wait_ge(xn2_ready, near.t + 1)
                        turn_rows(xn2).then_inc(xn2_turned, 1)
                    if last.real:
                        if before.real:
                            pe.wait_ge(logits_taken, before.t + 1)
                        elif near.real:
                            pe.wait_ge(y_taken, near.t + 1)
                        for c in range(C):
                            mm = pe.matmul(acc[1][:, 0:D], o2T[:, c, :], w_outT[:, c, :], start=(c == 0), stop=(c == C - 1))
                        mm.then_inc(y2_done, 1)
                elif q == 2 and ahead.real:
                    pe.wait_ge(o_staged[ahead.odd], ahead.half * 16 + 16)
                    if near.real:
                        pe.wait_ge(xn2_taken, near.t + 1)
                    for r in range(4, 8):
                        tr = pe.transpose(tp[1][:, (r - 4) * P:(r - 3) * P], o_tile[ahead.odd][:, r * P:(r + 1) * P], ident[:])
                    tr.then_inc(second_turned, 1)
                    if last.real:
                        pe.wait_ge(y2_taken, last.t + 1)
                    elif near.real:
                        pe.wait_ge(y_taken, near.t + 1)
                    for r in range(4):
                        tr = pe.transpose(acc[1][:, r * P:(r + 1) * P], o_tile[ahead.odd][:, r * P:(r + 1) * P], ident[:])
                    tr.then_inc(first_turned, 1)
                elif q == 3:
                    if ahead.real:
                        pe.wait_ge(second_taken, ahead.t + 1)
                    if last.real:
                        pe.wait_ge(xn3_ready, last.t + 1)
                        turn_rows(xn3[last.odd]).then_inc(xn3_turned, 1)
                    if ahead.real:
                        pe.wait_ge(first_taken, ahead.t + 1)
                        for r in range(J):
                            mm = pe.matmul(acc[1][:, 0:D], oT[:, r, :], wo_sb[:, r, :], start=(r == 0), stop=(r == J - 1))
                        mm.then_inc(y_done, 1)

            def cycle(tile, b, b_next):
                last, near = tile + -1, tile + 1
                for q in range(NQ):
                    if tile.real:
                        pe.wait_ge(cexp_done, tile.t * NQ + q + 1)
                        for r in range(UH):
                            tr = pe.transpose(tp[0][:, r * P:(r + 1) * P], pm[q % 2][:, r, :], ident[:])
                        tr.then_inc(pm_turned, 1)
                    if q < 2 and tile.real:
                        energies(tile, b, q + 2)
                    if q >= 2 and near.real:
                        energies(near, b_next, q - 2)
                    if tile.real:
                        if q == 0 and last.real:
                            pe.wait_ge(o2_ready, last.t + 1)
                        pe.transpose(acc[0][:, REST:REST + P], pr[q % 2].rearrange("p h k -> p (h k)"), ident[:]
                                     ).then_inc(pr_turned, 1)
                    besides(tile, q)
                    if tile.real:
                        pe.wait_ge(pr_taken, tile.t * NQ + q + 1)
                        pe.wait_ge(pm_taken, tile.t * NQ + q + 1)
                        at = q * UH * V1
                        pe.matmul(acc[0][:, at:at + UH * V1], prT[q % 2],
                                  v_rest[:, b, q * UH:(q + 1) * UH, :].rearrange("p h k -> p (h k)"),
                                  start=True, stop=False)
                        for r in range(UH):
                            mm = pe.matmul(acc[0][:, at + r * V1:at + (r + 1) * V1], pmT[q % 2][:, r, :],
                                           v_main[:, b, q * UH + r, :], start=False, stop=(r == UH - 1))
                        mm.then_inc(cpv_done, 1)
            tiles(cycle, pe.Fori)
            pe.wait_ge(both_ready, 1)
            bf = both.rearrange("p t e -> p (t e)")
            pe.matmul(acc[0][:, 0:NT * NE], lower[:], bf, start=True, stop=True)
            pe.matmul(acc[1][:, 0:NT * NE], ones[:], bf, start=True, stop=True).then_inc(counted, 1)

            def ffn_in(idx, x_hi, x_lo):
                for k in range(FJ):
                    if k % 4 == 0:
                        pe.wait_ge(w1_ready, idx * 2 + k // 4 + 1)
                    at = slice(k * P, (k + 1) * P)
                    terms = [(w, x, c) for w, x in ((w1_hi, x_hi), (w1_lo, x_hi), (w1_hi, x_lo)) for c in range(C)]
                    for i, (w, x, c) in enumerate(terms):
                        mm = pe.matmul(sc[:, k * BLK:(k + 1) * BLK], w[:, c, at], x(c),
                                       start=(i == 0), stop=(i == len(terms) - 1))
                    if k % 2:
                        mm.then_inc(h_done, 1)

            def ffn_out(m, idx):
                pe.wait_ge(ffn_taken, m + FREE)
                for k in range(FJ):
                    if k % 2 == 0:
                        pe.wait_ge(h_ready, m * (FJ // 2) + k // 2 + 1 + FREE_2)
                        pe.wait_ge(w2_ready, idx * 4 + k // 2 + 1)
                    for tt in range(TT):
                        rows = slice(tt * P, (tt + 1) * P)
                        for i, (h, w) in enumerate(((h_hi, w2_hi), (h_hi, w2_lo), (h_lo, w2_hi))):
                            mm = pe.matmul(acc[tt][:, 0:D], h[:, k, rows], w[:, k, :],
                                           start=(k == 0 and i == 0), stop=(k == FJ - 1 and i == 2))
                mm.then_inc(ffn_done, 1)

            def turn_block(n):
                pe.wait_ge(xb_in, n * 16 + 16)
                for c in range(C):
                    for tt in range(TT):
                        tr = pe.transpose(tp[0][:, c * BLK + tt * P:c * BLK + (tt + 1) * P],
                                          xb[:, tt, c * P:(c + 1) * P], ident[:])
                tr.then_inc(xb_turned, 1)

            def shared_in(m):
                ffn_in(0, lambda c: xT_hi[:, c, ds(m * BLK, BLK)], lambda c: xT_lo[:, c, ds(m * BLK, BLK)])

            def expert_in(n):
                pe.wait_ge(xb_ready, n + 1)
                ffn_in(n + 1, lambda c: xb_hi[:, c, :], lambda c: xb_lo[:, c, :])

            pe.wait_ge(dest_ready, 2)
            with pe.Fori(0, NSH - 1) as m:
                shared_in(m)
                ffn_out(m, 0)
            shared_in(NSH - 1)
            turn_block(0)
            ffn_out(NSH - 1, 0)
            with pe.Fori(0, MAX_BLOCKS - 1) as n:
                expert_in(n)
                turn_block(n + 1)
                ffn_out(n + NSH, n + 1)
            expert_in(MAX_BLOCKS - 1)
            ffn_out(MAX_BLOCKS - 1 + NSH, MAX_BLOCKS)


_INS = ['x', 'ctx_1024', 'mask_Bx1xSxS2_ik1', 'L0_attn_Wq', 'L0_attn_Wk', 'L0_attn_Wv', 'L0_attn_bq', 'L0_attn_bk',
        'L0_attn_bv', 'L0_attn_Wo', 'L0_attn_bo', 'L0_xattn_W_out', 'L0_xattn_b_out', 'L0_ffn_shared_w1',
        'L0_ffn_shared_b1', 'L0_ffn_shared_w2', 'L0_ffn_shared_b2', 'L0_ffn_router_w', 'L0_ffn_router_b',
        'L0_ffn_exp_w1', 'L0_ffn_exp_b1', 'L0_ffn_exp_w2', 'L0_ffn_exp_b2']


def kernel(**inputs):
    import numpy as _np
    import concourse.bacc as _bacc
    from concourse import mybir as _mybir
    from concourse.bass_utils import run_bass_kernel_spmd as _run

    nc = _bacc.Bacc("TRN2", target_bir_lowering=False, num_devices=1)
    arrays, args = {}, []
    for name in _INS:
        a = _np.ascontiguousarray(inputs[name])
        arrays[f"in_{name}_dram"] = a
        args.append(nc.dram_tensor(f"in_{name}_dram", a.shape, _mybir.dt.from_np(a.dtype), kind="ExternalInput").ap())
    shape = inputs['x'].shape
    args.append(nc.dram_tensor("out_dram", shape, _mybir.dt.from_np(_np.dtype('float32')), kind="ExternalOutput").ap())
    decoder_layer(nc, *args)
    r = _run(nc, [arrays], core_ids=[0])
    return r.results[0]["out_dram"]
```

```python
from contextlib import ExitStack, contextmanager

import numpy as np
import concourse.bass as bass
from concourse import mybir

F32 = mybir.dt.float32
F32R = mybir.dt.float32r
BF16 = mybir.dt.bfloat16
I32 = mybir.dt.int32
U32 = mybir.dt.uint32
ALU = mybir.AluOpType
ACT = mybir.ActivationFunctionType
AX = mybir.AxisListType
ds = bass.ds

P = 128
EPS = 1e-5
MASKED = -1e30
FREE = 1
FREE_2 = 2
CROSS_MASKED = -1e20


class Chain:

    def __init__(self, eng, sem):
        self.eng, self.sem, self.base, self.k, self.turn, self.per = eng, sem, 0, 0, 0, 0

    def loop(self, turn, per):
        self.base += self.k
        self.turn, self.per, self.k = turn, per, 0

    def end(self, turns):
        assert self.k == self.per, (self.k, self.per)
        self.base += turns * self.per
        self.turn, self.per, self.k = 0, 0, 0

    def __call__(self, ins):
        self.k += 1
        ins.then_inc(self.sem, 1)
        self.eng.wait_ge(self.sem, self.turn * self.per + (self.base + self.k))


def decoder_layer(nc, x, ctx, mask, wq, wk, wv, bq, bk, bv, wo, bo, w_out, b_out,
                  sw1, sb1, sw2, sb2, rw, rb, ew1, eb1, ew2, eb2, out):
    NB, S, D = x.shape
    H, _, DH = wq.shape
    K2 = ctx.shape[1]
    F = sw1.shape[1]
    NE = rw.shape[1]
    T = NB * S
    NT = T // P
    TB = S // P
    C = D // P
    NP = H // 2
    HD = H * DH
    J = HD // P
    FJ = F // P
    CD = D // H
    HC = P // CD
    KR = K2 - P
    RS = 32
    UH = 4
    NQ = H // UH
    V1 = CD + 1
    BLK = 256
    TT = BLK // P
    NSH = T // BLK
    FIRST = NSH // 2
    RING = 8
    LAST = NSH - FIRST
    MAX_BLOCKS = 2 * T // BLK + NE - 1
    assert DH * 2 == P and TB == 8 and C == 2 and 0 < KR <= RS and HC == 8 and (NT, LAST) == (16, 4)

    with ExitStack() as stack:
        def sb(name, shape, dt=F32):
            return stack.enter_context(nc.sbuf_tensor(name, shape, dt))

        def sem(name):
            return stack.enter_context(nc.semaphore(name))

        x_sb = sb("x_sb", [P, NT, D])
        xT_hi = sb("xT_hi", [P, C, T], F32R)
        xT_lo = sb("xT_lo", [P, C, T], F32R)
        wo_sb = sb("wo_sb", [P, J, D])
        ctxT = sb("ctxT", [P, NB, NQ, K2])
        v_main = sb("v_main", [P, NB, H, V1])
        v_rest = sb("v_rest", [P, NB, H, V1])
        w_outT = sb("w_outT", [P, C, D])
        rw_sb = sb("rw_sb", [P, C, NE])
        ident = sb("ident", [P, P])
        identb = sb("identb", [P, P], BF16)
        causal = sb("causal", [P, P], BF16)
        bias_qkv = sb("bias_qkv", [P, 3, NP])
        bias_now = sb("bias_now", [P, 3])
        bo_b = sb("bo_b", [P, D])
        bout_b = sb("bout_b", [P, D])
        sb2_b = sb("sb2_b", [P, D])
        rb_b = sb("rb_b", [P, NE])
        b1T = sb("b1T", [P, (NE + 1) * FJ])
        mean_var = sb("mean_var", [P, NT, 2])
        stats = sb("stats", [P, NT, 6])
        rstd = sb("rstd", [P, NT])
        power = sb("power", [P, NT])
        logits = sb("logits", [P, NT, NE])
        weight = sb("weight", [P, 2, NT])
        dest = sb("dest", [P, 2, NT], U32)
        block_expert = sb("block_expert", [P, MAX_BLOCKS], I32)
        zero_rows = sb("zero_rows", [P, D])
        head_of = sb("head_of", [P, HC])
        in_head = sb("in_head", [P, UH])
        arena = sb("arena", [P, 12288])
        arena_r = sb("arena_r", [P, 13824], F32R)

        place = [0]

        def region(*shape, dt=F32):
            words = int(np.prod(shape))
            a = arena[:, place[0]:place[0] + words]
            place[0] += words
            assert place[0] <= arena.shape[1], place[0]
            if dt is not F32:
                a = a.bitcast(dt)
            names = "abcd"[:len(shape)]
            if len(shape) > 1:
                a = a.rearrange(f"p ({' '.join(names)}) -> p {' '.join(names)}",
                                **{n: s for n, s in zip(names, shape)})
            return a

        place_r = [0]

        def region_r(*shape):
            words = int(np.prod(shape))
            a = arena_r[:, place_r[0]:place_r[0] + words]
            place_r[0] += words
            assert place_r[0] <= arena_r.shape[1], place_r[0]
            names = "abcd"[:len(shape)]
            if len(shape) > 1:
                a = a.rearrange(f"p ({' '.join(names)}) -> p {' '.join(names)}",
                                **{n: s for n, s in zip(names, shape)})
            return a

        xn = [region(D) for _ in range(2)]
        w_pair = region(3, C, P)
        fresh = [region(S // 2) for _ in range(2)]
        projections_end = place[0]
        o_turn = [region(TB, P) for _ in range(2)]
        v_pair = [region(TB, P) for _ in range(2)]
        ctx_in = region(NB, 2, D)
        bias_in = region(P)
        b1_in = region(P)
        wout_in = region(C, D)
        place[0] -= NB * 2 * D + 2 * P + C * D
        prob = [region(S) for _ in range(2)]
        probT = [region(TB, P) for _ in range(2)]
        neg_max = region(2)
        row_sum = region(2 * TB)
        row_inv = region(2 * TB)
        w_pair_hi, w_pair_lo = region_r(3, C, P), region_r(3, C, P)
        q_parts = [[region_r(S) for _ in range(2)] for _ in range(2)]
        k_hi = [[region_r(S) for _ in range(2)] for _ in range(2)]
        k_lo = [[region_r(S) for _ in range(2)] for _ in range(2)]
        half_rows = [slice(0, DH), slice(DH, P)]
        place[0] = 0
        o_tile = [region(HD) for _ in range(2)]
        assert place[0] <= projections_end
        place[0] = projections_end + 2 * TB * P
        oT = region(J, P)
        xn2, ln2_sum, ln2_sq, ln2_var, ln2_r = region(D), region(1), region(D), region(1), region(1)
        place_r[0] = 0
        xn2_parts = [region_r(C, 2, P) for _ in range(2)]
        ctx_hi, ctx_lo = region_r(NB, NQ, UH, K2), region_r(NB, NQ, UH, K2)
        mask_in = [region(K2, dt=I32) for _ in range(2)]
        mask_add = [region(K2 // 2, dt=BF16) for _ in range(2)]
        energy = [region(UH, K2) for _ in range(2)]
        pm = [region(UH, P) for _ in range(2)]
        pr = [region(UH, RS) for _ in range(2)]
        pmT = [region(UH, P) for _ in range(2)]
        prT = [region(P) for _ in range(2)]
        cmax = [region(UH) for _ in range(2)]
        cinv, o2, o2T = region(H), region(D), region(C, P)
        xn3 = [region(D) for _ in range(2)]
        ln3_sum, ln3_sq, ln3_var, ln3_r, xn3T = region(1), region(D), region(1), region(1), region(C, P)
        REST = 320
        place[0] = 0
        w1_raw = region(C, F)
        w2_raw = region(FJ, D)
        h_raw = [region(2, BLK) for _ in range(2)]
        xb = region(TT, D)
        yb = region(TT, D)
        b2_all = region(NE, D)
        x3_rows = region(NT, D)
        place[0] -= NT * D
        y_got = [region(RING, D) for _ in range(2)]
        place_r[0] = 0
        w1_hi, w1_lo = region_r(C, F), region_r(C, F)
        w2_hi, w2_lo = region_r(FJ, D), region_r(FJ, D)
        h_hi, h_lo = region_r(FJ, BLK), region_r(FJ, BLK)
        xb_hi, xb_lo = region_r(C, BLK), region_r(C, BLK)

        route = sb("route", [P, 12, NT, NE])
        hot1, hot2, eq, cand, masked, shifted, expd, both, pos, picked, jm8, pos2 = [
            route[:, i] for i in range(12)]
        tile_sums = [sb(f"tile_sums{i}", [P, NT // 2 + NT, NE]) for i in range(2)]
        tile_base = tile_sums[0][:, NT // 2 - 1:, :]
        block_sums = [sb(f"block_sums{i}", [P, NE // 2 + NE]) for i in range(2)]
        small = sb("small", [P, 11, NT])
        first_max, first_at, second_max, second_at, gap, gap_exp, total, inv_total, w_sum, w_inv, destf = [
            small[:, i, :] for i in range(11)]
        ne_small = sb("ne_small", [P, 2, NE])
        n_blocks, expert_base = [ne_small[:, i, :] for i in range(2)]
        block_starts = sb("block_starts", [P, NE, T // BLK])
        block_cmp = sb("block_cmp", [P, NE, T // BLK])
        block_no = sb("block_no", [P, MAX_BLOCKS, NE])
        block_ge = sb("block_ge", [P, MAX_BLOCKS, NE])
        block_f = sb("block_f", [P, MAX_BLOCKS])
        lower = sb("lower", [P, P])
        ones = sb("ones", [P, P])

        xs = nc.dram_tensor("x_sorted", [MAX_BLOCKS * BLK, D], F32, kind="Internal").ap()
        o_dram = nc.dram_tensor("attention_out", [T, HD], F32, kind="Internal").ap()
        x3_dram = nc.dram_tensor("x3", [T, D], F32, kind="Internal").ap()
        ys = nc.dram_tensor("y_sorted", [MAX_BLOCKS * BLK, D], F32, kind="Internal").ap()

        sc = stack.enter_context(nc.psum_tensor("sc", [P, 4 * 512], F32))
        tp = [stack.enter_context(nc.psum_tensor(f"tp{i}", [P, 512], F32)) for i in range(2)]
        acc = [stack.enter_context(nc.psum_tensor(f"acc{i}", [P, 512], F32)) for i in range(2)]

        def pair(name):
            return [sem(name + "_even"), sem(name + "_odd")]

        pool_step, vector_step = sem("pool_step"), sem("vector_step")
        x_in = [sem(f"x_in_{q}") for q in range(4)]
        small_in, w_in, rows_in, rest_in, zeros_ready, xs_zero = [sem(n) for n in (
            "small_in", "w_in", "rows_in", "rest_in", "zeros_ready", "xs_zero")]
        consts_ready, prep_turned, prep_copied = sem("consts_ready"), sem("prep_turned"), sem("prep_copied")
        ctxT_copied = sem("ctxT_copied")
        ctx_hi_ready, ctx_ready, xn2_low = sem("ctx_hi_ready"), sem("ctx_ready"), sem("xn2_low")
        stats_done, rstd_done = sem("stats_done"), sem("rstd_done")
        xn_ready, xn_turned, xT_hi_ready, xT_ready = [sem(n) for n in ("xn_ready", "xn_turned", "xT_hi_ready", "xT_ready")]
        w_hi_ready, w_lo_ready = sem("w_hi_ready"), sem("w_lo_ready")
        o_stored, x3_loaded = sem("o_stored"), sem("x3_loaded")
        w_pair_in, proj_done, fresh_ready, hi_ready, lo_ready, v_turned, v_taken = [sem(n) for n in (
            "w_pair_in", "proj_done", "fresh_ready", "hi_ready", "lo_ready", "v_turned", "v_taken")]
        turned, turned_taken = pair("turned"), pair("turned_taken")
        scores_done, max_done, exp_done, pv_done, o_taken = [sem(n) for n in (
            "scores_done", "max_done", "exp_done", "pv_done", "o_taken")]
        o_staged, mask_staged, x3_stored = pair("o_staged"), pair("mask_staged"), pair("x3_stored")
        mask_ready, first_turned, second_turned, first_taken, second_taken, y_done, y_taken, var2_done, rstd2_done = [
            sem(n) for n in ("mask_ready", "first_turned", "second_turned", "first_taken", "second_taken", "y_done",
                             "y_taken", "var2_done", "rstd2_done")]
        xn2_ready, xn2_turned, xn2_taken = [sem(n) for n in ("xn2_ready", "xn2_turned", "xn2_taken")]
        energy_done, shifted_done, cexp_done, pm_turned, pr_turned, pm_taken, pr_taken, cpv_done = [sem(n) for n in (
            "energy_done", "shifted_done", "cexp_done", "pm_turned", "pr_turned", "pm_taken", "pr_taken", "cpv_done")]
        o2_ready, o2_turned, o2_taken, y2_done, y2_taken, var3_done, rstd3_done = [sem(n) for n in (
            "o2_ready", "o2_turned", "o2_taken", "y2_done", "y2_taken", "var3_done", "rstd3_done")]
        xn3_ready, xn3_turned, xn3_taken, xn3_low, x3_free, logits_done, logits_taken = [sem(n) for n in (
            "xn3_ready", "xn3_turned", "xn3_taken", "xn3_low", "x3_free", "logits_done", "logits_taken")]
        gap_ready, route_exp_done, both_ready, counted, experts_ready, dest_ready, scattered = [sem(n) for n in (
            "gap_ready", "route_exp_done", "both_ready", "counted", "experts_ready", "dest_ready", "scattered")]
        o_free = sem("o_free")
        b2_in, w1_in, xb_in = [sem(n) for n in ("b2_in", "w1_in", "xb_in")]
        w2_in = [sem("w2_in_first_half"), sem("w2_in_second_half")]
        w1_hi_ready, w1_ready, w2_hi_ready, w2_ready = [sem(n) for n in (
            "w1_hi_ready", "w1_ready", "w2_hi_ready", "w2_ready")]
        xb_turned, xb_hi_ready, xb_ready = [sem(n) for n in ("xb_turned", "xb_hi_ready", "xb_ready")]
        h_done, gelu_done, h_ready, ffn_done, ffn_taken = [sem(n) for n in (
            "h_done", "gelu_done", "h_ready", "ffn_done", "ffn_taken")]
        yb_taken, y_stored, gathered, final_done, out_stored = (
            sem("yb_taken"), sem("y_stored"), [sem(f"gathered_{r}") for r in range(RING)], sem("final_done"), sem("out_stored"))

        xf = x.rearrange("b (t p) d -> p (b t) d", p=P)
        of = out.rearrange("b (t p) d -> p (b t) d", p=P)
        STEPS = 2 * TB
        TURNS = NB * NP
        chunks = [[(s % 2, 0, s // 2 + 1)] if s // 2 < 4 else [(0, 0, 4), (1, 4, s // 2 - 3)] for s in range(STEPS)]
        fills = [[sum(cb == k for r in range(s + 1) for cb, _, _ in chunks[r]) for k in range(2)]
                 for s in range(STEPS)]
        FILLS = fills[-1][0]
        assert (NT, NE) == (2 ** 4, 2 ** 3)
        assert fills[-1] == [FILLS, FILLS] and NB == 2
        SLOTS = [("q", 0, 0), ("q", 1, 1), ("k", 0, 2), ("k", 1, 3), ("v", 0, 4), ("turn", 0, 0), ("v", 1, 5), ("turn", 1, 1)]
        UNITS, QK, HALVES = 6, 4, 2
        SLOT_OF = {0: 0, 2: 1, 4: 2, 6: 3, 7: 4, 9: 5, 11: 6, 13: 7}
        SPLIT_AT = 12
        HS = S // 2

        def prelude(tile, slot):
            for t in range(NT):
                tile(t)
                if t >= TB:
                    slot(t - TB)

        stage1_banks = [tp[0], tp[1], acc[0]]

        def attention(turn, loop):
            with loop(0, NP - 1) as p:
                turn(p, 0, True, True)
                turn(p, 1, True, True)
            turn(NP - 1, 0, True, False)
            turn(NP - 1, 1, False, False)


        class Tile:

            def __init__(self, j, n):
                self.j, self.n, self.odd = j, n, n % 2
                self.t, self.half = (n, n // 2) if j is None else (j * 2 + n, j + n // 2)
                self.real = j is not None or 0 <= n < NT

            def __add__(self, k):
                return Tile(self.j, self.n + k)

        def tiles(cycle, loop):
            def peeled(first, end):
                for n in range(first, end):
                    cycle(Tile(None, n), n // TB, (n + 1) // TB)

            def looped(first, end, b):
                with loop(0, (end - first) // 2) as j:
                    for n in (first, first + 1):
                        cycle(Tile(j, n), b, b)
            peeled(-2, 2)
            looped(2, TB - 2, 0)
            peeled(TB - 2, TB)
            looped(TB, NT - 2, 1)
            peeled(NT - 2, NT + 2)

        def after(eng, signal, count):
            if not isinstance(count, int) or count > 0:
                eng.wait_ge(signal, count)

        block = stack.enter_context(nc.Block())

        @block.sync
        def _(sp):
            sp.sem_inc(y_stored, 16 * FREE)
            for q in range(4):
                at = slice(q * NT // 4, (q + 1) * NT // 4)
                sp.dma_start(x_sb[:, at, :], xf[:, at, :]).then_inc(x_in[q], 16)
            for b in range(NB):
                sp.dma_start(ctx_in[:, b, 0, :], ctx[b, 0:P, :]).then_inc(small_in, 16)
                sp.dma_start(ctx_in[0:KR, b, 1, :], ctx[b, P:K2, :]).then_inc(small_in, 16)
            for k, w in enumerate((bq, bk, bv)):
                sp.dma_start(bias_in[k * NP:(k + 1) * NP, :], w.rearrange("(p h) d -> p (h d)", h=2)).then_inc(small_in, 16)
            sp.dma_start(b1_in[0:NE * FJ, :], eb1.rearrange("e (j p) -> (e j) p", p=P)).then_inc(small_in, 16)
            sp.dma_start(b1_in[NE * FJ:(NE + 1) * FJ, :], sb1.rearrange("(j p) -> j p", p=P)).then_inc(small_in, 16)
            sp.dma_start(wout_in, w_out.rearrange("(c p) d -> p c d", p=P)).then_inc(small_in, 16)
            def load_pair(p):
                for k, w in enumerate((wq, wk, wv)):
                    for c in range(C):
                        sp.dma_start(w_pair[:, k, c, :].rearrange("e (h d) -> e h d", h=2),
                                     w[ds(2 * p, 2), c * P:(c + 1) * P, :].rearrange("h e d -> e h d")
                                     ).then_inc(w_pair_in, 16)
            load_pair(0)
            sp.wait_ge(consts_ready, 1)
            for r in range(UH):
                for b in range(NB):
                    sp.dma_start(v_rest[r * RS:r * RS + KR, b, r::UH, 0:CD],
                                 ctx[b, P:K2, :].rearrange("k (h d) -> k h d", d=CD)[:, r::UH, :]).then_inc(rest_in, 16)
            sp.dma_start(wo_sb[:], wo.rearrange("(j p) d -> p j d", p=P)).then_inc(w_in, 16)
            sp.dma_start(rw_sb[:], rw.rearrange("(c p) f -> p c f", p=P)).then_inc(w_in, 16)
            for dst, src in ((bo_b, bo), (bout_b, b_out), (sb2_b, sb2), (rb_b, rb)):
                sp.dma_start(dst[:], src.partition_broadcast(P)).then_inc(rows_in, 16)
            for n in range(MAX_BLOCKS * TT):
                sp.dma_start(xs[n * P:(n + 1) * P, :], zero_rows[:]).then_inc(xs_zero, 16)
            with sp.Fori(0, NP - 1) as p:
                sp.wait_ge(w_lo_ready, p + 1)
                load_pair(p + 1)
            def load_outputs(t, u):
                sp.dma_start(o_tile[u], o_dram[ds(t * P, P), :]).then_inc(o_staged[u], 16)

            def load_mask(t, u):
                sp.wait_ge(mask_ready, t - 1 + FREE_2)
                sp.dma_start(mask_in[u], mask.rearrange("b a q k -> (b a q) k")[ds(t * P, P), :]).then_inc(mask_staged[u], 16)
            sp.wait_ge(o_free, TURNS - 1 + FREE_2)
            sp.wait_ge(lo_ready, TURNS * QK)
            sp.wait_ge(v_turned, TURNS * HALVES)
            for u in range(2):
                load_outputs(u, u)
            sp.wait_ge(o_taken, TURNS * STEPS + FREE)
            sp.wait_ge(o_free, TURNS + FREE_2)
            with sp.Fori(0, NT // 2 - 1) as j:
                for u in range(2):
                    t = j * 2 + u
                    load_mask(t, u)
                    sp.wait_ge(first_turned, t + 1 + FREE_2)
                    load_outputs(t + 2, u)
            for u in range(2):
                load_mask(NT - 2 + u, u)
            sp.wait_ge(logits_taken, NT)
            for u in range(2):
                sp.wait_ge(x3_stored[u], 16 * (NT // 2))
            def load_w2(src, before):
                for half in range(2):
                    after(sp, w2_ready, (before - 1) * 4 + (half + 1) * 2 if not isinstance(before, int) or before else 0)
                    at = slice(half * FJ // 2, (half + 1) * FJ // 2)
                    sp.dma_start(w2_raw[:, at, :], src[:, at, :]).then_inc(w2_in[half], 16)

            sp.dma_start(w1_raw, sw1.rearrange("(c p) f -> p c f", p=P)).then_inc(w1_in, 16)
            load_w2(sw2.rearrange("(c p) f -> p c f", p=P), 0)
            sp.dma_start(x3_rows, x3_dram.rearrange("(t p) d -> p t d", p=P)).then_inc(x3_loaded, 16)
            sp.dma_start(b2_all, eb2.rearrange("e d -> (e d)").partition_broadcast(P)
                         .rearrange("p (e d) -> p e d", d=D)).then_inc(b2_in, 16)
            sp.wait_ge(experts_ready, 1)
            def store_results(n):
                sp.wait_ge(yb_taken, n + 1)
                sp.dma_start(ys[ds(n * BLK, BLK), :].rearrange("(t p) d -> p t d", p=P), yb).then_inc(y_stored, 16)

            def load_block(n, store):
                e = sp.value_load(block_expert[0:1, ds(n, 1)], min_val=0, max_val=NE - 1)
                sp.wait_ge(w1_ready, n * 2 + 2)
                sp.dma_start(w1_raw, ew1[ds(e, 1)].rearrange("a (c p) f -> p (a c) f", p=P)).then_inc(w1_in, 16)
                sp.wait_ge(scattered, 16 * 2 * NT)
                sp.wait_ge(xb_turned, n + FREE)
                sp.dma_start(xb, xs[ds(n * BLK, BLK), :].rearrange("(t p) d -> p t d", p=P)).then_inc(xb_in, 16)
                if store:
                    store_results(n - 2)
                load_w2(ew2[ds(e, 1)].rearrange("a (c p) f -> p (a c) f", p=P), n + 1)
            load_block(0, False)
            load_block(1, False)
            with sp.Fori(0, MAX_BLOCKS - 2) as j:
                load_block(j + 2, True)
            sp.wait_ge(w1_ready, MAX_BLOCKS * 2 + 2)
            sp.dma_start(w1_raw, sw1.rearrange("(c p) f -> p c f", p=P)).then_inc(w1_in, 16)
            store_results(MAX_BLOCKS - 2)
            load_w2(sw2.rearrange("(c p) f -> p c f", p=P), MAX_BLOCKS + 1)
            store_results(MAX_BLOCKS - 1)
            with sp.Fori(0, NT) as t:
                sp.wait_ge(final_done, t + 1)
                sp.dma_start(of[:, ds(t, 1), :], x_sb[:, ds(t, 1), :]).then_inc(out_stored, 16)
            sp.wait_ge(out_stored, 16 * NT)

        @block.gpsimd
        def _(pool):
            step = Chain(pool, pool_step)
            pool.sem_inc(x3_free, FREE)
            pool.sem_inc(o_free, FREE_2)
            step(pool.memset(ident[:], 0.0))
            step(pool.affine_select(out=ident[:], in_=ident[:], compare_op=ALU.not_equal, fill=1.0, base=0,
                                    pattern=[[-1, P]], channel_multiplier=1))
            step(pool.tensor_copy(identb[:], ident[:]))
            step(pool.memset(causal[:], 0.0))
            step(pool.affine_select(out=causal[:], in_=causal[:], compare_op=ALU.is_ge, fill=MASKED, base=0,
                                    pattern=[[-1, P]], channel_multiplier=1))
            step(pool.memset(ones[:], 1.0))
            step(pool.affine_select(out=lower[:], in_=ones[:], compare_op=ALU.is_gt, fill=0.0, base=0,
                                    pattern=[[1, P]], channel_multiplier=-1))
            step(pool.affine_select(out=head_of[:], in_=ones[:, 0:HC], compare_op=ALU.is_ge, fill=0.0, base=0,
                                    pattern=[[-CD, HC]], channel_multiplier=1))
            step(pool.affine_select(out=head_of[:], in_=head_of[:], compare_op=ALU.is_ge, fill=0.0, base=CD - 1,
                                    pattern=[[CD, HC]], channel_multiplier=-1))
            step(pool.tensor_tensor(in_head[:], head_of[:, 0:UH], head_of[:, UH:HC], ALU.add))
            step(pool.memset(power[:], -0.5))
            step(pool.memset(v_rest[:], 0.0))
            step(pool.memset(v_main[:], 1.0))
            for i in range(2):
                step(pool.memset(tile_sums[i][:], 0.0))
                step(pool.memset(block_sums[i][:], 0.0))
            for r in range(UH):
                step(pool.memset(v_rest[r * RS:r * RS + KR, :, r::UH, CD:V1], 1.0))
            step(pool.iota(jm8, [[0, NT], [1, NE]], base=-NE, channel_multiplier=0,
                           allow_small_or_imprecise_dtypes=True))
            step(pool.iota(block_starts[:], [[0, NE], [BLK, T // BLK]], base=0, channel_multiplier=0,
                           allow_small_or_imprecise_dtypes=True))
            step(pool.iota(block_no[:], [[1, MAX_BLOCKS], [0, NE]], base=0, channel_multiplier=0,
                           allow_small_or_imprecise_dtypes=True))
            pool.memset(zero_rows[:], 0.0).then_inc(consts_ready, 1)
            pool.wait_ge(consts_ready, 1)
            pool.wait_ge(stats_done, 1)
            step(pool.tensor_scalar(rstd[:], mean_var[:, :, 1], EPS, None, ALU.add))
            pool.tensor_tensor(rstd[:], rstd[:], power[:], ALU.pow).then_inc(rstd_done, 1)
            def weights_low(p):
                pool.wait_ge(w_hi_ready, p + 1)
                pool.tensor_tensor(w_pair_lo, w_pair, w_pair_hi.bitcast(F32), ALU.subtract).then_inc(w_lo_ready, 1)

            def low_parts(t, b, slot):
                what, half, k = SLOTS[slot]
                at = slice(half * HS, (half + 1) * HS)
                if what in "qk":
                    if not isinstance(t, int) or t * QK + k > 0:
                        pool.wait_ge(lo_ready, t * QK + k)
                    pool.wait_ge(hi_ready, t * QK + k + 1)
                if what == "q":
                    for h in range(2):
                        own, other = half_rows[h], half_rows[1 - h]
                        i = pool.tensor_tensor(q_parts[b][h][other, at], fresh[k % 2][own, :],
                                               q_parts[b][h][own, at].bitcast(F32), ALU.subtract)
                    i.then_inc(lo_ready, 1)
                if what == "k":
                    for h in range(2):
                        own = half_rows[h]
                        for rows in half_rows:
                            i = pool.tensor_tensor(k_lo[b][h][rows, at], fresh[k % 2][own, :],
                                                   k_hi[b][h][own, at].bitcast(F32), ALU.subtract)
                    i.then_inc(lo_ready, 1)

            def turn(p, b, next_turn, next_pair):
                it = p * NB + b
                for s in range(STEPS):
                    if next_turn and SLOT_OF.get(s) == 0:
                        pool.wait_ge(w_lo_ready, p + b + 1)
                    if next_turn and s in SLOT_OF:
                        low_parts(it + 1, 1 - b, SLOT_OF[s])
                    if s == SPLIT_AT and next_pair and b == 0:
                        pool.wait_ge(lo_ready, (it + 2) * QK)
                        weights_low(p + 1)
                    if s % 2:
                        pool.wait_ge(o_taken, it * STEPS + s + 1 + FREE)
                        pool.dma_start(o_dram[b * S + s // 2 * P:b * S + (s // 2 + 1) * P, ds(p * P, P)],
                                       o_turn[b][:, s // 2, :]).then_inc(o_stored, 16)
                pool.wait_ge(o_stored, (it + 1) * (TB * 16))
                pool.sem_inc(o_free, 1)
            weights_low(0)
            pool.wait_ge(w_lo_ready, 1)
            for slot in range(len(SLOTS)):
                low_parts(0, 0, slot)
            attention(turn, pool.Fori)
            pool.wait_ge(lo_ready, TURNS * QK)
            pool.wait_ge(o_taken, TURNS * STEPS + FREE)
            for u in range(2):
                step(pool.memset(pr[u], 0.0))
            pool.sem_inc(zeros_ready, 1)
            def cycle(tile, b, b_next):
                last, ahead = tile + -1, tile + 2
                if last.real:
                    pool.wait_ge(var3_done, last.t + 1)
                    pool.tensor_tensor(ln3_r, ln3_var, power[:, 0:1], ALU.pow).then_inc(rstd3_done, 1)
                    pool.wait_ge(xn3_ready, last.t + 1)
                    pool.dma_start(x3_dram[ds(last.t * P, P), :], xn3[last.odd]).then_inc(x3_stored[last.odd], 16)
                if ahead.real:
                    pool.wait_ge(var2_done, ahead.t + 1)
                    pool.tensor_tensor(ln2_r, ln2_var, power[:, 0:1], ALU.pow).then_inc(rstd2_done, 1)
                if last.real:
                    pool.wait_ge(x3_stored[last.odd], last.half * 16 + 16)
                    pool.sem_inc(x3_free, 1)
            tiles(cycle, pool.Fori)
            def w2_low(idx):
                for q in range(4):
                    pool.wait_ge(w2_hi_ready, idx * 4 + q + 1)
                    at = slice(q * FJ // 4, (q + 1) * FJ // 4)
                    pool.tensor_tensor(w2_lo[:, at, :], w2_raw[:, at, :], w2_hi[:, at, :].bitcast(F32), ALU.subtract
                                       ).then_inc(w2_ready, 1)
            w2_low(0)
            pool.wait_ge(dest_ready, 2)
            pool.wait_ge(x3_loaded, 16)
            pool.wait_ge(xs_zero, 16 * MAX_BLOCKS * TT)
            for t in range(NT):
                for k in range(2):
                    pool.indirect_dma_start(xs, bass.IndirectOffsetOnAxis(ap=dest[:, k, t:t + 1], axis=0),
                                            x3_rows[:, t, :], None).then_inc(scattered, 16)
            with pool.Fori(0, MAX_BLOCKS) as n:
                w2_low(n + 1)
            w2_low(MAX_BLOCKS + 1)
            pool.wait_ge(y_stored, 16 * MAX_BLOCKS + 16 * FREE)
            for t in range(NT):
                if t >= RING:
                    pool.wait_ge(final_done, t - RING + 1)
                for k in range(2):
                    pool.indirect_dma_start(y_got[k][:, t % RING, :], None, ys,
                                            bass.IndirectOffsetOnAxis(ap=dest[:, k, t:t + 1], axis=0)
                                            ).then_inc(gathered[t % RING], 16)

        @block.vector
        def _(v):
            step = Chain(v, vector_step)
            for signal in (ffn_taken, o_taken, turned_taken[0]):
                v.sem_inc(signal, FREE)
            for signal in (h_ready, mask_ready):
                v.sem_inc(signal, FREE_2)
            for t in range(NT):
                if t % (NT // 4) == 0:
                    v.wait_ge(x_in[t // (NT // 4)], 16)
                st = v.bn_stats(stats[:, t, :], x_sb[:, t, :])
            step(st)
            for t in range(NT):
                ag = v.bn_aggr(mean_var[:, t, :], stats[:, t, :])
            ag.then_inc(stats_done, 1)
            v.wait_ge(prep_turned, 1)
            v.wait_ge(consts_ready, 1)
            v.tensor_scalar(bias_qkv[:, 0, :], sc[:, 1536:1536 + NP], DH ** -0.5, None, ALU.mult)
            step(v.tensor_copy(bias_qkv[:, 1:3, :].rearrange("p a b -> p (a b)"), sc[:, 1536 + NP:1536 + 3 * NP]))
            v.tensor_copy(bias_now[:], bias_qkv[:, :, 0])
            v.tensor_copy(b1T[:], sc[:, 1536 + P:1536 + P + (NE + 1) * FJ]).then_inc(prep_copied, 1)
            for q in range(NQ):
                for rows in half_rows:
                    i = v.tensor_copy(ctxT[rows, 1, q, :], sc[half_rows[q % 2], 512 + q // 2 * K2:512 + (q // 2 + 1) * K2])
            i.then_inc(ctxT_copied, 1)

            def low_part(t, bank):
                at = ds(t * P, P)
                return v.tensor_tensor(xT_lo[:, :, at], bank[:, 0:D].rearrange("p (c t) -> p c t", c=C),
                                       xT_hi[:, :, at].bitcast(F32), ALU.subtract)

            def normalize(t):
                if t < NT:
                    if t >= 2:
                        v.wait_ge(xn_turned, t - 1)
                    v.tensor_scalar(xn[t % 2], x_sb[:, t, :], mean_var[:, t, 0:1], rstd[:, t:t + 1],
                                    ALU.subtract, ALU.mult).then_inc(xn_ready, 1)

            def stage1_tile(t):
                normalize(t + 2)
                v.wait_ge(xT_hi_ready, t + 1)
                low_part(t, stage1_banks[t % 3]).then_inc(xT_ready, 1)

            def high_parts(t, b, slot):
                what, half, k = SLOTS[slot]
                at = slice(half * HS, (half + 1) * HS)
                if what in "qk":
                    v.wait_ge(fresh_ready, t * UNITS + k + 1)
                if what == "q":
                    for h in range(2):
                        i = v.tensor_copy(q_parts[b][h][half_rows[h], at], fresh[k % 2][half_rows[h], :])
                    i.then_inc(hi_ready, 1)
                if what == "k":
                    for h in range(2):
                        for rows in half_rows:
                            i = v.tensor_copy(k_hi[b][h][rows, at], fresh[k % 2][half_rows[h], :])
                    i.then_inc(hi_ready, 1)
                if what == "turn":
                    v.wait_ge(v_turned, t * HALVES + k + 1)
                    v.tensor_copy(v_pair[b][:, half * 4:half * 4 + 4, :].rearrange("p a b -> p (a b)"), acc[1][:]
                                  ).then_inc(v_taken, 1)

            def row_max(it, s):
                n = (s // 2 + 1) * P
                v.wait_ge(scores_done, it * STEPS + s + 1)
                v.tensor_reduce(neg_max[:, s % 2:s % 2 + 1], sc[:, (s % 2) * 1024:(s % 2) * 1024 + n], AX.X, ALU.max,
                                negate=True).then_inc(max_done, 1)

            def turn(p, b, next_turn, next_pair):
                it = p * NB + b
                if next_turn:
                    v.tensor_copy(bias_now[:].unsqueeze(2), bias_qkv[:, :, ds(p + b, 1)])
                for s in range(STEPS):
                    for k, t0, m in chunks[s]:
                        if k == 0:
                            v.wait_ge(turned[0], it * FILLS + fills[s][0])
                            v.tensor_copy(probT[s % 2][:, t0:t0 + m, :].rearrange("p a b -> p (a b)"),
                                          tp[0][:, 0:m * P]).then_inc(turned_taken[0], 1)
                    if s + 2 < STEPS:
                        row_max(it, s + 2)
                    elif next_turn:
                        row_max(it + 1, s + 2 - STEPS)
                    if next_turn and s - 1 in SLOT_OF:
                        high_parts(it + 1, 1 - b, SLOT_OF[s - 1])
                    v.wait_ge(exp_done, it * STEPS + s + 1)
                    step(v.reciprocal(row_inv[:, s:s + 1], row_sum[:, s:s + 1]))
                    v.wait_ge(pv_done, it * STEPS + s + 1)
                    if s == 0:
                        v.wait_ge(o_free, it + FREE_2 - 1)
                    v.tensor_scalar(o_turn[b][:, s // 2, (s % 2) * DH:(s % 2 + 1) * DH],
                                    acc[0][:, 0:DH], row_inv[:, s:s + 1], None, ALU.mult).then_inc(o_taken, 1)

            v.wait_ge(rstd_done, 1)
            normalize(0)
            normalize(1)
            prelude(stage1_tile, lambda slot: high_parts(0, 0, slot))
            for b in range(NB):
                v.tensor_copy(v_main[:, b, :, 0:CD], ctx_in[:, b, 0, :].rearrange("p (h d) -> p h d", d=CD))
            v.sem_inc(ctxT_copied, 1)
            row_max(0, 0)
            row_max(0, 1)

            @contextmanager
            def counted_loop(first, end):
                with v.Fori(first, end) as p:
                    step.loop(p, NB * STEPS)
                    yield p
                step.end(end - first)
            attention(turn, counted_loop)

            def x_tile(t):
                return x_sb[:, ds(t, 1), :].rearrange("p a d -> p (a d)")

            def cross_output(tile):
                v.wait_ge(cpv_done, tile.t * NQ + NQ)
                sums = acc[0][:, 0:H * V1].rearrange("p (h d) -> p h d", d=V1)
                step(v.reciprocal(cinv, sums[:, :, CD]))
                v.tensor_tensor(o2.rearrange("p (h d) -> p h d", d=CD), sums[:, :, 0:CD],
                                cinv.unsqueeze(2).to_broadcast([P, H, CD]), ALU.mult).then_inc(o2_ready, 1)

            def residual(t, add, row, taken, rows, total, square, var, between=None):
                v.tensor_tensor(x_tile(t), add, x_tile(t), ALU.add).then_inc(taken, 1)
                v.wait_ge(taken, t + 1)
                step(v.scalar_tensor_tensor(x_tile(t), x_tile(t), 1.0, row, ALU.mult, ALU.add, accum_out=total))
                step(v.tensor_scalar(total, total, -1.0 / D, None, ALU.mult))
                step(v.tensor_scalar(rows, x_tile(t), total, None, ALU.add))
                if between is not None:
                    between()
                step(v.tensor_tensor_reduce(square, rows, rows, 1.0, 0.0, ALU.mult, ALU.add, var))
                return v.tensor_scalar(var, var, 1.0 / D, EPS, ALU.mult, ALU.add)

            def shift(tile, q):
                u = q % 2
                v.wait_ge(energy_done, tile.t * NQ + q + 1)
                e = sc[:, u * 1024:(u + 1) * 1024].rearrange("p (a n) -> p a n", a=2)[:, :, 0:2 * K2] \
                    .rearrange("p a (h k) -> p a h k", h=2)
                step(v.tensor_reduce(cmax[u].rearrange("p (a h) -> p a h", a=2), e, AX.X, ALU.max))
                for a in range(2):
                    i = v.tensor_tensor(energy[u][:, 2 * a:2 * a + 2, :], e[:, a],
                                        cmax[u][:, 2 * a:2 * a + 2].unsqueeze(2).to_broadcast([P, 2, K2]),
                                        ALU.subtract)
                i.then_inc(shifted_done, 1)

            def context_low(b):
                for h in range(UH):
                    v.wait_ge(ctx_hi_ready, b * UH + h + 1)
                    v.scalar_tensor_tensor(ctx_lo[:, b, :, h, :], ctxT[:, b, :, :], in_head[:, h:h + 1],
                                           ctx_hi[:, b, :, h, :].bitcast(F32), ALU.mult, ALU.subtract).then_inc(ctx_ready, 1)

            def cycle(tile, b, b_next):
                before, last, near, ahead = tile + -2, tile + -1, tile + 1, tile + 2
                for q in range(NQ):
                    if q == 3 and tile.j is None and tile.n in (-2, 0):
                        context_low((tile.n + 2) // 2)
                    if tile.real:
                        v.wait_ge(pr_turned, tile.t * NQ + q + 1)
                        v.tensor_copy(prT[q % 2], acc[0][:, REST:REST + P]).then_inc(pr_taken, 1)
                    of_unit = tile if q < 2 else near
                    if of_unit.real:
                        shift(of_unit, (q + 2) % NQ)
                    if q == 0:
                        if near.real:
                            v.wait_ge(mask_staged[near.odd], near.half * 16 + 16)
                            after(v, energy_done, tile.t * NQ)
                            v.tensor_scalar(mask_add[near.odd], mask_in[near.odd], 0.0, CROSS_MASKED,
                                            ALU.is_equal, ALU.mult).then_inc(mask_ready, 1)
                            v.wait_ge(rstd2_done, near.t + 1)
                            v.tensor_scalar(xn2, xn2, ln2_r, None, ALU.mult).then_inc(xn2_ready, 1)
                        if before.real:
                            v.wait_ge(logits_done, before.t + 1)
                            v.tensor_tensor(logits[:, ds(before.t, 1), :].rearrange("p a d -> p (a d)"),
                                            acc[1][:, 0:NE], rb_b[:], ALU.add).then_inc(logits_taken, 1)
                    if q == 1 and near.real:
                        v.wait_ge(xn2_taken, near.t + 1)
                        for r, rows in enumerate(half_rows):
                            i = v.tensor_tensor(xn2_parts[near.odd][half_rows[1 - r], :, r, :],
                                                tp[1][rows, 0:D].rearrange("p (c t) -> p c t", c=C),
                                                xn2_parts[near.odd][rows, :, r, :].bitcast(F32), ALU.subtract)
                        i.then_inc(xn2_low, 1)
                    if q == 1 and last.real:
                        v.wait_ge(y2_done, last.t + 1)
                        after(v, x3_free, last.t - 1 + FREE)
                        residual(last.t, acc[1][:, 0:D], bout_b[:], y2_taken, xn3[last.odd], ln3_sum, ln3_sq, ln3_var
                                 ).then_inc(var3_done, 1)
                    elif q == 2:
                        if ahead.real:
                            v.wait_ge(first_turned, ahead.t + 1 + FREE_2)
                            v.tensor_copy(oT[:, 0:4, :].rearrange("p a b -> p (a b)"), acc[1][:]).then_inc(first_taken, 1)
                        if last.real:
                            v.wait_ge(rstd3_done, last.t + 1)
                            v.tensor_scalar(xn3[last.odd], xn3[last.odd], ln3_r, None, ALU.mult).then_inc(xn3_ready, 1)
                    elif q == 3:
                        if last.real:
                            v.wait_ge(xn3_taken, last.t + 1)
                            low_part(last.t, tp[1]).then_inc(xn3_low, 1)
                        if ahead.real:
                            v.wait_ge(y_done, ahead.t + 1)
                            after(v, xn2_turned, ahead.t)
                            residual(ahead.t, acc[1][:, 0:D], bo_b[:], y_taken, xn2, ln2_sum, ln2_sq, ln2_var,
                                     between=(lambda: cross_output(tile)) if tile.real else None).then_inc(var2_done, 1)
                        elif tile.real:
                            cross_output(tile)

            @contextmanager
            def counted_tiles(first, end):
                with v.Fori(first, end) as j:
                    step.loop(j, 2 * (1 + NQ + 4 + 4))
                    yield j
                step.end(end - first)
            v.wait_ge(rows_in, 64)
            tiles(cycle, counted_tiles)

            v.wait_ge(logits_taken, NT)

            def over_experts(a):
                return a.unsqueeze(2).to_broadcast([P, NT, NE])

            def top(src, best, at, hot):
                step(v.tensor_reduce(best, src, AX.X, ALU.max))
                step(v.tensor_tensor(eq, src, over_experts(best), ALU.is_equal))
                step(v.tensor_tensor(cand, eq, jm8, ALU.mult))
                step(v.tensor_reduce(at, cand, AX.X, ALU.min))
                step(v.tensor_tensor(hot, jm8, over_experts(at), ALU.is_equal))
            top(logits[:], first_max, first_at, hot1)
            step(v.scalar_tensor_tensor(masked, hot1, -3e38, logits[:], ALU.mult, ALU.add))
            top(masked, second_max, second_at, hot2)
            v.tensor_tensor(both, hot1, hot2, ALU.add).then_inc(both_ready, 1)
            v.tensor_tensor(gap, second_max, first_max, ALU.subtract)
            v.tensor_tensor(shifted, logits[:], over_experts(first_max), ALU.subtract).then_inc(gap_ready, 1)
            def w1_low(idx):
                for q in range(2):
                    v.wait_ge(w1_hi_ready, idx * 2 + q + 1)
                    at = slice(q * F // 2, (q + 1) * F // 2)
                    v.tensor_tensor(w1_lo[:, :, at], w1_raw[:, :, at], w1_hi[:, :, at].bitcast(F32), ALU.subtract
                                    ).then_inc(w1_ready, 1)

            w1_low(0)
            v.wait_ge(counted, 1)
            pad = NT // 2
            step(v.tensor_copy(tile_sums[0][:, pad:, :], acc[1][:, 0:NT * NE].rearrange("p (t e) -> p t e", e=NE)))
            for r in range(4):
                old, new = tile_sums[r % 2], tile_sums[1 - r % 2]
                step(v.tensor_tensor(new[:, pad:, :], old[:, pad:, :], old[:, pad - 2 ** r:pad - 2 ** r + NT, :], ALU.add))
            step(v.tensor_tensor(block_cmp[:], tile_base[:, NT, :].unsqueeze(2).to_broadcast([P, NE, T // BLK]),
                                 block_starts[:], ALU.is_gt))
            step(v.tensor_reduce(n_blocks, block_cmp[:], AX.X, ALU.add))
            pad = NE // 2
            step(v.tensor_copy(block_sums[0][:, pad:], n_blocks))
            for r in range(3):
                old, new = block_sums[r % 2], block_sums[1 - r % 2]
                step(v.tensor_tensor(new[:, pad:], old[:, pad:], old[:, pad - 2 ** r:pad - 2 ** r + NE], ALU.add))
            blocks_incl = block_sums[1][:, pad:]
            step(v.tensor_tensor(block_ge[:], blocks_incl.unsqueeze(1).to_broadcast([P, MAX_BLOCKS, NE]),
                                 block_no[:], ALU.is_le))
            step(v.tensor_reduce(block_f[:], block_ge[:], AX.X, ALU.add))
            v.tensor_scalar(block_expert[:], block_f[:], float(NE - 1), None, ALU.min).then_inc(experts_ready, 1)
            step(v.tensor_tensor(expert_base, blocks_incl, n_blocks, ALU.subtract))
            step(v.tensor_scalar(expert_base, expert_base, float(BLK), None, ALU.mult))
            step(v.tensor_tensor(pos, acc[0][:, 0:NT * NE].rearrange("p (t e) -> p t e", e=NE), tile_base[:, 0:NT, :], ALU.add))
            step(v.tensor_tensor(pos2, pos, expert_base.unsqueeze(1).to_broadcast([P, NT, NE]), ALU.add))
            for k, hot in enumerate((hot1, hot2)):
                step(v.tensor_tensor(picked, hot, pos2, ALU.mult))
                step(v.tensor_reduce(destf, picked, AX.X, ALU.add))
                step(v.tensor_copy(dest[:, k, :], destf))
            v.sem_inc(dest_ready, 2)
            def hidden_parts(m):
                for k in range(FJ // 2):
                    at = slice(2 * k, 2 * k + 2)
                    v.wait_ge(gelu_done, m * (FJ // 2) + k + 1)
                    if k == 0:
                        v.wait_ge(ffn_done, m + FREE)
                    step(v.tensor_copy(h_hi[:, at, :], h_raw[k % 2]))
                    v.tensor_tensor(h_lo[:, at, :], h_raw[k % 2], h_hi[:, at, :].bitcast(F32), ALU.subtract
                                    ).then_inc(h_ready, 1)

            def next_block(n):
                v.wait_ge(xb_hi_ready, n + 1)
                v.tensor_tensor(xb_lo.rearrange("p a b -> p (a b)"), tp[0][:], xb_hi.rearrange("p a b -> p (a b)").bitcast(F32),
                                ALU.subtract).then_inc(xb_ready, 1)
                w1_low(n + 1)

            def shared_block(block, m, besides):
                hidden_parts(m)
                besides()
                v.wait_ge(ffn_done, m + 1 + FREE)
                for tt in range(TT):
                    step(v.tensor_tensor(x_tile(block * TT + tt), acc[tt][:, 0:D], x_tile(block * TT + tt), ALU.add))
                for tt in range(TT):
                    step(v.tensor_tensor(x_tile(block * TT + tt), x_tile(block * TT + tt), sb2_b[:], ALU.add))
                v.sem_inc(ffn_taken, 1)

            def combine(tiles_of):
                for t in tiles_of:
                    v.wait_ge(gathered[t % RING], (t // RING + 1) * 32)
                    step(v.scalar_tensor_tensor(x_sb[:, t, :], y_got[0][:, t % RING, :], weight[:, 0, t:t + 1],
                                                x_sb[:, t, :], ALU.mult, ALU.add))
                    v.scalar_tensor_tensor(x_sb[:, t, :], y_got[1][:, t % RING, :], weight[:, 1, t:t + 1],
                                           x_sb[:, t, :], ALU.mult, ALU.add).then_inc(final_done, 1)

            def expert_block(n, last):
                hidden_parts(n + FIRST)
                if last:
                    w1_low(MAX_BLOCKS + 1)
                else:
                    next_block(n + 1)
                e = v.value_load(block_expert[0:1, ds(n, 1)], min_val=0, max_val=NE - 1)
                v.wait_ge(ffn_done, n + (FIRST + 1 + FREE))
                v.wait_ge(y_stored, n * 16 + 16 * FREE)
                for tt in range(TT):
                    y = v.tensor_tensor(yb[:, tt, :], acc[tt][:, 0:D], b2_all[:, ds(e, 1), :].rearrange("p a d -> p (a d)"),
                                        ALU.add)
                y.then_inc(yb_taken, 1)
                v.sem_inc(ffn_taken, 1)

            v.wait_ge(route_exp_done, 1)
            step(v.tensor_reduce(total, expd, AX.X, ALU.add))
            step(v.reciprocal(inv_total, total))
            step(v.tensor_tensor(gap_exp, gap_exp, inv_total, ALU.mult))
            step(v.tensor_tensor(w_sum, inv_total, gap_exp, ALU.add))
            step(v.tensor_scalar(w_sum, w_sum, 1e-9, None, ALU.add))
            step(v.reciprocal(w_inv, w_sum))
            step(v.tensor_tensor(weight[:, 0, :], inv_total, w_inv, ALU.mult))
            step(v.tensor_tensor(weight[:, 1, :], gap_exp, w_inv, ALU.mult))
            with v.Fori(0, FIRST - 1) as m:
                step.loop(m, FJ // 2 + 2 * TT)
                shared_block(m, m, lambda: None)
            step.end(FIRST - 1)
            shared_block(FIRST - 1, FIRST - 1, lambda: next_block(0))
            v.wait_ge(b2_in, 16)
            with v.Fori(0, MAX_BLOCKS - 1) as n:
                step.loop(n, FJ // 2)
                expert_block(n, False)
            step.end(MAX_BLOCKS - 1)
            expert_block(MAX_BLOCKS - 1, True)
            shares = [range(0), range(0, 3), range(3, 8), range(8, 14)]
            for i, share in enumerate(shares):
                shared_block(FIRST + i, FIRST + MAX_BLOCKS + i, lambda: combine(share))
            combine(range(14, NT))

        @block.scalar
        def _(act):
            act.sem_inc(turned_taken[1], FREE)
            act.wait_ge(prep_turned, 1)
            act.wait_ge(consts_ready, 1)
            act.activation(w_outT[:].rearrange("p c d -> p (c d)"), sc[:, 1024:1536], ACT.Copy)
            for q in range(NQ):
                for rows in half_rows:
                    i = act.activation(ctxT[rows, 0, q, :], sc[half_rows[q % 2], q // 2 * K2:(q // 2 + 1) * K2], ACT.Copy)
            i.then_inc(ctxT_copied, 1)

            def stage1_tile(t):
                act.wait_ge(xn_turned, t + 1)
                act.activation(xT_hi[:, :, t * P:(t + 1) * P], stage1_banks[t % 3][:, 0:D].rearrange("p (c t) -> p c t", c=C),
                               ACT.Copy).then_inc(xT_hi_ready, 1)

            def weights_high(p):
                act.wait_ge(w_pair_in, p * (16 * 3 * C) + 16 * 3 * C)
                act.activation(w_pair_hi, w_pair, ACT.Copy).then_inc(w_hi_ready, 1)

            def take_projection(t, b, slot):
                what, half, k = SLOTS[slot]
                if what == "turn":
                    return
                if k >= 2:
                    act.wait_ge(lo_ready, t * QK + k - 1)
                elif not isinstance(t, int) or t > 0:
                    act.wait_ge(v_turned, t * HALVES + k - 1)
                act.wait_ge(proj_done, t * UNITS + k + 1)
                kind = "qkv".index(what)
                act.activation(fresh[k % 2], acc[1][:], ACT.Identity, bias=bias_now[:, kind:kind + 1],
                               scale=DH ** -0.5 if what == "q" else 1.0).then_inc(fresh_ready, 1)

            def softmax(it, s):
                n = (s // 2 + 1) * P
                act.wait_ge(max_done, it * STEPS + s + 1)
                act.activation(prob[s % 2][:, 0:n], sc[:, (s % 2) * 1024:(s % 2) * 1024 + n], ACT.Exp,
                               bias=neg_max[:, s % 2:s % 2 + 1], accum_out=row_sum[:, s:s + 1]).then_inc(exp_done, 1)

            def turn(p, b, next_turn, next_pair):
                it = p * NB + b
                for s in range(STEPS):
                    for k, t0, m in chunks[s]:
                        if k == 1:
                            act.wait_ge(turned[1], it * FILLS + fills[s][1])
                            act.activation(probT[s % 2][:, t0:t0 + m, :].rearrange("p a b -> p (a b)"),
                                           tp[1][:, 0:m * P], ACT.Copy).then_inc(turned_taken[1], 1)
                    if s + 2 < STEPS:
                        softmax(it, s + 2)
                    elif next_turn:
                        softmax(it + 1, s + 2 - STEPS)
                    if next_turn and s in SLOT_OF:
                        take_projection(it + 1, 1 - b, SLOT_OF[s])
                    if s == SPLIT_AT and next_pair and b == 0:
                        act.wait_ge(proj_done, (it + 2) * UNITS)
                        weights_high(p + 1)

            weights_high(0)
            act.wait_ge(prep_copied, 1)
            prelude(stage1_tile, lambda slot: take_projection(0, 0, slot))
            softmax(0, 0)
            softmax(0, 1)
            attention(turn, act.Fori)
            def cross_exp(tile, q):
                u = q % 2
                if tile.j is None and tile.n == 0 and q == 0:
                    act.wait_ge(zeros_ready, 1)
                act.wait_ge(shifted_done, tile.t * NQ + q + 1)
                act.activation(pm[u], energy[u][:, :, 0:P], ACT.Exp, scale=CD ** -0.5)
                act.activation(pr[u][:, :, 0:KR], energy[u][:, :, P:K2], ACT.Exp, scale=CD ** -0.5).then_inc(cexp_done, 1)

            def context_high(b):
                for h in range(UH):
                    act.activation(ctx_hi[:, b, :, h, :], ctxT[:, b, :, :], ACT.Copy, scale=in_head[:, h:h + 1]
                                   ).then_inc(ctx_hi_ready, 1)

            def cycle(tile, b, b_next):
                last, near, ahead = tile + -1, tile + 1, tile + 2
                rows_turned = tp[1][:, 0:D].rearrange("p (c t) -> p c t", c=C)
                for q in range(NQ):
                    if q == 3 and tile.j is None and tile.n in (-2, 0):
                        context_high((tile.n + 2) // 2)
                    if tile.real:
                        act.wait_ge(pm_turned, tile.t * NQ + q + 1)
                        act.activation(pmT[q % 2].rearrange("p a b -> p (a b)"), tp[0][:], ACT.Copy).then_inc(pm_taken, 1)
                    if q == 0 and last.real:
                        act.wait_ge(o2_turned, last.t + 1)
                        act.activation(o2T, rows_turned, ACT.Copy).then_inc(o2_taken, 1)
                    elif q == 1 and near.real:
                        act.wait_ge(xn2_turned, near.t + 1)
                        for r, rows in enumerate(half_rows):
                            i = act.activation(xn2_parts[near.odd][rows, :, r, :],
                                               tp[1][rows, 0:D].rearrange("p (c t) -> p c t", c=C), ACT.Copy)
                        i.then_inc(xn2_taken, 1)
                    elif q == 2 and ahead.real:
                        act.wait_ge(second_turned, ahead.t + 1)
                        act.activation(oT[:, 4:8, :].rearrange("p a b -> p (a b)"), tp[1][:], ACT.Copy
                                       ).then_inc(second_taken, 1)
                    elif q == 3 and last.real:
                        act.wait_ge(xn3_turned, last.t + 1)
                        act.activation(xn3T, rows_turned, ACT.Copy)
                        act.activation(xT_hi[:, :, ds(last.t * P, P)], rows_turned, ACT.Copy).then_inc(xn3_taken, 1)
                    of_unit = tile if q < 2 else near
                    if of_unit.real:
                        cross_exp(of_unit, (q + 2) % NQ)
            tiles(cycle, act.Fori)
            act.wait_ge(gap_ready, 1)
            act.activation(gap_exp, gap, ACT.Exp)
            act.activation(expd, shifted, ACT.Exp).then_inc(route_exp_done, 1)
            def w1_high(idx):
                act.wait_ge(w1_in, idx * 16 + 16)
                for q in range(2):
                    at = slice(q * F // 2, (q + 1) * F // 2)
                    act.activation(w1_hi[:, :, at], w1_raw[:, :, at], ACT.Copy).then_inc(w1_hi_ready, 1)

            def w2_high(idx, q):
                if q % 2 == 0:
                    act.wait_ge(w2_in[q // 2], idx * 16 + 16)
                at = slice(q * FJ // 4, (q + 1) * FJ // 4)
                act.activation(w2_hi[:, at, :], w2_raw[:, at, :], ACT.Copy).then_inc(w2_hi_ready, 1)

            def hidden(m, first_bias, w2_idx):
                for k in range(FJ // 2):
                    act.wait_ge(h_done, m * (FJ // 2) + k + 1)
                    act.wait_ge(h_ready, m * (FJ // 2) + k + FREE_2 - 1)
                    for i in range(2):
                        y = act.activation(h_raw[k % 2][:, i, :], sc[:, k * 512 + i * BLK:k * 512 + (i + 1) * BLK], ACT.Gelu,
                                           bias=b1T[:, ds(first_bias + 2 * k + i, 1)])
                    y.then_inc(gelu_done, 1)
                    if w2_idx is not None:
                        w2_high(w2_idx, k)

            def next_block(n):
                act.wait_ge(xb_turned, n + 1 + FREE)
                act.activation(xb_hi.rearrange("p a b -> p (a b)"), tp[0][:], ACT.Copy).then_inc(xb_hi_ready, 1)
                w1_high(n + 1)

            def expert_block(n, last):
                e = act.value_load(block_expert[0:1, ds(n, 1)], min_val=0, max_val=NE - 1)
                hidden(n + FIRST, e * FJ, n + 1)
                if last:
                    w1_high(MAX_BLOCKS + 1)
                else:
                    next_block(n + 1)

            w1_high(0)
            for q in range(4):
                w2_high(0, q)
            with act.Fori(0, FIRST - 1) as m:
                hidden(m, NE * FJ, None)
            hidden(FIRST - 1, NE * FJ, None)
            next_block(0)
            act.wait_ge(experts_ready, 1)
            with act.Fori(0, MAX_BLOCKS - 1) as n:
                expert_block(n, False)
            expert_block(MAX_BLOCKS - 1, True)
            for i in range(LAST):
                hidden(FIRST + MAX_BLOCKS + i, NE * FJ, MAX_BLOCKS + 1 if i == 0 else None)

        @block.tensor
        def _(pe):
            for signal in (xb_turned, ffn_done):
                pe.sem_inc(signal, FREE)
            pe.sem_inc(first_turned, FREE_2)
            pe.wait_ge(consts_ready, 1)
            pe.wait_ge(small_in, 16 * (2 * NB + 6))
            for b in range(NB):
                for c in range(C):
                    at = b * 512 + c * K2
                    pe.transpose(sc[:, at:at + P], ctx_in[:, b, 0, c * P:(c + 1) * P], ident[:])
                    pe.transpose(sc[:, at + P:at + K2], ctx_in[0:KR, b, 1, c * P:(c + 1) * P], ident[0:KR, 0:KR])
            for ci in range(C):
                for co in range(C):
                    pe.transpose(sc[:, 1024 + ci * D + co * P:1024 + ci * D + (co + 1) * P],
                                 wout_in[:, co, ci * P:(ci + 1) * P], ident[:])
            pe.transpose(sc[:, 1536:1536 + 3 * NP], bias_in[0:3 * NP, :], ident[0:3 * NP, 0:3 * NP])
            nb1 = (NE + 1) * FJ
            pe.transpose(sc[:, 1536 + P:1536 + P + nb1], b1_in[0:nb1, :], ident[0:nb1, 0:nb1]).then_inc(prep_turned, 1)
            def stage1_tile(t):
                pe.wait_ge(xn_ready, t + 1)
                if t >= 3:
                    pe.wait_ge(xT_ready, t - 2)
                for c in range(C):
                    tr = pe.transpose(stage1_banks[t % 3][:, c * P:(c + 1) * P], xn[t % 2][:, c * P:(c + 1) * P], ident[:])
                tr.then_inc(xn_turned, 1)

            def project(t, b, slot):
                what, half, k = SLOTS[slot]
                if what == "turn":
                    pe.wait_ge(fresh_ready, t * UNITS + 5 + k)
                    for m in range(4):
                        tr = pe.transpose(acc[1][:, m * P:(m + 1) * P], fresh[k][:, m * P:(m + 1) * P], ident[:])
                    tr.then_inc(v_turned, 1)
                    return
                if what == "v" and half == 1:
                    pe.wait_ge(v_taken, t * HALVES + 1)
                elif k > 0:
                    pe.wait_ge(fresh_ready, t * UNITS + k)
                elif not isinstance(t, int) or t > 0:
                    pe.wait_ge(v_taken, t * HALVES)
                kind = "qkv".index(what)
                tokens = slice(b * S + half * HS, b * S + (half + 1) * HS)
                terms = [(w, x, c) for w, x in ((w_pair_hi, xT_hi), (w_pair_lo, xT_hi), (w_pair_hi, xT_lo))
                         for c in range(C)]
                for i, (w, x, c) in enumerate(terms):
                    mm = pe.matmul(acc[1][:], w[:, kind, c, :], x[:, c, tokens],
                                   start=(i == 0), stop=(i == len(terms) - 1))
                mm.then_inc(proj_done, 1)

            def scores(it, b, s):
                i, h = s // 2, s % 2
                n = (i + 1) * P
                at = h * 1024
                if s == 0:
                    pe.wait_ge(lo_ready, it * QK + QK)
                for n0 in range(0, n, 512):
                    w = min(512, n - n0)
                    last = n0 + w == n
                    for r, k in enumerate((k_hi, k_lo)):
                        pe.matmul(sc[:, at + n0:at + n0 + w], q_parts[b][h][:, i * P:(i + 1) * P], k[b][h][:, n0:n0 + w],
                                  start=(r == 0), stop=(r == 1 and not last))
                pe.matmul(sc[:, at + n - P:at + n], identb[:], causal[:], start=False, stop=True
                          ).then_inc(scores_done, 1)

            def turn(p, b, next_turn, next_pair):
                it = p * NB + b
                for s in range(STEPS):
                    i, h = s // 2, s % 2
                    pe.wait_ge(exp_done, it * STEPS + s + 1)
                    for k, t0, m in chunks[s]:
                        pe.wait_ge(turned_taken[k], it * FILLS + fills[s][k] - 1 + FREE)
                        for r in range(m):
                            tr = pe.transpose(tp[k][:, r * P:(r + 1) * P], prob[h][:, (t0 + r) * P:(t0 + r + 1) * P],
                                              ident[:])
                        tr.then_inc(turned[k], 1)
                    if s + 2 < STEPS:
                        scores(it, b, s + 2)
                    elif next_turn:
                        scores(it + 1, 1 - b, s + 2 - STEPS)
                    if next_turn and s in SLOT_OF:
                        if SLOT_OF[s] == 0:
                            pe.wait_ge(w_lo_ready, p + b + 1)
                        project(it + 1, 1 - b, SLOT_OF[s])
                    if s == 0:
                        pe.wait_ge(v_taken, it * HALVES + HALVES)
                    pe.wait_ge(o_taken, it * STEPS + s + FREE)
                    for k, t0, m in chunks[s]:
                        pe.wait_ge(turned_taken[k], it * FILLS + fills[s][k] + FREE)
                        for r in range(t0, t0 + m):
                            mm = pe.matmul(acc[0][:, 0:DH], probT[h][:, r, :], v_pair[b][:, r, h * DH:(h + 1) * DH],
                                           start=(r == 0), stop=(r == i))
                    mm.then_inc(pv_done, 1)

            def first_projection(slot):
                if slot == 0:
                    pe.wait_ge(w_lo_ready, 1)
                    pe.wait_ge(xT_ready, TB)
                project(0, 0, slot)
            prelude(stage1_tile, first_projection)
            pe.wait_ge(xT_ready, NT)
            pe.wait_ge(ctxT_copied, 2)
            scores(0, 0, 0)
            scores(0, 0, 1)
            attention(turn, pe.Fori)
            pe.wait_ge(o_taken, TURNS * STEPS + FREE)
            pe.wait_ge(ctxT_copied, 3)
            pe.wait_ge(w_in, 32)
            pe.wait_ge(rest_in, 16 * UH * NB)
            def energies(tile, b, q):
                u = q % 2
                if q == 0:
                    pe.wait_ge(xn2_low, tile.t + 1)
                    pe.wait_ge(mask_ready, tile.t + 1 + FREE_2)
                    if tile.j is None and tile.n % TB == 0:
                        pe.wait_ge(ctx_ready, (b + 1) * UH)
                for a in range(2):
                    bank = sc[:, u * 1024 + a * 512:u * 1024 + a * 512 + 2 * K2]
                    for part, keys in enumerate((ctx_hi, ctx_lo)):
                        pe.matmul(bank, xn2_parts[tile.odd][:, q // 2, q % 2, :],
                                  keys[:, b, q, 2 * a:2 * a + 2, :].rearrange("p h k -> p (h k)"),
                                  start=(part == 0), stop=False)
                    mm = pe.matmul(bank.rearrange("p (h k) -> p h k", h=2), identb[:],
                                   mask_add[tile.odd].unsqueeze(1).to_broadcast([P, 2, K2]), start=False, stop=True)
                mm.then_inc(energy_done, 1)

            def turn_rows(rows):
                for c in range(C):
                    tr = pe.transpose(tp[1][:, c * P:(c + 1) * P], rows[:, c * P:(c + 1) * P], ident[:])
                return tr

            def besides(tile, q):
                before, last, near, ahead = tile + -2, tile + -1, tile + 1, tile + 2
                if q == 0:
                    if last.real:
                        pe.wait_ge(o2_ready, last.t + 1)
                        after(pe, xn3_low, last.t)
                        turn_rows(o2).then_inc(o2_turned, 1)
                    if before.real:
                        pe.wait_ge(xn3_taken, before.t + 1)
                        if near.real:
                            pe.wait_ge(y_taken, near.t + 1)
                        for c in range(C):
                            mm = pe.matmul(acc[1][:, 0:NE], xn3T[:, c, :], rw_sb[:, c, :], start=(c == 0), stop=(c == C - 1))
                        mm.then_inc(logits_done, 1)
                elif q == 1:
                    if last.real:
                        pe.wait_ge(o2_taken, last.t + 1)
                    if near.real:
                        pe.wait_ge(xn2_ready, near.t + 1)
                        turn_rows(xn2).then_inc(xn2_turned, 1)
                    if last.real:
                        if before.real:
                            pe.wait_ge(logits_taken, before.t + 1)
                        elif near.real:
                            pe.wait_ge(y_taken, near.t + 1)
                        for c in range(C):
                            mm = pe.matmul(acc[1][:, 0:D], o2T[:, c, :], w_outT[:, c, :], start=(c == 0), stop=(c == C - 1))
                        mm.then_inc(y2_done, 1)
                elif q == 2 and ahead.real:
                    pe.wait_ge(o_staged[ahead.odd], ahead.half * 16 + 16)
                    if near.real:
                        pe.wait_ge(xn2_low, near.t + 1)
                    for r in range(4, 8):
                        tr = pe.transpose(tp[1][:, (r - 4) * P:(r - 3) * P], o_tile[ahead.odd][:, r * P:(r + 1) * P], ident[:])
                    tr.then_inc(second_turned, 1)
                    if last.real:
                        pe.wait_ge(y2_taken, last.t + 1)
                    elif near.real:
                        pe.wait_ge(y_taken, near.t + 1)
                    for r in range(4):
                        tr = pe.transpose(acc[1][:, r * P:(r + 1) * P], o_tile[ahead.odd][:, r * P:(r + 1) * P], ident[:])
                    tr.then_inc(first_turned, 1)
                elif q == 3:
                    if ahead.real:
                        pe.wait_ge(second_taken, ahead.t + 1)
                    if last.real:
                        pe.wait_ge(xn3_ready, last.t + 1)
                        turn_rows(xn3[last.odd]).then_inc(xn3_turned, 1)
                    if ahead.real:
                        pe.wait_ge(first_taken, ahead.t + 1)
                        for r in range(J):
                            mm = pe.matmul(acc[1][:, 0:D], oT[:, r, :], wo_sb[:, r, :], start=(r == 0), stop=(r == J - 1))
                        mm.then_inc(y_done, 1)

            def cycle(tile, b, b_next):
                last, near = tile + -1, tile + 1
                for q in range(NQ):
                    if tile.real:
                        pe.wait_ge(cexp_done, tile.t * NQ + q + 1)
                        for r in range(UH):
                            tr = pe.transpose(tp[0][:, r * P:(r + 1) * P], pm[q % 2][:, r, :], ident[:])
                        tr.then_inc(pm_turned, 1)
                    if q < 2 and tile.real:
                        energies(tile, b, q + 2)
                    if q >= 2 and near.real:
                        energies(near, b_next, q - 2)
                    if tile.real:
                        if q == 0 and last.real:
                            pe.wait_ge(o2_ready, last.t + 1)
                        pe.transpose(acc[0][:, REST:REST + P], pr[q % 2].rearrange("p h k -> p (h k)"), ident[:]
                                     ).then_inc(pr_turned, 1)
                    besides(tile, q)
                    if tile.real:
                        pe.wait_ge(pr_taken, tile.t * NQ + q + 1)
                        pe.wait_ge(pm_taken, tile.t * NQ + q + 1)
                        at = q * UH * V1
                        pe.matmul(acc[0][:, at:at + UH * V1], prT[q % 2],
                                  v_rest[:, b, q * UH:(q + 1) * UH, :].rearrange("p h k -> p (h k)"),
                                  start=True, stop=False)
                        for r in range(UH):
                            mm = pe.matmul(acc[0][:, at + r * V1:at + (r + 1) * V1], pmT[q % 2][:, r, :],
                                           v_main[:, b, q * UH + r, :], start=False, stop=(r == UH - 1))
                        mm.then_inc(cpv_done, 1)
            tiles(cycle, pe.Fori)
            pe.wait_ge(both_ready, 1)
            bf = both.rearrange("p t e -> p (t e)")
            pe.matmul(acc[0][:, 0:NT * NE], lower[:], bf, start=True, stop=True)
            pe.matmul(acc[1][:, 0:NT * NE], ones[:], bf, start=True, stop=True).then_inc(counted, 1)

            def ffn_in(idx, x_hi, x_lo):
                for k in range(FJ):
                    if k % 4 == 0:
                        pe.wait_ge(w1_ready, idx * 2 + k // 4 + 1)
                    at = slice(k * P, (k + 1) * P)
                    terms = [(w, x, c) for w, x in ((w1_hi, x_hi), (w1_lo, x_hi), (w1_hi, x_lo)) for c in range(C)]
                    for i, (w, x, c) in enumerate(terms):
                        mm = pe.matmul(sc[:, k * BLK:(k + 1) * BLK], w[:, c, at], x(c),
                                       start=(i == 0), stop=(i == len(terms) - 1))
                    if k % 2:
                        mm.then_inc(h_done, 1)

            def ffn_out(m, idx):
                pe.wait_ge(ffn_taken, m + FREE)
                for k in range(FJ):
                    if k % 2 == 0:
                        pe.wait_ge(h_ready, m * (FJ // 2) + k // 2 + 1 + FREE_2)
                        pe.wait_ge(w2_ready, idx * 4 + k // 2 + 1)
                    for tt in range(TT):
                        rows = slice(tt * P, (tt + 1) * P)
                        for i, (h, w) in enumerate(((h_hi, w2_hi), (h_hi, w2_lo), (h_lo, w2_hi))):
                            mm = pe.matmul(acc[tt][:, 0:D], h[:, k, rows], w[:, k, :],
                                           start=(k == 0 and i == 0), stop=(k == FJ - 1 and i == 2))
                mm.then_inc(ffn_done, 1)

            def turn_block(n):
                pe.wait_ge(xb_in, n * 16 + 16)
                for c in range(C):
                    for tt in range(TT):
                        tr = pe.transpose(tp[0][:, c * BLK + tt * P:c * BLK + (tt + 1) * P],
                                          xb[:, tt, c * P:(c + 1) * P], ident[:])
                tr.then_inc(xb_turned, 1)

            def shared_in(block, idx):
                ffn_in(idx, lambda c: xT_hi[:, c, ds(block * BLK, BLK)], lambda c: xT_lo[:, c, ds(block * BLK, BLK)])

            def expert_in(n):
                pe.wait_ge(xb_ready, n + 1)
                ffn_in(n + 1, lambda c: xb_hi[:, c, :], lambda c: xb_lo[:, c, :])

            shared_in(0, 0)
            pe.wait_ge(dest_ready, 2)
            ffn_out(0, 0)
            with pe.Fori(0, FIRST - 2) as j:
                shared_in(j + 1, 0)
                ffn_out(j + 1, 0)
            shared_in(FIRST - 1, 0)
            turn_block(0)
            ffn_out(FIRST - 1, 0)
            with pe.Fori(0, MAX_BLOCKS - 1) as n:
                expert_in(n)
                turn_block(n + 1)
                ffn_out(n + FIRST, n + 1)
            expert_in(MAX_BLOCKS - 1)
            ffn_out(MAX_BLOCKS - 1 + FIRST, MAX_BLOCKS)
            for i in range(LAST):
                shared_in(FIRST + i, MAX_BLOCKS + 1)
                ffn_out(FIRST + MAX_BLOCKS + i, MAX_BLOCKS + 1)


_INS = ['x', 'ctx_1024', 'mask_Bx1xSxS2_ik1', 'L0_attn_Wq', 'L0_attn_Wk', 'L0_attn_Wv', 'L0_attn_bq', 'L0_attn_bk',
        'L0_attn_bv', 'L0_attn_Wo', 'L0_attn_bo', 'L0_xattn_W_out', 'L0_xattn_b_out', 'L0_ffn_shared_w1',
        'L0_ffn_shared_b1', 'L0_ffn_shared_w2', 'L0_ffn_shared_b2', 'L0_ffn_router_w', 'L0_ffn_router_b',
        'L0_ffn_exp_w1', 'L0_ffn_exp_b1', 'L0_ffn_exp_w2', 'L0_ffn_exp_b2']


def kernel(**inputs):
    import numpy as _np
    import concourse.bacc as _bacc
    from concourse import mybir as _mybir
    from concourse.bass_utils import run_bass_kernel_spmd as _run

    nc = _bacc.Bacc("TRN2", target_bir_lowering=False, num_devices=1)
    arrays, args = {}, []
    for name in _INS:
        a = _np.ascontiguousarray(inputs[name])
        arrays[f"in_{name}_dram"] = a
        args.append(nc.dram_tensor(f"in_{name}_dram", a.shape, _mybir.dt.from_np(a.dtype), kind="ExternalInput").ap())
    shape = inputs['x'].shape
    args.append(nc.dram_tensor("out_dram", shape, _mybir.dt.from_np(_np.dtype('float32')), kind="ExternalOutput").ap())
    decoder_layer(nc, *args)
    r = _run(nc, [arrays], core_ids=[0])
    return r.results[0]["out_dram"]
```
